# Optimizing a Trainium2 kernel written in Bass

```python
import numpy as np
import jax
import jax.numpy as jnp

def _softmax(x, axis=-1):
    return jax.nn.softmax(x, axis=axis)

def _gelu(x):
    return jax.nn.gelu(x, approximate=True)

def _silu(x):
    return jax.nn.silu(x)

def _sigmoid(x):
    return jax.nn.sigmoid(x)

def _layernorm(x, axis=-1, eps=1e-05):
    m = jnp.mean(x, axis=axis, keepdims=True)
    v = jnp.var(x, axis=axis, keepdims=True)
    return (x - m) / jnp.sqrt(v + eps)

def _scatter_add(tgt, idx, src, axis=0):
    return tgt.at[idx].add(src)

def _segment_sum(src, seg, n):
    return jax.ops.segment_sum(src, seg, n)
kernel_name = 'mk_flamingo_gated_d1_seqx_r8_ee8fb1'

def setup_inputs(seed: int=0):
    np.random.seed(seed)
    _w = jnp.asarray

    def _rec_inputs():
        import jax
        import jax.numpy as jnp
        _rk = jax.random.key(seed)
        x = 7.22e-05 + 1 * jax.random.normal(jax.random.fold_in(_rk, 1), (16, 128, 256), jnp.float32)
        _lenS = 128 - jax.random.randint(jax.random.fold_in(_rk, 7), (16,), 0, max(1, 128 // 4) + 1, jnp.int32)
        _lenS2 = 128 - jax.random.randint(jax.random.fold_in(_rk, 8), (16,), 0, max(1, 128 // 4) + 1, jnp.int32)
        _ctx_1024P = jax.random.normal(jax.random.fold_in(_rk, 11), (16, 16, 128), jnp.float32)
        _ctx_1024c = jax.random.dirichlet(jax.random.fold_in(_rk, 511), 0.3 * jnp.ones((16,), jnp.float32), (16, 128))
        _ctx_1024t = jnp.einsum('bsk,bkd->bsd', _ctx_1024c, _ctx_1024P)
        _ctx_1024t = _ctx_1024t * jax.lax.rsqrt(jnp.mean(jnp.square(_ctx_1024t)) + 1e-12) * 0.953939
        ctx_1024 = -0.000673644 + 1.00013 * (_ctx_1024t + 0.3 * jax.random.normal(jax.random.fold_in(_rk, 611), (16, 128, 128), jnp.float32))
        _g = jax.random.normal(jax.random.fold_in(_rk, 9001), (2, 1), jnp.float32)
        _g = jnp.sign(_g) * jnp.maximum(jnp.abs(_g), 1.0) + (_g == 0) * 1.0
        g_xattn = _g[0]
        g_ffn = _g[1]
        return (x, ctx_1024, g_xattn, g_ffn)
    x, ctx_1024, g_xattn, g_ffn = _rec_inputs()

    def _L0_xattn_setup():
        import jax, jax.numpy as jnp
        import numpy as np
        B, S1, S2, DCA = (2, 256, 128, 16)
        QDIM, KDIM, H = (256, 128, 16)
        HD = QDIM // H
        SCALE = HD ** (-0.5)
        EPS = 1e-06
        DCA_WEIGHT = 1.0

        def _ln(t, w, b):
            m = jnp.mean(t, axis=-1, keepdims=True)
            v = jnp.var(t, axis=-1, keepdims=True)
            return (t - m) * jax.lax.rsqrt(v + EPS) * w + b

        def _attn(q, k, v):
            s = jnp.einsum('bhqd,bhkd->bhqk', q, k) * SCALE
            p = jax.nn.softmax(s, axis=-1)
            return jnp.einsum('bhqk,bhkd->bhqd', p, v)
        key = jax.random.key(seed)
        ks = jax.random.split(key, 8)
        w = lambda k, shape: jax.random.normal(k, shape, jnp.float32) * 0.02
        return {'x': jax.random.normal(ks[0], (B, S1, QDIM), jnp.float32), 'y': jax.random.normal(ks[1], (B, S2 + DCA, KDIM), jnp.float32), 'Wq': w(ks[2], (QDIM, QDIM)), 'bq': jnp.zeros((QDIM,), jnp.float32), 'Wk': w(ks[3], (KDIM, QDIM)), 'bk': jnp.zeros((QDIM,), jnp.float32), 'Wv': w(ks[4], (KDIM, QDIM)), 'bv': jnp.zeros((QDIM,), jnp.float32), 'Wkv_dca': w(ks[5], (KDIM, 2 * QDIM)), 'bkv_dca': jnp.zeros((2 * QDIM,), jnp.float32), 'qn_w': jnp.ones((HD,), jnp.float32), 'qn_b': jnp.zeros((HD,), jnp.float32), 'kn_w': jnp.ones((HD,), jnp.float32), 'kn_b': jnp.zeros((HD,), jnp.float32), 'kn_dca_w': jnp.ones((HD,), jnp.float32), 'kn_dca_b': jnp.zeros((HD,), jnp.float32), 'Wo': w(ks[6], (QDIM, QDIM)), 'bo': jnp.zeros((QDIM,), jnp.float32)}
    _L0_xattn_all = _L0_xattn_setup()
    _L0_xattn_in = {k: v for k, v in _L0_xattn_all.items() if k in ('Wq', 'bq', 'Wk', 'bk', 'Wv', 'bv', 'Wkv_dca', 'bkv_dca', 'qn_w', 'qn_b', 'kn_w', 'kn_b', 'kn_dca_w', 'kn_dca_b', 'Wo', 'bo')}
    del _L0_xattn_all

    def _L0_ffn_setup():
        import jax, jax.numpy as jnp
        import numpy as np
        H = 256
        NH = 16
        NOPE = 128
        ROPE = 64
        VD = 128
        QHD = NOPE + ROPE
        E = 16
        I = 176
        TOPK = 4
        NSH = 2
        SHI = I * NSH
        EPS = 1e-06
        B, S = (2, 128)

        def rmsnorm(x, w):
            return x * jax.lax.rsqrt(jnp.mean(x * x, axis=-1, keepdims=True) + EPS) * w
        key = jax.random.key(seed)
        ks = jax.random.split(key, 12)
        sd = lambda fan_in: 1.0 / np.sqrt(fan_in)
        return {'hidden_states': jax.random.normal(ks[0], (B, S, H), jnp.float32), 'positions': jnp.broadcast_to(jnp.arange(S, dtype=jnp.int32), (B, S)), 'ln1_w': jnp.ones((H,), jnp.float32), 'ln2_w': jnp.ones((H,), jnp.float32), 'q_w': jax.random.normal(ks[1], (NH * QHD, H), jnp.float32) * sd(H), 'kv_w': jax.random.normal(ks[2], (NH * (NOPE + VD) + ROPE, H), jnp.float32) * sd(H), 'o_w': jax.random.normal(ks[3], (H, NH * VD), jnp.float32) * sd(NH * VD), 'gate_w': jax.random.normal(ks[4], (E, H), jnp.float32) * sd(H), 'w1': jax.random.normal(ks[5], (E, 2 * I, H), jnp.float32) * sd(H), 'w2': jax.random.normal(ks[6], (E, H, I), jnp.float32) * sd(I), 'sh_gu_w': jax.random.normal(ks[7], (2 * SHI, H), jnp.float32) * sd(H), 'sh_down_w': jax.random.normal(ks[8], (H, SHI), jnp.float32) * sd(SHI)}
    _L0_ffn_all = _L0_ffn_setup()
    _L0_ffn_in = {k: v for k, v in _L0_ffn_all.items() if k in ('positions', 'ln1_w', 'ln2_w', 'q_w', 'kv_w', 'o_w', 'gate_w', 'w1', 'w2', 'sh_gu_w', 'sh_down_w')}
    del _L0_ffn_all
    return {'x': x, 'ctx_1024': ctx_1024, 'g_xattn': g_xattn, 'g_ffn': g_ffn, 'L0_xattn_Wq': _L0_xattn_in['Wq'], 'L0_xattn_bq': _L0_xattn_in['bq'], 'L0_xattn_Wk': _L0_xattn_in['Wk'], 'L0_xattn_bk': _L0_xattn_in['bk'], 'L0_xattn_Wv': _L0_xattn_in['Wv'], 'L0_xattn_bv': _L0_xattn_in['bv'], 'L0_xattn_Wkv_dca': _L0_xattn_in['Wkv_dca'], 'L0_xattn_bkv_dca': _L0_xattn_in['bkv_dca'], 'L0_xattn_qn_w': _L0_xattn_in['qn_w'], 'L0_xattn_qn_b': _L0_xattn_in['qn_b'], 'L0_xattn_kn_w': _L0_xattn_in['kn_w'], 'L0_xattn_kn_b': _L0_xattn_in['kn_b'], 'L0_xattn_kn_dca_w': _L0_xattn_in['kn_dca_w'], 'L0_xattn_kn_dca_b': _L0_xattn_in['kn_dca_b'], 'L0_xattn_Wo': _L0_xattn_in['Wo'], 'L0_xattn_bo': _L0_xattn_in['bo'], 'L0_ffn_positions': _L0_ffn_in['positions'], 'L0_ffn_ln1_w': _L0_ffn_in['ln1_w'], 'L0_ffn_ln2_w': _L0_ffn_in['ln2_w'], 'L0_ffn_q_w': _L0_ffn_in['q_w'], 'L0_ffn_kv_w': _L0_ffn_in['kv_w'], 'L0_ffn_o_w': _L0_ffn_in['o_w'], 'L0_ffn_gate_w': _L0_ffn_in['gate_w'], 'L0_ffn_w1': _L0_ffn_in['w1'], 'L0_ffn_w2': _L0_ffn_in['w2'], 'L0_ffn_sh_gu_w': _L0_ffn_in['sh_gu_w'], 'L0_ffn_sh_down_w': _L0_ffn_in['sh_down_w']}

def reference(x, ctx_1024, g_xattn, g_ffn, L0_xattn_Wq, L0_xattn_bq, L0_xattn_Wk, L0_xattn_bk, L0_xattn_Wv, L0_xattn_bv, L0_xattn_Wkv_dca, L0_xattn_bkv_dca, L0_xattn_qn_w, L0_xattn_qn_b, L0_xattn_kn_w, L0_xattn_kn_b, L0_xattn_kn_dca_w, L0_xattn_kn_dca_b, L0_xattn_Wo, L0_xattn_bo, L0_ffn_positions, L0_ffn_ln1_w, L0_ffn_ln2_w, L0_ffn_q_w, L0_ffn_kv_w, L0_ffn_o_w, L0_ffn_gate_w, L0_ffn_w1, L0_ffn_w2, L0_ffn_sh_gu_w, L0_ffn_sh_down_w):
    import jax
    import jax.numpy as jnp

    def _L0_xattn_ref(x, y, Wq, bq, Wk, bk, Wv, bv, Wkv_dca, bkv_dca, qn_w, qn_b, kn_w, kn_b, kn_dca_w, kn_dca_b, Wo, bo):
        import jax, jax.numpy as jnp
        import numpy as np
        B, S1, S2, DCA = (2, 256, 128, 16)
        QDIM, KDIM, H = (256, 128, 16)
        HD = QDIM // H
        SCALE = HD ** (-0.5)
        EPS = 1e-06
        DCA_WEIGHT = 1.0

        def _ln(t, w, b):
            m = jnp.mean(t, axis=-1, keepdims=True)
            v = jnp.var(t, axis=-1, keepdims=True)
            return (t - m) * jax.lax.rsqrt(v + EPS) * w + b

        def _attn(q, k, v):
            s = jnp.einsum('bhqd,bhkd->bhqk', q, k) * SCALE
            p = jax.nn.softmax(s, axis=-1)
            return jnp.einsum('bhqk,bhkd->bhqd', p, v)
        b, s1, _ = x.shape
        y_dca = y[:, -DCA:, :]
        y_main = y[:, :-DCA, :]
        kv_dca = (y_dca @ Wkv_dca + bkv_dca).reshape(b, DCA, 2, H, HD)
        k_dca = _ln(kv_dca[:, :, 0], kn_dca_w, kn_dca_b)
        v_dca = kv_dca[:, :, 1]
        s2 = y_main.shape[1]
        q = _ln((x @ Wq + bq).reshape(b, s1, H, HD), qn_w, qn_b)
        kv = jnp.concatenate([y_main @ Wk + bk, y_main @ Wv + bv], axis=-1)
        kv = kv.reshape(b, s2, H, 2 * HD)
        k = _ln(kv[..., :HD], kn_w, kn_b)
        v = kv[..., HD:]
        qT = q.transpose(0, 2, 1, 3)
        ctx = _attn(qT, k.transpose(0, 2, 1, 3), v.transpose(0, 2, 1, 3))
        ctx = ctx.transpose(0, 2, 1, 3).reshape(b, s1, QDIM)
        ctx_dca = _attn(qT, k_dca.transpose(0, 2, 1, 3), v_dca.transpose(0, 2, 1, 3))
        ctx_dca = ctx_dca.transpose(0, 2, 1, 3).reshape(b, s1, QDIM)
        ctx = ctx + DCA_WEIGHT * ctx_dca
        return ctx @ Wo + bo

    def _L0_ffn_ref(hidden_states, positions, ln1_w, ln2_w, q_w, kv_w, o_w, gate_w, w1, w2, sh_gu_w, sh_down_w):
        import jax, jax.numpy as jnp
        import numpy as np
        H = 256
        NH = 16
        NOPE = 128
        ROPE = 64
        VD = 128
        QHD = NOPE + ROPE
        E = 16
        I = 176
        TOPK = 4
        NSH = 2
        SHI = I * NSH
        EPS = 1e-06
        B, S = (2, 128)

        def rmsnorm(x, w):
            return x * jax.lax.rsqrt(jnp.mean(x * x, axis=-1, keepdims=True) + EPS) * w
        b, s, h = hidden_states.shape
        x = rmsnorm(hidden_states, ln1_w)
        q = jnp.einsum('bsh,dh->bsd', x, q_w).reshape(b, s, NH, QHD)[..., :NOPE]
        kv = jnp.einsum('bsh,dh->bsd', x, kv_w)
        k = kv[..., :NH * NOPE].reshape(b, s, NH, NOPE)
        v = kv[..., NH * NOPE:NH * (NOPE + VD)].reshape(b, s, NH, VD)
        scale = QHD ** (-0.5)
        scores = jnp.einsum('bqnd,bknd->bnqk', q, k) * scale
        causal = jnp.tril(jnp.ones((s, s), bool))
        scores = jnp.where(causal, scores, -1000000000.0)
        p = jax.nn.softmax(scores, axis=-1)
        attn = jnp.einsum('bnqk,bknd->bqnd', p, v).reshape(b, s, NH * VD)
        attn_out = jnp.einsum('bsd,hd->bsh', attn, o_w)
        hid = hidden_states + attn_out
        x2 = rmsnorm(hid, ln2_w).reshape(-1, h)
        logits = x2 @ gate_w.T
        probs = jax.nn.softmax(logits, axis=-1)
        top_w, top_i = jax.lax.top_k(probs, TOPK)
        top_w = top_w / jnp.sum(top_w, axis=-1, keepdims=True)
        wfull = jnp.sum(jax.nn.one_hot(top_i, E, dtype=x2.dtype) * top_w[..., None], axis=1)
        gu = jnp.einsum('th,eih->tei', x2, w1)
        g, u = (gu[..., :I], gu[..., I:])
        act = jax.nn.silu(g) * u
        down = jnp.einsum('tei,ehi->teh', act, w2)
        routed = jnp.einsum('te,teh->th', wfull, down)
        sgu = x2 @ sh_gu_w.T
        sg, su = (sgu[..., :SHI], sgu[..., SHI:])
        shared = jax.nn.silu(sg) * su @ sh_down_w.T
        return hid + (routed + shared).reshape(b, s, h)
    x = x + jnp.tanh(g_xattn[0]) * _L0_xattn_ref(_layernorm(x, axis=-1), ctx_1024, L0_xattn_Wq, L0_xattn_bq, L0_xattn_Wk, L0_xattn_bk, L0_xattn_Wv, L0_xattn_bv, L0_xattn_Wkv_dca, L0_xattn_bkv_dca, L0_xattn_qn_w, L0_xattn_qn_b, L0_xattn_kn_w, L0_xattn_kn_b, L0_xattn_kn_dca_w, L0_xattn_kn_dca_b, L0_xattn_Wo, L0_xattn_bo)
    x = x + jnp.tanh(g_ffn[0]) * _L0_ffn_ref(_layernorm(x, axis=-1), L0_ffn_positions, L0_ffn_ln1_w, L0_ffn_ln2_w, L0_ffn_q_w, L0_ffn_kv_w, L0_ffn_o_w, L0_ffn_gate_w, L0_ffn_w1, L0_ffn_w2, L0_ffn_sh_gu_w, L0_ffn_sh_down_w)
    return x

_drawn_inputs = setup_inputs


def setup_inputs(seed=0):
    import zlib

    import numpy as np

    out = dict(_drawn_inputs(seed))
    spreads = {'L0_xattn_bq': (0.0, 0.1),
     'L0_xattn_bk': (0.0, 0.1),
     'L0_xattn_bv': (0.0, 0.1),
     'L0_xattn_bkv_dca': (0.0, 0.1),
     'L0_xattn_qn_w': (1.0, 0.6),
     'L0_xattn_qn_b': (0.0, 0.535),
     'L0_xattn_kn_w': (1.0, 0.6),
     'L0_xattn_kn_b': (0.0, 0.8),
     'L0_xattn_kn_dca_w': (1.0, 0.6),
     'L0_xattn_kn_dca_b': (0.0, 0.8),
     'L0_xattn_bo': (0.0, 0.1),
     'L0_ffn_ln1_w': (1.0, 0.2),
     'L0_ffn_ln2_w': (1.0, 0.2)}
    factors = {}
    for name, (base, spread) in spreads.items():
        noise = np.random.default_rng([zlib.crc32(name.encode()), seed]).standard_normal(out[name].shape)
        drawn = base * np.exp(spread * noise) if base else spread * noise
        out[name] = jnp.asarray(drawn.astype(out[name].dtype))
    for name, factor in factors.items():
        out[name] = (out[name] * factor).astype(out[name].dtype)
    return out
```

```python
from contextlib import ExitStack

import numpy as np
import concourse.bass as bass
from concourse import mybir
from concourse.alu_op_type import AluOpType as ALU

ACT = mybir.ActivationFunctionType
AX = mybir.AxisListType
F32, F16, BF16, U32 = mybir.dt.float32, mybir.dt.float16, mybir.dt.bfloat16, mybir.dt.uint32

P = 128
NB, S, D = 16, 128, 256
KC = D // P
GB = 4
NG = NB // GB
T = GB * S
XH, XD = 16, 16
DCA = 16
MAIN = S - DCA
NH, QHD, HD = 16, 192, 128
NE, EI, TOPK = 16, 176, 4
SHI = 352
NC = -(-(NE * EI + SHI) // P)
HW = 3 * D + D
CW = 3 * D
WALL = NH * HW + NC * CW
UNITS = 16
UW = WALL // UNITS
WS = 64.0
PS = 256.0
WA = 2048
C_BIAS, C_LNW, C_LNB, C_BO, C_LN1, C_LN2, C_GATE, C_RT, C_IOTA, CWID = (
    0, 768, 1280, 1792, 2048, 2304, 2560, 2562, 2594, 2612)
PRIMED = 1
MASKED = -1.0e12


def build(nc, x, yT, wa, wall, cst, ident, identb, maskb, sel, out):
    assert WALL % UNITS == 0
    with ExitStack() as ctx:
        def sb(name, shape, dt):
            return ctx.enter_context(nc.sbuf_tensor(name, shape, dt))

        sems = {}

        def sem(name):
            if name not in sems:
                sems[name] = ctx.enter_context(nc.semaphore(name))
            return sems[name]

        primed = {"xa_x1": "dve", "p_exp": "act", "pT_sb": "dve", "o_lo": "dve", "me_a": "dve",
                  "me_b": "dve", "me_v": "dve", "p_lo": "pool", "pT_ps": "pe", "op_ps": "pe",
                  "me_lo": "pool", "o_ps": "pe", "xa_pv": "pe", "out_done": "sp", "d_ps": "pe"}

        def apart(eng):
            eng.sem_inc(sem("apart"), 1)

        def prime(eng, name):
            for s, by in primed.items():
                if by == name:
                    eng.sem_inc(sem(s), PRIMED)

        whi = sb("whi", [P, WALL], F16)
        wlo = sb("wlo", [P, WALL], F16)
        wahi = sb("wahi", [P, WA], F16)
        walo = sb("walo", [P, WA], F16)
        cs = sb("cs", [P, CWID], F32)
        idn = sb("idn", [P, P], F16)
        idb = sb("idb", [P, P], BF16)
        msk = sb("msk", [P, GB * S], BF16)
        sl = sb("sl", [P, NC * P], F16)
        x_t = sb("x_t", [P, D], F32)
        y_t = sb("y_t", [P, S], F32)
        x1 = sb("x1", [P, GB, D], F32)
        ysp = sb("ysp", [P, 4, S], F16)
        wcat = sb("wcat", [P, GB, P], F16)
        wT = sb("wT", [P, T], F16)
        sm = sb("sm", [P, 512], F32)
        gt = sb("gt", [P, 2], F32)
        mhalf = sb("mhalf", [P, 32], F32)
        grw = sb("grw", [P, 2, KC, NE], F16)
        ar = sb("ar", [P, 7168], F32)
        ps = ctx.enter_context(nc.psum_tensor("ps", [P, 8, 512], F32))

        def words(a, n):
            return ar[:, a:a + n]

        def halves(a, n):
            return ar[:, a:a + n].bitcast(F16)

        def bank16(b, n=1):
            return ps[:, b:b + n, :].rearrange("p b w -> p (b w)").bitcast(F16)

        def bank(b, n=1):
            return ps[:, b:b + n, :].rearrange("p b w -> p (b w)")

        stage = [words(0, UW), words(UW, UW)]
        xT = halves(0, 1024).rearrange("p (l k t) -> p l k t", l=2, k=KC)
        hid = words(1024, 1024).rearrange("p (j d) -> p j d", j=GB)
        qkT = halves(2048, 1024).rearrange("p (w l t) -> p w l t", w=2, l=2)
        vv = halves(3072, 2048).rearrange("p (r l j c) -> p r l j c", r=2, l=2, j=GB)
        pr = words(5120, 512).rearrange("p (j k) -> p j k", j=GB)
        phl = halves(5632, 512).rearrange("p (l j k) -> p l j k", l=2, j=GB)
        pT = halves(6144, 512).rearrange("p (l j k) -> p l j k", l=2, j=GB)
        oT = halves(6656, 512).rearrange("p (l j k) -> p l j k", l=2, j=GB)
        xr = words(3072, 1024).rearrange("p (j d) -> p j d", j=GB)
        xrs = halves(4096, 1024).rearrange("p (l j d) -> p l j d", l=2, j=GB)
        me_tt, me_bb, me_vv = words(2048, 512), words(2560, 512), words(3072, 512)
        me_hl = halves(3584, 1024).rearrange("p (r l t) -> p r l t", r=2, l=2)
        A0 = 1024
        qk = words(A0, 512).rearrange("p (h d) -> p h d", d=XD)
        sq = words(A0 + 512, 512).rearrange("p (h d) -> p h d", d=XD)
        xp = words(A0, 1024).rearrange("p (h k) -> p h k", h=8)
        cat = halves(A0 + 1024, 1024).rearrange("p (h a b d) -> p h a b d", a=2, b=2, d=XD)
        catf = halves(A0 + 1024, 1024)
        xphl = halves(A0 + 1024, 1024).rearrange("p (l h k) -> p l h k", l=2, h=8)
        catT = halves(A0 + 2048, 1024).rearrange("p (h t) -> p h t", h=16)
        xpT = halves(A0 + 3072, 1024).rearrange("p (l h k) -> p l h k", l=2, h=8)
        xn = words(A0 + 4096, 256)
        xs = halves(A0 + 4352, 256).rearrange("p (l d) -> p l d", l=2)
        xsT = halves(A0 + 4608, 256).rearrange("p (l k t) -> p l k t", l=2, k=KC)
        vf = words(A0 + 4864, 256)
        vs = halves(A0 + 5120, 256).rearrange("p (l d) -> p l d", l=2)

        st4 = sm[:, 0:24].rearrange("p (j s) -> p j s", j=GB)
        mv4 = sm[:, 24:32].rearrange("p (j s) -> p j s", j=GB)
        ve4, rs4, ss4 = sm[:, 32:36], sm[:, 36:40], sm[:, 40:44]
        rve4, rrs4 = sm[:, 44:48], sm[:, 48:52]
        mx4, nm4, es4, er4, eq4 = (sm[:, 52 + 4 * n:56 + 4 * n] for n in range(5))
        a_st, a_mv, a_ve, a_rs = sm[:, 72:78], sm[:, 78:80], sm[:, 80:81], sm[:, 81:82]
        a_mu, a_nmu, a_ss, a_ve2, a_rq = (sm[:, 96 + 32 * n:128 + 32 * n] for n in range(5))
        a_mx, a_sm, a_r, a_r2 = (sm[:, 256 + 16 * n:272 + 16 * n].rearrange("p (s h) -> p s h", s=2)
                                 for n in range(4))
        rt = sb("rt", [P, 1024], F32)
        rt_l, rt_e, rt_p, rt_m, rt_w, rt_f = (
            rt[:, 64 * n:64 * n + 64].rearrange("p (j e) -> p j e", j=GB) for n in range(6))
        rt_8 = rt[:, 384:416].rearrange("p (j k) -> p j k", j=GB)
        rt_ix = rt[:, 416:448].bitcast(U32).rearrange("p (j k) -> p j k", j=GB)
        rt_xf = rt[:, 448:464].rearrange("p (j k) -> p j k", j=GB)
        rt_mx, rt_s, rt_r, rt_s2, rt_r2 = (rt[:, 464 + 4 * n:468 + 4 * n] for n in range(5))
        rt_eq = rt[:, 512:768].rearrange("p (j e k) -> p j e k", j=GB, e=NE)

        def wcol(w, off, n=P):
            return w[:, bass.ds(off, n)]

        x_d = x.rearrange("b s d -> s b d")
        y_d = yT.rearrange("b k s -> k b s")
        out_d = out.rearrange("b s d -> s b d")
        block = ctx.enter_context(nc.Block())

        XA, XB, XC = 0, 1, 2
        SB_, QB, KB, VB, TB, OB, AB = 0, 1, 2, 3, 4, 5, 6
        GBK, UBK, WBK = 3, 4, 5

        @block.sync
        def _(sp):
            prime(sp, "sp")
            sp.dma_start(cs[:, :], cst).then_inc(sem("const_in"), 16)
            sp.dma_start(idn[:, :], ident).then_inc(sem("const_in"), 16)
            sp.dma_start(idb[:, :], identb).then_inc(sem("const_in"), 16)
            sp.dma_start(msk[:, :], maskb).then_inc(sem("const_in"), 16)
            sp.dma_start(sl[:, :], sel).then_inc(sem("const_in"), 16)
            sp.dma_start(stage[0][:, 0:WA], wa).then_inc(sem("stage_in0"), 16)
            for u in range(UNITS):
                n = u + 1
                if n >= 2:
                    sp.wait_ge(sem("stage_cut"), n - 1)
                sp.dma_start(stage[n % 2], wall[:, u * UW:(u + 1) * UW]).then_inc(
                    sem(f"stage_in{n % 2}"), 16)
            with sp.Fori(0, NG) as g:
                with sp.Fori(0, GB) as j:
                    sp.wait_ge(sem("xa_x1"), g * GB + j + PRIMED)
                    sp.dma_start(x_t[:, :], x_d[:, bass.ds(g * GB + j, 1), :]
                                 .rearrange("p b d -> p (b d)")).then_inc(sem("x_in"), 16)
                    sp.dma_start(y_t[:, :], y_d[:, bass.ds(g * GB + j, 1), :]
                                 .rearrange("p b d -> p (b d)")).then_inc(sem("y_in"), 16)
                sp.wait_ge(sem("fin"), g + 1)
                sp.dma_start(out_d[:, bass.ds(g * GB, GB), :], hid).then_inc(sem("out_done"), 16)
            sp.wait_ge(sem("out_done"), 16 * NG + PRIMED)

        @block.tensor
        def _(pe):
            prime(pe, "pe")
            mm = nc.tensor.matmul

            def three(o, l_hi, l_lo, r_hi, r_lo, start, stop):
                mm(o, l_hi, r_hi, start=start, stop=False, skip_group_check=True)
                mm(o, l_hi, r_lo, start=False, stop=False, skip_group_check=True)
                return mm(o, l_lo, r_hi, start=False, stop=stop, skip_group_check=True)

            def xa_batch(i):
                t = bank16(XA)[:, 0:512].rearrange("p (l k t) -> p l k t", l=2, k=KC)
                pe.wait_ge(sem("xa_xl"), i + 1)
                for l in range(2):
                    for k in range(KC):
                        last = nc.tensor.transpose(t[:, l, k, :], xs[:, l, k * P:(k + 1) * P], idn[:, :])
                last.then_inc(sem("xa_xTp"), 1)
                pe.wait_ge(sem("xa_yl"), i + 1)
                kv = bank(XC)
                for n, w in enumerate((512, 1024)):
                    last = three(kv, ysp[:, 2 * n, :], ysp[:, 2 * n + 1, :],
                                 wahi[:, w:w + 512], walo[:, w:w + 512], n == 0, n == 1)
                last.then_inc(sem("xa_kvp"), 1)
                pe.wait_ge(sem("xa_xT"), i + 1)
                for k in range(KC):
                    last = three(bank(XB)[:, 0:D], xsT[:, 0, k, :], xsT[:, 1, k, :],
                                 wahi[:, k * D:(k + 1) * D], walo[:, k * D:(k + 1) * D],
                                 k == 0, k == KC - 1)
                last.then_inc(sem("xa_qp"), 1)
                pe.wait_ge(sem("xa_lo"), i + 1)
                for n in range(16):
                    last = nc.tensor.transpose(bank16(XA + n // 8)[:, (n % 8) * P:(n % 8 + 1) * P],
                                               catf[:, n * P:(n + 1) * P], idn[:, :])
                last.then_inc(sem("xa_catp"), 1)
                for half in range(2):
                    n = i * 2 + half
                    if half == 0:
                        pe.wait_ge(sem("xa_catT"), i + 1)
                    for q in range(4):
                        pair = 4 * half + q
                        for b in range(2):
                            r = slice(64 * b, 64 * b + 64)
                            last = mm(ps[:, XA + b, q * P:(q + 1) * P], catT[r, pair, :],
                                      catT[r, 8 + pair, :], start=True, stop=True,
                                      skip_group_check=True)
                    last.then_inc(sem("xa_s"), 1)
                    pe.wait_ge(sem("xa_pl"), n + 1)
                    for l in range(2):
                        for h in range(8):
                            last = nc.tensor.transpose(bank16(XA + l)[:, h * P:(h + 1) * P],
                                                       xphl[:, l, h, :], idn[:, :])
                    last.then_inc(sem("xa_pTp"), 1)
                    pe.wait_ge(sem("xa_pT"), n + 1)
                    for h8 in range(8):
                        head = 8 * half + 2 * (h8 % 4) + h8 // 4
                        c = slice(head * XD, (head + 1) * XD)
                        last = three(ps[:, XC, c], xpT[:, 0, h8, :], xpT[:, 1, h8, :],
                                     vs[:, 0, c], vs[:, 1, c], True, True)
                    last.then_inc(sem("xa_pv"), 1)
                pe.wait_ge(sem("xa_cl"), i + 1)
                for l in range(2):
                    for k in range(KC):
                        last = nc.tensor.transpose(t[:, l, k, :], xs[:, l, k * P:(k + 1) * P], idn[:, :])
                last.then_inc(sem("xa_cTp"), 1)
                pe.wait_ge(sem("xa_cT"), i + 1)
                for k in range(KC):
                    w = slice(1536 + k * D, 1536 + (k + 1) * D)
                    last = three(bank(XB)[:, 0:D], xsT[:, 0, k, :], xsT[:, 1, k, :],
                                 wahi[:, w], walo[:, w], k == 0, k == KC - 1)
                last.then_inc(sem("xa_yp"), 1)

            def turn_x(n):
                pe.wait_ge(sem("rms_lo"), n)
                for l in range(2):
                    o = bank16(VB + l).rearrange("p (k j t) -> p k j t", k=KC, j=GB)
                    for k in range(KC):
                        for j in range(GB):
                            last = nc.tensor.transpose(o[:, k, j, :], xrs[:, l, j, k * P:(k + 1) * P],
                                                       idn[:, :])
                last.then_inc(sem("rms_tp"), 1)

            def project(w, wh):
                for k in range(KC):
                    off = wh + (w * D + k * P)
                    last = three(bank(QB + w), wcol(whi, off), wcol(wlo, off),
                                 xT[:, 0, k, :], xT[:, 1, k, :], k == 0, k == KC - 1)
                last.then_inc(sem("q_ps" if w == 0 else "k_ps"), 1)

            def values(wh, half):
                for jj in range(2):
                    j = 2 * half + jj
                    for k in range(KC):
                        def rv(w):
                            return w[:, bass.ds(wh + (2 * D + k * P), 2 * HW)].rearrange(
                                "p (h c) -> p h c", h=2)[:, :, 0:P]
                        last = three(bank(VB)[:, jj * 256:(jj + 1) * 256].rearrange("p (h c) -> p h c", h=2),
                                     xT[:, 0, k, j * S:(j + 1) * S], xT[:, 1, k, j * S:(j + 1) * S],
                                     rv(whi), rv(wlo), jj == 0 and k == 0, jj == 1 and k == KC - 1)
                last.then_inc(sem("v_ps"), 1)

            def scores(it):
                pe.wait_ge(sem("q_lo"), it + 1)
                pe.wait_ge(sem("k_lo"), it + 1)
                pe.wait_ge(sem("p_exp"), it + PRIMED)
                mm(bank(SB_), idb[:, :], msk[:, :], start=True, stop=False, skip_group_check=True)
                for j in range(GB):
                    c = slice(j * S, (j + 1) * S)
                    last = three(bank(SB_)[:, c], qkT[:, 0, 0, c], qkT[:, 0, 1, c],
                                 qkT[:, 1, 0, c], qkT[:, 1, 1, c], False, j == GB - 1)
                last.then_inc(sem("s_ps"), 1)

            def turn_p(it):
                pe.wait_ge(sem("p_lo"), it + 1 + PRIMED)
                pe.wait_ge(sem("pT_sb"), it + PRIMED)
                o = bank16(TB).rearrange("p (l j k) -> p l j k", l=2, j=GB)
                for l in range(2):
                    for j in range(GB):
                        last = nc.tensor.transpose(o[:, l, j, :], phl[:, l, j, :], idn[:, :])
                last.then_inc(sem("pT_ps"), 1)

            def attend(it, par, odd):
                pe.wait_ge(sem("pT_sb"), it + 1 + PRIMED)
                pe.wait_ge(sem("o_lo"), it + PRIMED)
                for j in range(GB):
                    c = slice(odd * P, odd * P + P)
                    last = three(bank(OB)[:, j * S:(j + 1) * S], vv[:, par, 0, j, c], vv[:, par, 1, j, c],
                                 pT[:, 0, j, :], pT[:, 1, j, :], j == 0, j == GB - 1)
                last.then_inc(sem("o_ps"), 1)

            def out_project(it, wh, first, end):
                pe.wait_ge(sem("o_lo"), it + 1 + PRIMED)
                for j in range(GB):
                    o = bank(AB + j // 2)[:, (j % 2) * D:(j % 2 + 1) * D]
                    last = three(o, oT[:, 0, j, :], oT[:, 1, j, :], wcol(whi, wh + 3 * D, D),
                                 wcol(wlo, wh + 3 * D, D), first and j % 2 == 0, end and j % 2 == 1)
                last.then_inc(sem("op_ps"), 1)

            def head(g, h, hm, first=False, last2=0):
                it = g * NH + h
                scores(it)
                if last2 != 2:
                    project(0, (h + 1) * HW)
                if not first:
                    turn_p(it - 1)
                if last2 != 2:
                    project(1, (h + 1) * HW)
                if not first:
                    attend(it - 1, ((hm - 1) % 4) // 2, (hm - 1) % 2)
                if not last2:
                    pe.wait_ge(sem("v_lo"), it + 2)
                    values((h - hm % 2 + 2) * HW, hm % 2)
                if not first:
                    out_project(it - 1, (h - 1) * HW, hm == 1 and first_pair[0], False)

            first_pair = [False]

            pe.wait_ge(sem("const_in"), 80)
            pe.wait_ge(sem("stage_cut"), UNITS + 1)
            with pe.Fori(0, NG) as g:
                with pe.Fori(0, GB) as jb:
                    xa_batch(g * GB + jb)
                turn_x(g * 2 + 1)
                pe.wait_ge(sem("rms_xT"), g * 2 + 1)
                project(0, 0)
                project(1, 0)
                values(0, 0)
                pe.wait_ge(sem("v_lo"), g * NH + 1)
                values(0, 1)
                first_pair[0] = True
                head(g, 0, 0, first=True)
                head(g, 1, 1)
                first_pair[0] = False
                with pe.Fori(0, 3) as t:
                    for u in range(4):
                        head(g, t * 4 + (2 + u), (2 + u) % 4)
                head(g, 14, 2, last2=1)
                head(g, 15, 3, last2=2)
                turn_p(g * NH + 15)
                attend(g * NH + 15, 1, 1)
                out_project(g * NH + 15, 15 * HW, False, True)
                turn_x(g * 2 + 2)
                pe.wait_ge(sem("rms_xT"), g * 2 + 2)
                for j in range(GB):
                    for k in range(KC):
                        xh, xl = (xT[:, l, k, j * S:(j + 1) * S] for l in range(2))
                        three(bank(OB)[:, j * NE:(j + 1) * NE], xh, xl, grw[:, 0, k, :], grw[:, 1, k, :],
                              k == 0, False)
                        last = mm(bank(OB)[:, j * NE:(j + 1) * NE], xl, grw[:, 1, k, :], start=False,
                                  stop=k == KC - 1, skip_group_check=True)
                last.then_inc(sem("rt_ps"), 1)
                pe.wait_ge(sem("rt_cat"), g + 1)
                for j in range(GB):
                    last = nc.tensor.transpose(bank16(OB)[:, j * P:(j + 1) * P], wcat[:, j, :], idn[:, :])
                last.then_inc(sem("wT_ps"), 1)
                pe.wait_ge(sem("wT_sb"), g + 1)

                def up(c):
                    n = g * NC + c
                    base = NH * HW
                    for w, b, free, made in ((0, GBK, "me_a", "g_ps"), (1, UBK, "me_b", "u_ps")):
                        pe.wait_ge(sem(free), n + PRIMED)
                        for k in range(KC):
                            off = c * CW + (base + w * D + k * P)
                            last = three(bank(b), wcol(whi, off), wcol(wlo, off), xT[:, 0, k, :],
                                         xT[:, 1, k, :], k == 0, k == KC - 1)
                        last.then_inc(sem(made), 1)
                    pe.wait_ge(sem("me_v"), n + PRIMED)
                    mm(bank(WBK), wcol(sl, c * P), wT[:, :], start=True, stop=True,
                       skip_group_check=True).then_inc(sem("w_ps"), 1)

                def down(c, par, first, end):
                    n = g * NC + c
                    pe.wait_ge(sem("me_lo"), n + 1 + PRIMED)
                    off = c * CW + (NH * HW + 2 * D)
                    for j in range(GB):
                        o = bank(AB + j // 2)[:, (j % 2) * D:(j % 2 + 1) * D]
                        cc = slice(j * S, (j + 1) * S)
                        last = three(o, me_hl[:, par, 0, cc], me_hl[:, par, 1, cc], wcol(whi, off, D),
                                     wcol(wlo, off, D), first and j % 2 == 0, end and j % 2 == 1)
                    last.then_inc(sem("d_ps"), 1)

                up(0)
                up(1)
                down(0, 0, True, False)
                up(2)
                down(1, 1, False, False)
                with pe.Fori(1, 12) as t:
                    for u in range(2):
                        up(t * 2 + (1 + u))
                        down(t * 2 + u, u % 2, False, False)
                down(24, 0, False, True)

        @block.scalar
        def _(act):
            prime(act, "act")
            A = nc.scalar.activation

            def xa_batch(i):
                act.wait_ge(sem("xa_xn"), i + 1)
                A(xs[:, 0, :], xn, ACT.Copy).then_inc(sem("xa_xh"), 1)
                act.wait_ge(sem("xa_v"), i + 1)
                A(vs[:, 0, :], vf, ACT.Copy).then_inc(sem("xa_vh"), 1)
                act.wait_ge(sem("xa_c"), i + 1)
                A(sq, qk, ACT.Square).then_inc(sem("xa_sq"), 1)
                act.wait_ge(sem("xa_n"), i + 1)
                A(cat[:, 0:16, 0, :, :], qk[:, 0:16, :].unsqueeze(2).broadcast_to([P, 16, 2, XD]), ACT.Copy)
                A(cat[:, 16:32, :, 0, :], qk[:, 16:32, :].unsqueeze(2).broadcast_to([P, 16, 2, XD]),
                  ACT.Copy).then_inc(sem("xa_hi"), 1)
                for half in range(2):
                    n = i * 2 + half
                    act.wait_ge(sem("xa_sub"), n + 1)
                    A(xp, xp, ACT.Exp, scale=XD ** -0.5).then_inc(sem("xa_e"), 1)
                    act.wait_ge(sem("xa_pn"), n + 1)
                    A(xphl[:, 0], xp, ACT.Copy).then_inc(sem("xa_ph"), 1)
                act.wait_ge(sem("xa_pv"), i * 2 + 2 + PRIMED)
                A(xs[:, 0, :], bank(XC)[:, 0:D], ACT.Copy, scale=1.0 / PS).then_inc(sem("xa_ch"), 1)

            def rms(n, ready, count):
                act.wait_ge(sem(ready), count)
                for j in range(GB):
                    last = A(xr[:, j, :], hid[:, j, :], ACT.Square, accum_out=ss4[:, j:j + 1])
                last.then_inc(sem("rms_ss"), 1)
                act.wait_ge(sem("rms_xr"), n)
                A(xrs[:, 0], xr, ACT.Copy).then_inc(sem("rms_hi"), 1)

            def hi_q(w, it):
                act.wait_ge(sem(("q_ps", "k_ps")[w]), it + 1)
                A(qkT[:, w, 0, :], bank(QB + w), ACT.Copy, scale=1.0 / WS).then_inc(
                    sem(("q_hi", "k_hi")[w]), 1)

            def hi_v(cnt, par, half):
                act.wait_ge(sem("v_ps"), cnt)
                A(vv[:, par, 0, 2 * half:2 * half + 2, :].rearrange("p j c -> p (j c)"), bank(VB),
                  ACT.Copy, scale=1.0 / WS).then_inc(sem("v_hi"), 1)

            def hi_o(it):
                act.wait_ge(sem("o_ps"), it + 1 + PRIMED)
                act.wait_ge(sem("op_ps"), it + PRIMED)
                A(oT[:, 0].rearrange("p j k -> p (j k)"), bank(OB), ACT.Copy,
                  scale=1.0 / PS).then_inc(sem("o_hi"), 1)

            def head(g, h, hm, first=False, last2=0):
                it = g * NH + h
                act.wait_ge(sem("m_neg"), it + 1)
                act.wait_ge(sem("p_lo"), it + PRIMED)
                for j in range(GB):
                    last = A(pr[:, j, :], bank(SB_)[:, j * S:(j + 1) * S], ACT.Exp,
                             bias=nm4[:, j:j + 1], scale=QHD ** -0.5, accum_out=es4[:, j:j + 1])
                last.then_inc(sem("p_exp"), 1)
                if last2 != 2:
                    hi_q(0, it + 1)
                    hi_q(1, it + 1)
                if not first:
                    hi_o(it - 1)
                if not last2:
                    hi_v(it + 3, ((hm + 2) % 4) // 2, hm % 2)
                act.wait_ge(sem("p_n"), it + 1)
                act.wait_ge(sem("pT_ps"), it + PRIMED)
                A(phl[:, 0], pr, ACT.Copy).then_inc(sem("p_hi"), 1)

            act.wait_ge(sem("const_in"), 80)
            A(gt[:, :], cs[:, C_GATE:C_GATE + 2], ACT.Tanh).then_inc(sem("gates"), 1)
            A(grw[:, 0].rearrange("p k e -> p (k e)"), cs[:, C_RT:C_RT + KC * NE], ACT.Copy,
              scale=WS).then_inc(sem("gr_hi"), 1)
            act.wait_ge(sem("stage_in0"), 16)
            A(wahi[:, :], stage[0][:, 0:WA], ACT.Copy, scale=WS).then_inc(sem("stage_hi"), 1)
            for u in range(UNITS):
                n = u + 1
                act.wait_ge(sem(f"stage_in{n % 2}"), 16 * (n // 2 + 1))
                A(whi[:, u * UW:(u + 1) * UW], stage[(u + 1) % 2], ACT.Copy,
                  scale=WS).then_inc(sem("stage_hi"), 1)
            with act.Fori(0, NG) as g:
                with act.Fori(0, GB) as jb:
                    xa_batch(g * GB + jb)
                rms(g * 2 + 1, "h0", g + 1)
                hi_q(0, g * NH)
                hi_q(1, g * NH)
                hi_v(g * NH + 1, 0, 0)
                hi_v(g * NH + 2, 0, 1)
                head(g, 0, 0, first=True)
                head(g, 1, 1)
                with act.Fori(0, 3) as t:
                    for u in range(4):
                        head(g, t * 4 + (2 + u), (2 + u) % 4)
                head(g, 14, 2, last2=1)
                head(g, 15, 3, last2=2)
                hi_o(g * NH + 15)
                rms(g * 2 + 2, "hid", g + 1)
                act.wait_ge(sem("rt_sub"), g + 1)
                A(rt_e, rt_l, ACT.Exp, scale=1.0 / WS).then_inc(sem("rt_exp"), 1)

                def chunk(c, par, first=False):
                    n = g * NC + c
                    act.wait_ge(sem("g_ps"), n + 1)
                    act.wait_ge(sem("me_a"), n + PRIMED)
                    A(me_tt, bank(GBK), ACT.Tanh, scale=0.5 / WS).then_inc(sem("me_t"), 1)
                    act.wait_ge(sem("me_v"), n + 1 + PRIMED)
                    if not first:
                        act.wait_ge(sem("d_ps"), n - 1 + PRIMED)
                    A(me_hl[:, par, 0, :], me_vv, ACT.Copy).then_inc(sem("me_hi"), 1)

                chunk(0, 0, first=True)
                with act.Fori(0, 12) as t:
                    for u in range(2):
                        chunk(t * 2 + (1 + u), (1 + u) % 2)

        @block.gpsimd
        def _(pool):
            prime(pool, "pool")
            TT = nc.gpsimd.tensor_tensor

            def rsqrt(out, tmp, in_, scale, eps, w, name, count):
                nc.gpsimd.tensor_scalar(tmp, in_, scale, eps, ALU.mult, ALU.add).then_inc(
                    sem(name + "_ve"), 1)
                pool.wait_ge(sem(name + "_ve"), count)
                TT(out, tmp, mhalf[:, 0:w], ALU.pow).then_inc(sem(name + "_rs"), 1)

            def xa_batch(i):
                pool.wait_ge(sem("xa_mv"), i + 1)
                apart(pool)
                rsqrt(a_rs, a_ve, a_mv[:, 1:2], 1.0, 1e-5, 1, "xa", i + 1)
                pool.wait_ge(sem("y_in"), (i + 1) * 16)
                apart(pool)
                nc.gpsimd.tensor_copy(ysp[:, 0, 0:MAIN], y_t[:, 0:MAIN])
                nc.gpsimd.tensor_copy(ysp[:, 2, MAIN:S], y_t[:, MAIN:S]).then_inc(sem("xa_yh"), 1)
                pool.wait_ge(sem("xa_yh"), i + 1)
                TT(ysp[:, 1, 0:MAIN], y_t[:, 0:MAIN], ysp[:, 0, 0:MAIN], ALU.subtract)
                TT(ysp[:, 3, MAIN:S], y_t[:, MAIN:S], ysp[:, 2, MAIN:S],
                   ALU.subtract).then_inc(sem("xa_yl"), 1)
                pool.wait_ge(sem("xa_vh"), i + 1)
                TT(vs[:, 1, :], vf, vs[:, 0, :], ALU.subtract).then_inc(sem("xa_vl"), 1)
                pool.wait_ge(sem("xa_ss"), i + 1)
                apart(pool)
                rsqrt(a_rq, a_ve2, a_ss, 1.0 / XD, 1e-6, 32, "xa_h", i + 1)
                pool.wait_ge(sem("xa_n1"), i + 1)
                f = qk.rearrange("p h d -> p (h d)")
                TT(f, f, cs[:, C_LNW:C_LNW + 512], ALU.mult).then_inc(sem("xa_n2"), 1)
                pool.wait_ge(sem("xa_n2"), i + 1)
                TT(f, f, cs[:, C_LNB:C_LNB + 512], ALU.add).then_inc(sem("xa_n"), 1)
                pool.wait_ge(sem("xa_hi"), i + 1)
                pool.wait_ge(sem("xa_n"), i + 1)
                TT(cat[:, 0:16, 1, :, :], qk[:, 0:16, :].unsqueeze(2).broadcast_to([P, 16, 2, XD]),
                   cat[:, 0:16, 0, :, :], ALU.subtract)
                TT(cat[:, 16:32, :, 1, :], qk[:, 16:32, :].unsqueeze(2).broadcast_to([P, 16, 2, XD]),
                   cat[:, 16:32, :, 0, :], ALU.subtract).then_inc(sem("xa_lo"), 1)
                for half in range(2):
                    n = i * 2 + half
                    pool.wait_ge(sem("xa_r2"), n + 1)
                    for s, k in ((0, slice(0, MAIN)), (1, slice(MAIN, S))):
                        last = TT(xp[:, :, k], xp[:, :, k],
                                  a_r2[:, s, :].unsqueeze(2).broadcast_to([P, 8, k.stop - k.start]), ALU.mult)
                    last.then_inc(sem("xa_pn"), 1)
                    pool.wait_ge(sem("xa_ph"), n + 1)
                    TT(xphl[:, 1], xp, xphl[:, 0], ALU.subtract).then_inc(sem("xa_pl"), 1)

            def rms(n):
                pool.wait_ge(sem("rms_ss"), n)
                apart(pool)
                rsqrt(rrs4, rve4, ss4, 1.0 / D, 1e-6, 4, "rms", n)
                pool.wait_ge(sem("rms_hi"), n)
                TT(xrs[:, 1], xr, xrs[:, 0], ALU.subtract).then_inc(sem("rms_lo"), 1)

            nc.gpsimd.memset(mhalf[:, :], -0.5)
            nc.gpsimd.memset(ysp[:, :, :], 0.0)
            nc.gpsimd.memset(wcat[:, :, :], 0.0).then_inc(sem("zeroed"), 1)
            pool.wait_ge(sem("zeroed"), 1)
            nc.gpsimd.memset(wcat[:, :, NE:NE + 1], 1.0).then_inc(sem("zeroed"), 1)
            pool.wait_ge(sem("const_in"), 80)
            with pool.Fori(0, NG) as g:
                with pool.Fori(0, GB) as jb:
                    xa_batch(g * GB + jb)
                pool.wait_ge(sem("ln_mv"), g + 1)
                apart(pool)
                rsqrt(rs4, ve4, mv4[:, :, 1], 1.0, 1e-5, 4, "ln", g + 1)
                rms(g * 2 + 1)
                with pool.Fori(0, NH) as h:
                    it = g * NH + h
                    pool.wait_ge(sem("p_r"), it + 1)
                    TT(pr, pr, eq4.unsqueeze(2).broadcast_to([P, GB, S]), ALU.mult).then_inc(
                        sem("p_n"), 1)
                    pool.wait_ge(sem("p_hi"), it + 1)
                    TT(phl[:, 1], pr, phl[:, 0], ALU.subtract).then_inc(sem("p_lo"), 1)
                rms(g * 2 + 2)

                def chunk(c, par):
                    n = g * NC + c
                    pool.wait_ge(sem("me_hi"), n + 1)
                    TT(me_hl[:, par, 1, :], me_vv, me_hl[:, par, 0, :], ALU.subtract).then_inc(
                        sem("me_lo"), 1)

                chunk(0, 0)
                with pool.Fori(0, 12) as t:
                    for u in range(2):
                        chunk(t * 2 + (1 + u), (1 + u) % 2)

        @block.vector
        def _(dve):
            prime(dve, "dve")
            V = nc.vector
            STT, TT = V.scalar_tensor_tensor, V.tensor_tensor

            def xa_batch(g, jb):
                i = g * GB + jb
                dve.wait_ge(sem("x_in"), (i + 1) * 16)
                V.bn_stats(a_st, x_t[:, :]).then_inc(sem("xa_st"), 1)
                dve.wait_ge(sem("xa_st"), i + 1)
                apart(dve)
                V.bn_aggr(a_mv, a_st).then_inc(sem("xa_mv"), 1)
                dve.wait_ge(sem("xa_rs"), i + 1)
                V.tensor_scalar(xn, x_t[:, :], a_mv[:, 0:1], a_rs, ALU.subtract, ALU.mult).then_inc(
                    sem("xa_xn"), 1)
                dve.wait_ge(sem("xa_xh"), i + 1)
                TT(xs[:, 1, :], xn, xs[:, 0, :], ALU.subtract).then_inc(sem("xa_xl"), 1)
                t = bank16(XA)[:, 0:512]
                dve.wait_ge(sem("xa_xTp"), i + 1)
                V.tensor_copy(xsT.rearrange("p l k t -> p (l k t)"), t).then_inc(sem("xa_xT"), 1)
                f = qk.rearrange("p h d -> p (h d)")
                dve.wait_ge(sem("xa_kvp"), i + 1)
                STT(vf, bank(XC)[:, 256:512], 1.0 / WS, cs[:, 512:768], ALU.mult, ALU.add).then_inc(
                    sem("xa_v"), 1)
                STT(f[:, 256:512], bank(XC)[:, 0:256], 1.0 / WS, cs[:, 256:512], ALU.mult, ALU.add)
                dve.wait_ge(sem("xa_qp"), i + 1)
                STT(f[:, 0:256], bank(XB)[:, 0:256], 1.0 / WS, cs[:, 0:256], ALU.mult, ALU.add).then_inc(
                    sem("xa_qk"), 1)
                dve.wait_ge(sem("xa_qk"), i + 1)
                V.tensor_reduce(a_mu, qk, AX.X, ALU.add).then_inc(sem("xa_mu"), 1)
                dve.wait_ge(sem("xa_mu"), i + 1)
                V.tensor_scalar(a_nmu, a_mu, -1.0 / XD, None, ALU.mult).then_inc(sem("xa_nmu"), 1)
                dve.wait_ge(sem("xa_nmu"), i + 1)
                TT(qk, qk, a_nmu.unsqueeze(2).broadcast_to([P, 32, XD]), ALU.add).then_inc(sem("xa_c"), 1)
                dve.wait_ge(sem("xa_sq"), i + 1)
                V.tensor_reduce(a_ss, sq, AX.X, ALU.add).then_inc(sem("xa_ss"), 1)
                dve.wait_ge(sem("xa_h_rs"), i + 1)
                TT(qk, qk, a_rq.unsqueeze(2).broadcast_to([P, 32, XD]), ALU.mult).then_inc(sem("xa_n1"), 1)
                dve.wait_ge(sem("xa_catp"), i + 1)
                V.tensor_copy(catT.rearrange("p h t -> p (h t)"), bank16(XA, 2)).then_inc(sem("xa_catT"), 1)
                segs = ((0, slice(0, MAIN)), (1, slice(MAIN, S)))
                sc = bank(XA, 2).rearrange("p (h k) -> p h k", h=8)
                for half in range(2):
                    n = i * 2 + half
                    dve.wait_ge(sem("xa_s"), n + 1)
                    for s, k in segs:
                        last = V.tensor_reduce(a_mx[:, s, :], sc[:, :, k], AX.X, ALU.max)
                    last.then_inc(sem("xa_mx"), 1)
                    dve.wait_ge(sem("xa_mx"), n + 1)
                    for s, k in segs:
                        last = TT(xp[:, :, k], sc[:, :, k],
                                  a_mx[:, s, :].unsqueeze(2).broadcast_to([P, 8, k.stop - k.start]),
                                  ALU.subtract)
                    last.then_inc(sem("xa_sub"), 1)
                    dve.wait_ge(sem("xa_e"), n + 1)
                    for s, k in segs:
                        last = V.tensor_reduce(a_sm[:, s, :], xp[:, :, k], AX.X, ALU.add)
                    last.then_inc(sem("xa_sm"), 1)
                    dve.wait_ge(sem("xa_sm"), n + 1)
                    V.reciprocal(a_r, a_sm).then_inc(sem("xa_r"), 1)
                    dve.wait_ge(sem("xa_r"), n + 1)
                    V.tensor_scalar(a_r2, a_r, PS, None, ALU.mult).then_inc(sem("xa_r2"), 1)
                    dve.wait_ge(sem("xa_pTp"), n + 1)
                    dve.wait_ge(sem("xa_pv"), n + PRIMED)
                    V.tensor_copy(xpT.rearrange("p l h k -> p (l h k)"), bank16(XA, 2)).then_inc(
                        sem("xa_pT"), 1)
                dve.wait_ge(sem("xa_ch"), i + 1)
                STT(xs[:, 1, :], bank(XC)[:, 0:D], 1.0 / PS, xs[:, 0, :], ALU.mult, ALU.subtract).then_inc(
                    sem("xa_cl"), 1)
                dve.wait_ge(sem("xa_cTp"), i + 1)
                V.tensor_copy(xsT.rearrange("p l k t -> p (l k t)"), t).then_inc(sem("xa_cT"), 1)
                dve.wait_ge(sem("xa_yp"), i + 1)
                STT(xn, bank(XB)[:, 0:D], 1.0 / WS, cs[:, C_BO:C_BO + D], ALU.mult, ALU.add).then_inc(
                    sem("xa_o"), 1)
                dve.wait_ge(sem("xa_o"), i + 1)
                STT(x1[:, bass.ds(jb, 1), :].rearrange("p b d -> p (b d)"), xn, gt[:, 0:1], x_t[:, :],
                    ALU.mult, ALU.add).then_inc(sem("xa_x1"), 1)

            def rms(n, c_ln):
                dve.wait_ge(sem("rms_rs"), n)
                for j in range(GB):
                    last = STT(xr[:, j, :], hid[:, j, :], rrs4[:, j:j + 1], cs[:, c_ln:c_ln + D],
                               ALU.mult, ALU.mult)
                last.then_inc(sem("rms_xr"), 1)
                dve.wait_ge(sem("rms_tp"), n)
                V.tensor_copy(xT.rearrange("p l k t -> p (l k t)"), bank16(VB, 2)).then_inc(sem("rms_xT"), 1)

            def lo_q(w, it):
                dve.wait_ge(sem(("q_hi", "k_hi")[w]), it + 1)
                STT(qkT[:, w, 1, :], bank(QB + w), 1.0 / WS, qkT[:, w, 0, :], ALU.mult,
                    ALU.subtract).then_inc(sem(("q_lo", "k_lo")[w]), 1)

            def lo_v(cnt, par, half):
                dve.wait_ge(sem("v_hi"), cnt)
                js = slice(2 * half, 2 * half + 2)
                STT(vv[:, par, 1, js, :].rearrange("p j c -> p (j c)"), bank(VB), 1.0 / WS,
                    vv[:, par, 0, js, :].rearrange("p j c -> p (j c)"), ALU.mult,
                    ALU.subtract).then_inc(sem("v_lo"), 1)

            def copy_pT(it):
                dve.wait_ge(sem("pT_ps"), it + 1 + PRIMED)
                dve.wait_ge(sem("o_ps"), it + PRIMED)
                V.tensor_copy(pT.rearrange("p l j k -> p (l j k)"), bank16(TB)).then_inc(sem("pT_sb"), 1)

            def lo_o(it):
                dve.wait_ge(sem("o_hi"), it + 1)
                STT(oT[:, 1].rearrange("p j k -> p (j k)"), bank(OB), 1.0 / PS,
                    oT[:, 0].rearrange("p j k -> p (j k)"), ALU.mult, ALU.subtract).then_inc(
                    sem("o_lo"), 1)

            def head(g, h, hm, first=False, last2=0):
                it = g * NH + h
                dve.wait_ge(sem("s_ps"), it + 1)
                V.tensor_reduce(mx4, bank(SB_).rearrange("p (j k) -> p j k", j=GB), AX.X,
                                ALU.max).then_inc(sem("m_max"), 1)
                dve.wait_ge(sem("m_max"), it + 1)
                V.tensor_scalar(nm4, mx4, -(QHD ** -0.5), None, ALU.mult).then_inc(sem("m_neg"), 1)
                if last2 != 2:
                    lo_q(0, it + 1)
                if not first:
                    copy_pT(it - 1)
                dve.wait_ge(sem("p_exp"), it + 1 + PRIMED)
                V.reciprocal(er4, es4).then_inc(sem("p_rec"), 1)
                dve.wait_ge(sem("p_rec"), it + 1)
                V.tensor_scalar(eq4, er4, PS, None, ALU.mult).then_inc(sem("p_r"), 1)
                if last2 != 2:
                    lo_q(1, it + 1)
                if not first:
                    lo_o(it - 1)
                if not last2:
                    lo_v(it + 3, ((hm + 2) % 4) // 2, hm % 2)

            dve.wait_ge(sem("const_in"), 80)
            dve.wait_ge(sem("gr_hi"), 1)
            STT(grw[:, 1].rearrange("p k e -> p (k e)"), cs[:, C_RT:C_RT + KC * NE], WS,
                grw[:, 0].rearrange("p k e -> p (k e)"), ALU.mult, ALU.subtract)
            dve.wait_ge(sem("stage_hi"), 1)
            STT(walo[:, :], stage[0][:, 0:WA], WS, wahi[:, :], ALU.mult, ALU.subtract).then_inc(
                sem("stage_cut"), 1)
            for u in range(UNITS):
                dve.wait_ge(sem("stage_hi"), u + 2)
                c = slice(u * UW, (u + 1) * UW)
                STT(wlo[:, c], stage[(u + 1) % 2], WS, whi[:, c], ALU.mult, ALU.subtract).then_inc(
                    sem("stage_cut"), 1)
            dve.wait_ge(sem("gates"), 1)
            dve.wait_ge(sem("zeroed"), 2)
            with dve.Fori(0, NG) as g:
                with dve.Fori(0, GB) as jb:
                    xa_batch(g, jb)
                dve.wait_ge(sem("xa_x1"), (g + 1) * GB + PRIMED)
                for j in range(GB):
                    last = V.bn_stats(st4[:, j, :], x1[:, j, :])
                last.then_inc(sem("ln_st"), 1)
                dve.wait_ge(sem("ln_st"), g + 1)
                apart(dve)
                for j in range(GB):
                    last = V.bn_aggr(mv4[:, j, :], st4[:, j, :])
                last.then_inc(sem("ln_mv"), 1)
                dve.wait_ge(sem("ln_rs"), g + 1)
                dve.wait_ge(sem("out_done"), g * 16 + PRIMED)
                for j in range(GB):
                    last = V.tensor_scalar(hid[:, j, :], x1[:, j, :], mv4[:, j, 0:1], rs4[:, j:j + 1],
                                           ALU.subtract, ALU.mult)
                last.then_inc(sem("h0"), 1)
                rms(g * 2 + 1, C_LN1)
                lo_q(0, g * NH)
                lo_q(1, g * NH)
                lo_v(g * NH + 1, 0, 0)
                lo_v(g * NH + 2, 0, 1)
                head(g, 0, 0, first=True)
                head(g, 1, 1)
                with dve.Fori(0, 3) as t:
                    for u in range(4):
                        head(g, t * 4 + (2 + u), (2 + u) % 4)
                head(g, 14, 2, last2=1)
                head(g, 15, 3, last2=2)
                copy_pT(g * NH + 15)
                lo_o(g * NH + 15)
                hf = hid.rearrange("p j d -> p (j d)")
                dve.wait_ge(sem("op_ps"), g * NH + NH + PRIMED)
                STT(hf, bank(AB, 2), 1.0 / WS, hf, ALU.mult, ALU.add).then_inc(sem("hid"), 1)
                rms(g * 2 + 2, C_LN2)
                RC = 14
                step = [0]

                def link(ins):
                    step[0] += 1
                    ins.then_inc(sem("rt_step"), 1)
                    dve.wait_ge(sem("rt_step"), g * RC + step[0])
                    apart(dve)

                b16 = [P, GB, NE]
                dve.wait_ge(sem("rt_ps"), g + 1)
                lg = bank(OB)[:, 0:GB * NE].rearrange("p (j e) -> p j e", j=GB)
                link(V.tensor_reduce(rt_mx, lg, AX.X, ALU.max))
                TT(rt_l, lg, rt_mx.unsqueeze(2).broadcast_to(b16), ALU.subtract).then_inc(sem("rt_sub"), 1)
                dve.wait_ge(sem("rt_exp"), g + 1)
                link(V.tensor_reduce(rt_s, rt_e, AX.X, ALU.add))
                link(V.reciprocal(rt_r, rt_s))
                link(TT(rt_p, rt_e, rt_r.unsqueeze(2).broadcast_to(b16), ALU.mult))
                for j in range(GB):
                    last = V.max(rt_8[:, j, :], rt_p[:, j, :])
                link(last)
                for j in range(GB):
                    last = V.max_index(rt_ix[:, j, :], rt_8[:, j, :], rt_p[:, j, :])
                link(last)
                link(V.tensor_copy(rt_xf, rt_ix[:, :, 0:TOPK]))
                link(TT(rt_eq, cs[:, C_IOTA:C_IOTA + NE].unsqueeze(1).unsqueeze(3)
                        .broadcast_to([P, GB, NE, TOPK]),
                        rt_xf.unsqueeze(2).broadcast_to([P, GB, NE, TOPK]), ALU.is_equal))
                link(V.tensor_reduce(rt_m, rt_eq, AX.X, ALU.add))
                link(TT(rt_w, rt_p, rt_m, ALU.mult))
                link(V.tensor_reduce(rt_s2, rt_w, AX.X, ALU.add))
                link(V.reciprocal(rt_r2, rt_s2))
                link(TT(rt_f, rt_w, rt_r2.unsqueeze(2).broadcast_to(b16), ALU.mult))
                link(V.tensor_copy(wcat[:, :, 0:NE], rt_f))
                assert step[0] == RC
                TT(wcat[:, :, 32:32 + NE], rt_f, wcat[:, :, 0:NE], ALU.subtract).then_inc(sem("rt_cat"), 1)
                dve.wait_ge(sem("wT_ps"), g + 1)
                V.tensor_copy(wT[:, :], bank16(OB)[:, 0:T]).then_inc(sem("wT_sb"), 1)

                def chunk(c):
                    n = g * NC + c
                    dve.wait_ge(sem("me_t"), n + 1)
                    STT(me_bb, me_tt, 1.0, bank(GBK), ALU.add, ALU.mult).then_inc(sem("me_a"), 1)
                    dve.wait_ge(sem("u_ps"), n + 1)
                    dve.wait_ge(sem("me_a"), n + 1 + PRIMED)
                    TT(me_bb, me_bb, bank(UBK), ALU.mult).then_inc(sem("me_b"), 1)
                    dve.wait_ge(sem("w_ps"), n + 1)
                    dve.wait_ge(sem("me_b"), n + 1 + PRIMED)
                    dve.wait_ge(sem("me_lo"), n + PRIMED)
                    TT(me_vv, me_bb, bank(WBK), ALU.mult).then_inc(sem("me_v"), 1)

                with dve.Fori(0, NC) as c:
                    chunk(c)
                dve.wait_ge(sem("d_ps"), (g + 1) * NC + PRIMED)
                STT(hf, bank(AB, 2), 1.0 / WS, hf, ALU.mult, ALU.add).then_inc(sem("fin_h"), 1)
                dve.wait_ge(sem("fin_h"), g + 1)
                STT(hf, hf, gt[:, 1:2], x1.rearrange("p j d -> p (j d)"), ALU.mult, ALU.add).then_inc(
                    sem("fin"), 1)


def kernel(x, ctx_1024, g_xattn, g_ffn, L0_xattn_Wq, L0_xattn_bq, L0_xattn_Wk, L0_xattn_bk,
           L0_xattn_Wv, L0_xattn_bv, L0_xattn_Wkv_dca, L0_xattn_bkv_dca, L0_xattn_qn_w, L0_xattn_qn_b,
           L0_xattn_kn_w, L0_xattn_kn_b, L0_xattn_kn_dca_w, L0_xattn_kn_dca_b, L0_xattn_Wo, L0_xattn_bo,
           L0_ffn_positions, L0_ffn_ln1_w, L0_ffn_ln2_w, L0_ffn_q_w, L0_ffn_kv_w, L0_ffn_o_w,
           L0_ffn_gate_w, L0_ffn_w1, L0_ffn_w2, L0_ffn_sh_gu_w, L0_ffn_sh_down_w):
    import numpy as np
    import ml_dtypes
    import concourse.bacc as bacc
    from concourse import mybir
    from concourse.bass_utils import run_bass_kernel_spmd as run

    f = lambda a: np.asarray(a, dtype=np.float32)
    wkv = np.concatenate([f(L0_xattn_Wk), f(L0_xattn_Wv)], 1).reshape(P, XH, 2, XD)
    wkv = wkv.transpose(0, 2, 1, 3).reshape(P, 512)
    bkv = np.concatenate([f(L0_xattn_bk), f(L0_xattn_bv)]).reshape(XH, 2, XD).transpose(1, 0, 2).reshape(512)
    two = lambda w: f(w).reshape(KC, P, D).transpose(1, 0, 2).reshape(P, KC * D)
    wa = np.concatenate([two(L0_xattn_Wq), wkv, f(L0_xattn_Wkv_dca), two(L0_xattn_Wo)], 1)
    inT = lambda w: f(w).reshape(-1, P, KC, P).transpose(3, 0, 2, 1)
    q = inT(f(L0_ffn_q_w).reshape(NH, QHD, D)[:, :HD].reshape(NH * HD, D))
    kv = f(L0_ffn_kv_w)
    k, v = inT(kv[:NH * HD]), inT(kv[NH * HD:2 * NH * HD])
    o = f(L0_ffn_o_w).reshape(D, NH, HD).transpose(2, 1, 0)
    heads = np.concatenate([w.reshape(P, NH, D) for w in (q, k, v, o)], 2).reshape(P, NH * HW)
    w1, w2 = f(L0_ffn_w1), f(L0_ffn_w2)
    sgu = f(L0_ffn_sh_gu_w)
    pad = np.zeros((NC * P - NE * EI - SHI, D), np.float32)
    wg = inT(np.concatenate([w1[:, :EI].reshape(-1, D), sgu[:SHI], pad]))
    wu = inT(np.concatenate([w1[:, EI:].reshape(-1, D), sgu[SHI:], pad]))
    wd = np.concatenate([w2.transpose(0, 2, 1).reshape(-1, D), f(L0_ffn_sh_down_w).T, pad])
    wd = wd.reshape(NC, P, D).transpose(1, 0, 2)
    chunks = np.concatenate([wg.reshape(P, NC, D), wu.reshape(P, NC, D), wd], 2).reshape(P, NC * CW)
    wall = np.ascontiguousarray(np.concatenate([heads, chunks], 1))
    c = np.zeros((P, CWID), np.float32)
    c[:, 0:256] = f(L0_xattn_bq)
    c[:MAIN, 256:768] = bkv
    c[MAIN:, 256:768] = f(L0_xattn_bkv_dca)
    for off, qn, kn, kd in ((C_LNW, L0_xattn_qn_w, L0_xattn_kn_w, L0_xattn_kn_dca_w),
                            (C_LNB, L0_xattn_qn_b, L0_xattn_kn_b, L0_xattn_kn_dca_b)):
        c[:, off:off + 256] = np.tile(f(qn), XH)
        c[:MAIN, off + 256:off + 512] = np.tile(f(kn), XH)
        c[MAIN:, off + 256:off + 512] = np.tile(f(kd), XH)
    c[:, C_BO:C_BO + D] = f(L0_xattn_bo)
    c[:, C_LN1:C_LN1 + D] = f(L0_ffn_ln1_w)
    c[:, C_LN2:C_LN2 + D] = f(L0_ffn_ln2_w)
    c[:, C_GATE] = f(g_xattn)[0]
    c[:, C_GATE + 1] = f(g_ffn)[0]
    c[:, C_RT:C_RT + KC * NE] = f(L0_ffn_gate_w).reshape(NE, KC, P).transpose(2, 1, 0).reshape(P, KC * NE)
    c[:, C_IOTA:C_IOTA + NE] = np.arange(NE)
    sel = np.zeros((P, NC * P), np.float16)
    rows = np.arange(NC * P)
    sel[np.minimum(rows // EI, NE), rows] = 0.5 / WS / WS
    sel[32 + np.minimum(rows // EI, NE), rows] = 0.5 / WS / WS
    mask = np.where(np.tril(np.ones((S, S), bool)), 0.0, MASKED)
    arrays = {
        "in_x": f(x), "in_yT": np.ascontiguousarray(f(ctx_1024).transpose(0, 2, 1)),
        "in_wa": np.ascontiguousarray(wa), "in_wall": wall, "in_cst": c,
        "in_ident": np.eye(P, dtype=np.float16), "in_identb": np.eye(P).astype(ml_dtypes.bfloat16),
        "in_maskb": np.tile(mask, (1, GB)).astype(ml_dtypes.bfloat16), "in_sel": sel,
    }
    nc = bacc.Bacc("TRN2", target_bir_lowering=False, num_devices=1)
    args = [nc.dram_tensor(n, a.shape, mybir.dt.from_np(a.dtype), kind="ExternalInput").ap()
            for n, a in arrays.items()]
    args.append(nc.dram_tensor("out_0", (NB, S, D), mybir.dt.float32, kind="ExternalOutput").ap())
    build(nc, *args)
    r = run(nc, [arrays], core_ids=[0])
    return r.results[0]["out_0"]
```

```python
from contextlib import ExitStack

import numpy as np
import concourse.bass as bass
from concourse import mybir
from concourse.alu_op_type import AluOpType as ALU

ACT = mybir.ActivationFunctionType
AX = mybir.AxisListType
F32, F16, BF16 = mybir.dt.float32, mybir.dt.float16, mybir.dt.bfloat16
U32, I32 = mybir.dt.uint32, mybir.dt.int32

P = 128
NB, S, D = 16, 128, 256
KC = D // P
GB = 4
NG = NB // GB
T = GB * S
XH, XD = 16, 16
DCA = 16
MAIN = S - DCA
NH, QHD, HD = 16, 192, 128
NE, EI, TOPK = 16, 176, 4
SHI = 352
NC = -(-(NE * EI + SHI) // P)
HW = 3 * D + D
CW = 3 * D
WALL = NH * HW + NC * CW
UNITS = 32
UW = WALL // UNITS
WS = 64.0
PS = 256.0
WA = 2048
NQ = 4
QH = XH // NQ
PERIODS = GB + 1
SLOTS = NC // PERIODS
UPP = UNITS // GB
NEWTON = 13
SEGS = ((0, slice(0, MAIN)), (1, slice(MAIN, S)))
C_BIAS, C_LNW, C_LNB, C_BO, C_LN1, C_LN2, C_GATE, C_RT, C_IOTA, C_SEG, CWID = (
    0, 768, 800, 832, 1088, 1344, 1600, 1602, 1634, 1650, 1652)
PRIMED = 1
MASKED = -1.0e12

ORDER = {
    "pe": """
        e:gate.0 e:weight.0 3:turn_c 2:scores.0 e:down.0 e:up.0 2:maxima.0 3:project 1:turn
        2:exp.0 e:gate.1 2:scores.1 1:keys e:up.1 2:maxima.1 1:query e:weight.1 2:exp.1
        2:context.0 e:gate.2 2:scores.2 e:down.1 e:up.2 2:maxima.2 2:context.1 e:weight.2
        e:gate.3 e:down.2 2:exp.2 e:up.3 2:scores.3 e:weight.3 e:down.3 2:maxima.3 e:gate.4
        2:exp.3 2:context.2 e:weight.4 e:up.4 1:cat_q e:down.4 2:context.3 1:cat_k 3:turn_z
        """,
    "act": """
        e:gate.0 3:turn_c 1:x_hi 2:maxima.0 2:v_hi 1:turn 2:exp.0 e:m_hi.0 e:gate.1 2:p_hi.0
        2:maxima.1 1:square 2:exp.1 e:gate.2 2:p_hi.1 2:c_hi.0 e:m_hi.1 2:maxima.2 e:gate.3
        3:square e:m_hi.2 2:exp.2 2:p_hi.2 1:qk_hi 2:c_hi.1 2:maxima.3 e:gate.4 e:m_hi.3 2:exp.3
        2:p_hi.3 3:z_hi 2:c_hi.2 1:cat_q e:m_hi.4 1:cat_k 2:c_hi.3 3:turn_z
        """,
    "pool": """
        1:x_rs 1:y_cut 1:x_lo e:m_lo.0 2:p_lo.0 2:v_ones 2:p_lo.1 3:x_rs e:m_lo.1 e:m_lo.2
        2:p_lo.2 1:qk_lo 3:z_rs e:m_lo.3 2:p_lo.3 3:z_lo e:m_lo.4
        """,
    "dve": """
        1:stats 1:mean e:gate.0 2:max.0 1:x_norm 2:negate.0 e:up.0 e:weight.0 3:out 3:new_x
        2:v_lo 3:stats 2:max.1 e:gate.1 2:negate.1 1:v_row 1:k_row e:up.1 1:q_row e:weight.1
        2:c_sum.0 1:newton.0 1:newton.1 3:mean 2:c_over.0 1:newton.2 1:newton.3 2:max.2
        1:newton.4 1:newton.5 2:c_add.0 e:gate.2 1:newton.6 2:negate.2 1:newton.7 2:c_lo.0
        1:newton.8 e:up.2 2:c_sum.1 1:newton.9 1:newton.10 1:newton.11 e:weight.2 1:newton.12
        3:h0 2:c_over.1 1:qk_rs 2:c_add.1 1:qk_w 1:qk_b e:gate.3 2:max.3 2:negate.3 e:up.3
        e:weight.3 2:c_lo.1 2:c_sum.2 e:gate.4 2:c_over.2 3:z_norm 2:c_add.2 e:up.4 2:c_lo.2
        e:weight.4 2:c_sum.3 2:c_over.3 2:c_add.3 2:c_lo.3
        """,
}
ORDER_START = {
    "pe": """
        2:scores.0 2:maxima.0 3:turn_c 2:exp.0 3:project 2:scores.1 1:turn 2:maxima.1 1:keys
        2:context.0 2:exp.1 1:query 2:scores.2 2:context.1 2:maxima.2 2:exp.2 2:scores.3
        2:maxima.3 2:exp.3 2:context.2 1:cat_q 2:context.3 1:cat_k 3:turn_z
        """,
    "act": """
        2:v_hi w:cut.0 2:maxima.0 3:turn_c 1:x_hi 2:exp.0 w:cut.1 1:turn 2:p_hi.0 2:maxima.1
        w:cut.2 2:exp.1 1:square w:cut.3 2:p_hi.1 2:c_hi.0 w:cut.4 3:square 2:maxima.2 2:exp.2
        w:cut.5 2:p_hi.2 2:c_hi.1 1:qk_hi 2:maxima.3 w:cut.6 2:exp.3 2:p_hi.3 3:z_hi 2:c_hi.2
        1:cat_q w:cut.7 1:cat_k 2:c_hi.3 3:turn_z
        """,
    "pool": """
        2:v_ones 1:x_rs 1:x_lo 1:y_cut 2:p_lo.0 3:x_rs 2:p_lo.1 3:z_rs 2:p_lo.2 1:qk_lo 2:p_lo.3
        3:z_lo
        """,
    "dve": """
        1:stats 1:mean 2:max.0 2:negate.0 1:x_norm w:cut.0 2:v_lo 3:out 2:max.1 2:negate.1
        3:new_x w:cut.1 3:stats 1:v_row 3:mean 1:k_row 2:c_sum.0 w:cut.2 1:q_row 2:max.2
        2:c_over.0 1:newton.0 1:newton.1 2:negate.2 1:newton.2 2:c_add.0 1:newton.3 1:newton.4
        w:cut.3 1:newton.5 1:newton.6 2:c_lo.0 1:newton.7 1:newton.8 1:newton.9 1:newton.10 3:h0
        1:newton.11 w:cut.4 1:newton.12 2:c_sum.1 1:qk_rs 2:c_over.1 1:qk_w 2:c_add.1 1:qk_b
        2:max.3 2:negate.3 w:cut.5 3:z_norm 2:c_lo.1 2:c_sum.2 2:c_over.2 2:c_add.2 w:cut.6
        2:c_lo.2 2:c_sum.3 2:c_over.3 2:c_add.3 w:cut.7 2:c_lo.3
        """,
}


def build(nc, x, yT, wa, wall, cst, ident, identb, maskb, sel, out):
    assert WALL % UNITS == 0
    with ExitStack() as ctx:
        def sb(name, shape, dt):
            return ctx.enter_context(nc.sbuf_tensor(name, shape, dt))

        sems = {}

        def sem(name):
            if name not in sems:
                sems[name] = ctx.enter_context(nc.semaphore(name))
            return sems[name]

        primed = {"p_exp": "act", "pT_sb": "dve", "o_lo": "dve", "me_a": "dve", "me_b": "dve",
                  "me_v": "dve", "p_lo": "pool", "pT_ps": "pe", "op_ps": "pe", "me_lo": "pool",
                  "o_ps": "pe", "d_ps": "pe", "out_done": "sp", "xa_yl": "pool", "xa_kvp": "pe",
                  "xa_catp": "pe", "xa_ck": "act", "xa_sT": "pe", "xa_vl": "dve", "xa_pv": "pe",
                  "xa_e": "act", "xa_pl": "pool", "xa_mTp": "pe", "xa_cl": "dve", "xa_o": "dve",
                  "xa_cTp": "pe", "xb_tp": "pe", "xb_xT": "act"}

        def apart(eng):
            eng.sem_inc(sem("apart"), 1)

        def prime(eng, name):
            for s, by in primed.items():
                if by == name:
                    eng.sem_inc(sem(s), PRIMED)

        def seen(name, n):
            assert name in primed
            return sem(name), n + PRIMED

        whi = sb("whi", [P, WALL], F16)
        wlo = sb("wlo", [P, WALL], F16)
        wahi = sb("wahi", [P, WA], F16)
        walo = sb("walo", [P, WA], F16)
        cs = sb("cs", [P, CWID], F32)
        idn2 = sb("idn2", [P, 2 * P], F16)
        idb = sb("idb", [P, P], BF16)
        msk = sb("msk", [P, S], BF16)
        sl = sb("sl", [P, NC * P], F16)
        y_t = sb("y_t", [P, S], F32)
        x1 = sb("x1", [P, GB, D], F32)
        ysp = sb("ysp", [P, 4, S], F16)
        wT = sb("wT", [P, T], F16)
        sm = sb("sm", [P, 256], F32)
        gt = sb("gt", [P, 3], F32)
        mhalf = sb("mhalf", [P, GB], F32)
        grw = sb("grw", [P, 2, KC, NE], F16)
        ar = sb("ar", [P, 10016], F32)
        ps = ctx.enter_context(nc.psum_tensor("ps", [P, 8, 512], F32))

        idn, seg = idn2[:, 0:P], idn2[:, P:2 * P]

        def words(a, n):
            return ar[:, a:a + n]

        def halves(a, n):
            return ar[:, a:a + n].bitcast(F16)

        def bank16(b, n=1):
            return ps[:, b:b + n, :].rearrange("p b w -> p (b w)").bitcast(F16)

        def bank(b, n=1):
            return ps[:, b:b + n, :].rearrange("p b w -> p (b w)")

        XS, XP, XF = 0, 1, 2
        SB_, QB, KB, VB, TB, OB, AB = 0, 1, 2, 3, 4, 5, 6
        GBK, UBK, WBK = 3, 4, 5

        xTn = halves(0, 1024).rearrange("p (l k t) -> p l k t", l=2, k=KC)
        xT = halves(1024, 1024).rearrange("p (l k t) -> p l k t", l=2, k=KC)
        hid = words(2048, 1024).rearrange("p (j d) -> p j d", j=GB)
        me_t, me_p = words(3072, 512), words(3584, 512)
        me_hl = halves(4096, 512).rearrange("p (l t) -> p l t", l=2)
        stage = [words(1024, UW), words(1024 + UW, UW)]
        stage_a = words(1024, WA)
        assert 1024 + max(2 * UW, WA) <= 4608
        A0 = 4608
        qkT = halves(A0, 1024).rearrange("p (w l t) -> p w l t", w=2, l=2)
        vv = halves(A0 + 1024, 2048).rearrange("p (r l j c) -> p r l j c", r=2, l=2, j=GB)
        pr = words(A0 + 3072, 512).rearrange("p (j k) -> p j k", j=GB)
        phl = halves(A0 + 3584, 512).rearrange("p (l j k) -> p l j k", l=2, j=GB)
        pT = halves(A0 + 4096, 512).rearrange("p (l j k) -> p l j k", l=2, j=GB)
        oT = halves(A0 + 4608, 512).rearrange("p (l j k) -> p l j k", l=2, j=GB)
        wcat = halves(A0 + 2048, 256).rearrange("p (j c) -> p j c", j=GB)
        w_mu = words(A0 + 2048, 96)
        xr = words(A0, 1024).rearrange("p (j d) -> p j d", j=GB)
        xrs = halves(A0 + 1024, 1024).rearrange("p (l j d) -> p l j d", l=2, j=GB)
        xn = words(A0, 256)
        xs = halves(A0 + 256, 256).rearrange("p (l d) -> p l d", l=2)
        xsT = halves(A0 + 512, 256).rearrange("p (l k t) -> p l k t", l=2, k=KC)
        sq = words(A0, 512).rearrange("p (h d) -> p h d", d=XD)
        cat = halves(A0, 1024).rearrange("p (h a b d) -> p h a b d", a=2, b=2, d=XD)
        catf = halves(A0, 1024)
        qk = words(A0 + 1024, 512).rearrange("p (h d) -> p h d", d=XD)
        vf = words(A0 + 1536, 256)
        catT = halves(A0 + 1792, 1024).rearrange("p (w h t) -> p w h t", w=2, h=8)
        vs = halves(A0 + 2816, 544).rearrange("p (l h s c) -> p l h s c", l=2, h=XH, s=2)
        xp = words(A0 + 3360, 512)
        xpT = halves(A0 + 3872, 512).rearrange("p (l h q) -> p l h q", l=2, h=QH)
        shift = halves(A0 + 4384, 256)
        xc = halves(A0 + 4640, 256).rearrange("p (l d) -> p l d", l=2)
        xcT = halves(A0 + 4896, 256).rearrange("p (l k t) -> p l k t", l=2, k=KC)
        zs = halves(A0 + 4896, 256).rearrange("p (l d) -> p l d", l=2)
        zjunk = words(A0 + 4896, 256)
        z = words(A0 + 5152, 256)

        st4 = sm[:, 0:24].rearrange("p (j s) -> p j s", j=GB)
        mv4 = sm[:, 24:32].rearrange("p (j s) -> p j s", j=GB)
        ve4, rs4, ss4 = sm[:, 32:36], sm[:, 36:40], sm[:, 40:44]
        rve4, rrs4 = sm[:, 44:48], sm[:, 48:52]
        mx4, nm4, es4, er4, eq4 = (sm[:, 52 + 4 * n:56 + 4 * n] for n in range(5))
        a_st, a_mv, a_ve, a_rs = sm[:, 72:78], sm[:, 78:80], sm[:, 80:81], sm[:, 81:82]
        b_st, b_mv, b_ve, b_rs = sm[:, 82:88], sm[:, 88:90], sm[:, 90:91], sm[:, 91:92]
        b_ss, b_ve2, b_rs2 = sm[:, 92:93], sm[:, 93:94], sm[:, 94:95]
        a_ss, a_v, a_y, a_t = (sm[:, 96 + 32 * n:128 + 32 * n] for n in range(4))
        a_mx, a_r = (sm[:, 224 + 8 * n:232 + 8 * n].rearrange("p (h s) -> p h s", s=2)
                     for n in range(2))
        a_mn = sm[:, 240:244].bitcast(F16).rearrange("p (h s) -> p h s", s=2)
        ln_ps = sm[:, 244:245]
        rt = words(3072, 768)
        rt_l, rt_e, rt_p, rt_m, rt_w, rt_f = (
            rt[:, 64 * n:64 * n + 64].rearrange("p (j e) -> p j e", j=GB) for n in range(6))
        rt_8 = rt[:, 384:416].rearrange("p (j k) -> p j k", j=GB)
        rt_ix = rt[:, 416:448].bitcast(U32).rearrange("p (j k) -> p j k", j=GB)
        rt_xf = rt[:, 448:464].rearrange("p (j k) -> p j k", j=GB)
        rt_mx, rt_s, rt_r, rt_s2, rt_r2 = (rt[:, 464 + 4 * n:468 + 4 * n] for n in range(5))
        rt_eq = rt[:, 512:768].rearrange("p (j e k) -> p j e k", j=GB, e=NE)

        def context(l, q):
            return xc[:, l, :].rearrange("p (r b d) -> p r b d", b=2, d=XD)[
                :, 4 * (q // 2):4 * (q // 2) + 4, q % 2, :]

        def head_of(q, h):
            return 2 * (4 * (q // 2) + h) + q % 2

        ctx_ps = bank(XP)[:, 0:QH * 2 * (XD + 1)].rearrange("p (h s c) -> p h s c", h=QH, s=2)
        ctx_sum = bank(XP)[:, 256:256 + QH * XD].rearrange("p (h d) -> p h d", d=XD)

        def ln_rows(c):
            return cs[:, c:c + 32].rearrange("p (w d) -> p w d", w=2).unsqueeze(2).broadcast_to(
                [P, 2, XH, XD])

        def wcol(w, off, n=P):
            return w[:, bass.ds(off, n)]

        x_d = x.rearrange("b s d -> s b d")
        y_d = yT.rearrange("b k s -> k b s")
        out_d = out.rearrange("b s d -> s b d")

        def period(steps, order, b1, b2, b3, g, first, units):
            for word in order.split():
                name, _, number = word.partition(".")
                number = int(number or 0)
                step = steps[name]
                if name[0] == "1" and b1:
                    step(*b1, number) if name == "1:newton" else step(*b1)
                elif name[0] == "2" and b2:
                    step(*b2) if name in ("2:v_hi", "2:v_lo", "2:v_ones") else step(b2[0], number)
                elif name[0] == "3" and b3:
                    step(*b3, b2 is not None)
                elif name == "e:down" and g is not None:
                    if first + number > 0:
                        step(g, first + number - 1)
                elif name[0] == "e" and g is not None:
                    step(g, first + number)
                elif name[0] == "w" and units is not None:
                    step(units + number)

        def cross(engine, steps, g, chunks):
            base = (g + 1) * GB if chunks else 0
            order = (ORDER if chunks else ORDER_START)[engine]
            for p in range(PERIODS):
                b = [(base + q, q) if 0 <= q < GB else None for q in (p, p - 1, p - 2)]
                period(steps, order, *b, g if chunks else None, p * SLOTS,
                       p * UPP if not chunks and p < GB else None)
            if chunks:
                if "e:down" in steps:
                    steps["e:down"](g, NC - 1)
                if "e:finish" in steps:
                    steps["e:finish"](g)
            period(steps, order, None, None, (base + GB - 1, GB - 1), None, 0, None)

        def last_experts(eng, steps):
            g = NG - 1

            def chunk(c):
                for name in ("e:gate", "e:up", "e:weight", "e:down", "e:m_hi", "e:m_lo"):
                    if name in steps and name != "e:down":
                        steps[name](g, c)
                    elif name in steps and not (isinstance(c, int) and c == 0):
                        steps[name](g, c - 1)

            chunk(0)
            chunk(1)
            with eng.Fori(2, NC) as c:
                chunk(c)
            if "e:down" in steps:
                steps["e:down"](g, NC - 1)
            if "e:finish" in steps:
                steps["e:finish"](g)

        block = ctx.enter_context(nc.Block())

        @block.sync
        def _(sp):
            prime(sp, "sp")
            sp.dma_start(stage_a, wa).then_inc(sem("wa_in"), 16)
            sp.dma_start(cs[:, :], cst).then_inc(sem("const_in"), 16)
            sp.dma_start(idn2[:, :], ident).then_inc(sem("const_in"), 16)
            sp.dma_start(x1[:, :, :], x_d[:, 0:GB, :]).then_inc(sem("x_in"), 16)
            sp.dma_start(y_t[:, :], y_d[:, 0, :]).then_inc(sem("y_in"), 16)
            sp.dma_start(idb[:, :], identb).then_inc(sem("const_in"), 16)
            sp.dma_start(msk[:, :], maskb).then_inc(sem("const_in"), 16)
            sp.dma_start(sl[:, :], sel).then_inc(sem("const_in"), 16)
            for u in range(UNITS):
                sp.wait_ge(sem("stage_cut"), max(u, 1))
                sp.dma_start(stage[u % 2], wall[:, u * UW:(u + 1) * UW]).then_inc(
                    sem(f"stage_in{u % 2}"), 16)
                if u % UPP == UPP - 1 and u // UPP + 1 < GB:
                    b = u // UPP + 1
                    sp.wait_ge(*seen("xa_yl", b))
                    sp.dma_start(y_t[:, :], y_d[:, b, :]).then_inc(sem("y_in"), 16)
            with sp.Fori(0, NG - 1) as g:
                sp.wait_ge(sem("z"), g + 1)
                sp.dma_start(x1[:, :, :], x_d[:, bass.ds((g + 1) * GB, GB), :]).then_inc(sem("x_in"), 16)
                for q in range(GB):
                    sp.wait_ge(*seen("xa_yl", (g + 1) * GB + q))
                    sp.dma_start(y_t[:, :], y_d[:, bass.ds((g + 1) * GB + q, 1), :]
                                 .rearrange("p b d -> p (b d)")).then_inc(sem("y_in"), 16)
                sp.wait_ge(sem("fin"), g + 1)
                sp.dma_start(out_d[:, bass.ds(g * GB, GB), :], hid).then_inc(sem("out_done"), 16)
            sp.wait_ge(sem("fin"), NG)
            sp.dma_start(out_d[:, (NG - 1) * GB:NG * GB, :], hid).then_inc(sem("out_done"), 16)
            sp.wait_ge(*seen("out_done", 16 * NG))

        @block.tensor
        def _(pe):
            prime(pe, "pe")
            mm = nc.tensor.matmul

            def three(o, l_hi, l_lo, r_hi, r_lo, start, stop):
                mm(o, l_hi, r_hi, start=start, stop=False, skip_group_check=True)
                mm(o, l_hi, r_lo, start=False, stop=False, skip_group_check=True)
                return mm(o, l_lo, r_hi, start=False, stop=stop, skip_group_check=True)

            def turn_rows(b, rows):
                t = bank16(b)[:, 0:512].rearrange("p (l k t) -> p l k t", l=2, k=KC)
                for l in range(2):
                    for k in range(KC):
                        last = nc.tensor.transpose(t[:, l, k, :], rows[:, l, k * P:(k + 1) * P], idn)
                return last

            def x1_turn(i, j):
                pe.wait_ge(sem("xa_xl"), i + 1)
                pe.wait_ge(*seen("xa_ck", i))
                turn_rows(XF, xs).then_inc(sem("xa_xTp"), 1)

            def x1_keys(i, j):
                pe.wait_ge(sem("xa_xT"), i + 1)
                pe.wait_ge(*seen("xa_yl", i + 1))
                for n, w in enumerate((512, 1024)):
                    last = three(bank(XF), ysp[:, 2 * n, :], ysp[:, 2 * n + 1, :],
                                 wahi[:, w:w + 512], walo[:, w:w + 512], n == 0, n == 1)
                last.then_inc(sem("xa_kvp"), 1)

            def x1_query(i, j):
                pe.wait_ge(sem("xa_k"), i + 1)
                for k in range(KC):
                    last = three(bank(XF)[:, 0:D], xsT[:, 0, k, :], xsT[:, 1, k, :],
                                 wahi[:, k * D:(k + 1) * D], walo[:, k * D:(k + 1) * D],
                                 k == 0, k == KC - 1)
                last.then_inc(sem("xa_qp"), 1)

            def turn_cat(w):
                for n in range(8):
                    last = nc.tensor.transpose(bank16(XF)[:, n * P:(n + 1) * P],
                                               catf[:, (8 * w + n) * P:(8 * w + n + 1) * P], idn)
                return last

            def cat_q(i, j):
                pe.wait_ge(sem("xa_lo"), i + 1)
                turn_cat(0).then_inc(sem("xa_catq"), 1)

            def cat_k(i, j):
                pe.wait_ge(sem("xa_cq"), i + 1)
                turn_cat(1).then_inc(sem("xa_catp"), 1)

            def x2_scores(i, q):
                n = i * NQ + q
                if q == 0:
                    pe.wait_ge(sem("xa_cq"), i + 1)
                    pe.wait_ge(*seen("xa_ck", i + 1))
                    if not (isinstance(i, int) and i == 0):
                        pe.wait_ge(*seen("xb_xT", i - 1))
                pe.wait_ge(*seen("xa_e", n))
                r = slice(64 * (q % 2), 64 * (q % 2) + 64)
                for h in range(QH):
                    pair = 4 * (q // 2) + h
                    last = mm(bank(XS)[:, h * P:(h + 1) * P], catT[r, 0, pair, :], catT[r, 1, pair, :],
                              start=True, stop=True, skip_group_check=True)
                last.then_inc(sem("xa_s"), 1)

            def x2_maxima(i, q):
                pe.wait_ge(sem("xa_mn"), i * NQ + q + 1)
                for h in range(QH):
                    last = nc.tensor.transpose(bank16(XS)[0:2, h * P:(h + 1) * P], a_mn[:, h, :], idn)
                last.then_inc(sem("xa_mTp"), 1)

            def x2_exp(i, q):
                pe.wait_ge(sem("xa_mT"), i * NQ + q + 1)
                mm(bank(XS), seg, shift, start=True, stop=False, skip_group_check=True)
                r = slice(64 * (q % 2), 64 * (q % 2) + 64)
                for h in range(QH):
                    pair = 4 * (q // 2) + h
                    last = mm(bank(XS)[:, h * P:(h + 1) * P], catT[r, 1, pair, :], catT[r, 0, pair, :],
                              start=False, stop=h == QH - 1, skip_group_check=True)
                last.then_inc(sem("xa_sT"), 1)

            def x2_context(i, q):
                n = i * NQ + q
                pe.wait_ge(*seen("xa_pl", n + 1))
                if q == 0:
                    pe.wait_ge(*seen("xa_vl", i + 1))
                    pe.wait_ge(sem("xa_ones"), i + 1)
                    pe.wait_ge(*seen("xa_o", i))
                pe.wait_ge(*seen("xa_cl", n))
                for h in range(QH):
                    v_hi, v_lo = (vs[:, l, head_of(q, h)].rearrange("p s c -> p (s c)") for l in range(2))
                    last = three(ctx_ps[:, h].rearrange("p s c -> p (s c)"), xpT[:, 0, h, :],
                                 xpT[:, 1, h, :], v_hi, v_lo, True, True)
                last.then_inc(sem("xa_pv"), 1)

            def x3_turn_c(i, j, beside):
                pe.wait_ge(*seen("xa_cl", i * NQ + NQ))
                turn_rows(XP, xc).then_inc(sem("xa_cTp"), 1)

            def x3_project(i, j, beside):
                pe.wait_ge(sem("xa_cT"), i + 1)
                for k in range(KC):
                    w = slice(1536 + k * D, 1536 + (k + 1) * D)
                    last = three(bank(XP)[:, 0:D], xcT[:, 0, k, :], xcT[:, 1, k, :],
                                 wahi[:, w], walo[:, w], k == 0, k == KC - 1)
                last.then_inc(sem("xa_yp"), 1)

            def turn_z(i, j, beside):
                pe.wait_ge(sem("xb_zl"), i + 1)
                pe.wait_ge(*seen("xb_xT", i))
                if beside:
                    pe.wait_ge(*seen("xa_e", i * NQ + 2 * NQ))
                turn_rows(XS, zs).then_inc(sem("xb_tp"), 1)

            def gate_or_up(g, c, w, b, free, made):
                n = g * NC + c
                pe.wait_ge(*seen(free, n))
                for k in range(KC):
                    off = c * CW + (NH * HW + w * D + k * P)
                    last = three(bank(b), wcol(whi, off), wcol(wlo, off), xT[:, 0, k, :],
                                 xT[:, 1, k, :], k == 0, k == KC - 1)
                last.then_inc(sem(made), 1)

            def gate(g, c):
                gate_or_up(g, c, 0, GBK, "me_a", "g_ps")

            def up(g, c):
                gate_or_up(g, c, 1, UBK, "me_b", "u_ps")

            def weight(g, c):
                pe.wait_ge(*seen("me_v", g * NC + c))
                mm(bank(WBK), wcol(sl, c * P), wT[:, :], start=True, stop=True,
                   skip_group_check=True).then_inc(sem("w_ps"), 1)

            def down(g, c):
                n = g * NC + c
                first, end = isinstance(c, int) and c == 0, isinstance(c, int) and c == NC - 1
                pe.wait_ge(*seen("me_lo", n + 1))
                off = c * CW + (NH * HW + 2 * D)
                for j in range(GB):
                    o = bank(AB + j // 2)[:, (j % 2) * D:(j % 2 + 1) * D]
                    cc = slice(j * S, (j + 1) * S)
                    last = three(o, me_hl[:, 0, cc], me_hl[:, 1, cc], wcol(whi, off, D),
                                 wcol(wlo, off, D), first and j % 2 == 0, end and j % 2 == 1)
                last.then_inc(sem("d_ps"), 1)

            steps = {"1:turn": x1_turn, "1:keys": x1_keys, "1:query": x1_query, "1:cat_q": cat_q,
                     "1:cat_k": cat_k, "2:scores": x2_scores, "2:maxima": x2_maxima, "2:exp": x2_exp,
                     "2:context": x2_context, "3:turn_c": x3_turn_c, "3:project": x3_project,
                     "3:turn_z": turn_z, "e:gate": gate, "e:up": up, "e:weight": weight,
                     "e:down": down}

            def turn_x(n):
                pe.wait_ge(sem("rms_lo"), n)
                for l in range(2):
                    o = bank16(VB + l).rearrange("p (k j t) -> p k j t", k=KC, j=GB)
                    for k in range(KC):
                        for j in range(GB):
                            last = nc.tensor.transpose(o[:, k, j, :], xrs[:, l, j, k * P:(k + 1) * P],
                                                       idn)
                last.then_inc(sem("rms_tp"), 1)

            def project(w, wh):
                for k in range(KC):
                    off = wh + (w * D + k * P)
                    last = three(bank(QB + w), wcol(whi, off), wcol(wlo, off),
                                 xTn[:, 0, k, :], xTn[:, 1, k, :], k == 0, k == KC - 1)
                last.then_inc(sem("q_ps" if w == 0 else "k_ps"), 1)

            def values(wh, half):
                for jj in range(2):
                    j = 2 * half + jj
                    for k in range(KC):
                        def rv(w):
                            return w[:, bass.ds(wh + (2 * D + k * P), 2 * HW)].rearrange(
                                "p (h c) -> p h c", h=2)[:, :, 0:P]
                        last = three(bank(VB)[:, jj * 256:(jj + 1) * 256].rearrange("p (h c) -> p h c", h=2),
                                     xTn[:, 0, k, j * S:(j + 1) * S], xTn[:, 1, k, j * S:(j + 1) * S],
                                     rv(whi), rv(wlo), jj == 0 and k == 0, jj == 1 and k == KC - 1)
                last.then_inc(sem("v_ps"), 1)

            def scores(it):
                pe.wait_ge(sem("q_lo"), it + 1)
                pe.wait_ge(sem("k_lo"), it + 1)
                pe.wait_ge(*seen("p_exp", it))
                mm(bank(SB_).rearrange("p (j k) -> p j k", j=GB), idb[:, :],
                   msk[:, :].unsqueeze(1).broadcast_to([P, GB, S]), start=True, stop=False,
                   skip_group_check=True)
                for j in range(GB):
                    c = slice(j * S, (j + 1) * S)
                    last = three(bank(SB_)[:, c], qkT[:, 0, 0, c], qkT[:, 0, 1, c],
                                 qkT[:, 1, 0, c], qkT[:, 1, 1, c], False, j == GB - 1)
                last.then_inc(sem("s_ps"), 1)

            def turn_p(it):
                pe.wait_ge(*seen("p_lo", it + 1))
                pe.wait_ge(*seen("pT_sb", it))
                o = bank16(TB).rearrange("p (l j k) -> p l j k", l=2, j=GB)
                for l in range(2):
                    for j in range(GB):
                        last = nc.tensor.transpose(o[:, l, j, :], phl[:, l, j, :], idn)
                last.then_inc(sem("pT_ps"), 1)

            def attend(it, par, odd):
                pe.wait_ge(*seen("pT_sb", it + 1))
                pe.wait_ge(*seen("o_lo", it))
                for j in range(GB):
                    c = slice(odd * P, odd * P + P)
                    last = three(bank(OB)[:, j * S:(j + 1) * S], vv[:, par, 0, j, c], vv[:, par, 1, j, c],
                                 pT[:, 0, j, :], pT[:, 1, j, :], j == 0, j == GB - 1)
                last.then_inc(sem("o_ps"), 1)

            def out_project(it, wh, first, end):
                pe.wait_ge(*seen("o_lo", it + 1))
                for j in range(GB):
                    o = bank(AB + j // 2)[:, (j % 2) * D:(j % 2 + 1) * D]
                    last = three(o, oT[:, 0, j, :], oT[:, 1, j, :], wcol(whi, wh + 3 * D, D),
                                 wcol(wlo, wh + 3 * D, D), first and j % 2 == 0, end and j % 2 == 1)
                last.then_inc(sem("op_ps"), 1)

            def head(g, h, hm, first=False, second=False, last2=0):
                it = g * NH + h
                scores(it)
                if last2 != 2:
                    project(0, (h + 1) * HW)
                if not first:
                    turn_p(it - 1)
                if last2 != 2:
                    project(1, (h + 1) * HW)
                if not first:
                    attend(it - 1, ((hm - 1) % 4) // 2, (hm - 1) % 2)
                if not last2:
                    pe.wait_ge(sem("v_lo"), it + 2)
                    values((h - hm % 2 + 2) * HW, hm % 2)
                if not first:
                    out_project(it - 1, (h - 1) * HW, second, False)

            def attention(g):
                pe.wait_ge(*seen("xb_xT", g * GB + GB))
                project(0, 0)
                project(1, 0)
                values(0, 0)
                pe.wait_ge(sem("v_lo"), g * NH + 1)
                values(0, 1)
                head(g, 0, 0, first=True)
                head(g, 1, 1, second=True)
                with pe.Fori(0, 3) as t:
                    for u in range(4):
                        head(g, t * 4 + (2 + u), (2 + u) % 4)
                head(g, 14, 2, last2=1)
                head(g, 15, 3, last2=2)
                turn_p(g * NH + 15)
                attend(g * NH + 15, 1, 1)
                out_project(g * NH + 15, 15 * HW, False, True)

            def router(g):
                turn_x(g + 1)
                pe.wait_ge(sem("rms_xT"), g + 1)
                for j in range(GB):
                    for k in range(KC):
                        xh, xl = (xT[:, l, k, j * S:(j + 1) * S] for l in range(2))
                        three(bank(OB)[:, j * NE:(j + 1) * NE], xh, xl, grw[:, 0, k, :], grw[:, 1, k, :],
                              k == 0, False)
                        last = mm(bank(OB)[:, j * NE:(j + 1) * NE], xl, grw[:, 1, k, :], start=False,
                                  stop=k == KC - 1, skip_group_check=True)
                last.then_inc(sem("rt_ps"), 1)
                pe.wait_ge(sem("rt_cat"), g + 1)
                for j in range(GB):
                    last = nc.tensor.transpose(bank16(OB)[:, j * P:(j + 1) * P], wcat[:, j, :], idn)
                last.then_inc(sem("wT_ps"), 1)
                pe.wait_ge(sem("wT_sb"), g + 1)

            pe.wait_ge(sem("const_in"), 80)
            pe.wait_ge(sem("stage_cut"), 1)
            cross("pe", steps, 0, False)
            pe.wait_ge(sem("stage_cut"), UNITS + 1)
            with pe.Fori(0, NG - 1) as g:
                attention(g)
                router(g)
                cross("pe", steps, g, True)
            attention(NG - 1)
            router(NG - 1)
            last_experts(pe, steps)

        @block.scalar
        def _(act):
            prime(act, "act")
            A = nc.scalar.activation

            def x1_norm(i, j):
                act.wait_ge(sem("xa_xn"), i + 1)
                A(xs[:, 0, :], xn, ACT.Copy).then_inc(sem("xa_xh"), 1)

            def x1_turn(i, j):
                act.wait_ge(sem("xa_xTp"), i + 1)
                A(xsT.rearrange("p l k t -> p (l k t)"), bank16(XF)[:, 0:512], ACT.Copy).then_inc(
                    sem("xa_xT"), 1)

            def x1_square(i, j):
                act.wait_ge(sem("xa_qk"), i + 1)
                A(sq, qk, ACT.Square).then_inc(sem("xa_sq"), 1)

            def x1_hi(i, j):
                act.wait_ge(sem("xa_n"), i + 1)
                A(cat[:, 0:16, 0, :, :], qk[:, 0:16, :].unsqueeze(2).broadcast_to([P, 16, 2, XD]), ACT.Copy)
                A(cat[:, 16:32, :, 0, :], qk[:, 16:32, :].unsqueeze(2).broadcast_to([P, 16, 2, XD]),
                  ACT.Copy).then_inc(sem("xa_hi"), 1)

            def cat_q(i, j):
                act.wait_ge(sem("xa_catq"), i + 1)
                act.wait_ge(*seen("xa_sT", i * NQ))
                A(catT[:, 0].rearrange("p h t -> p (h t)"), bank16(XF), ACT.Copy).then_inc(
                    sem("xa_cq"), 1)

            def cat_k(i, j):
                act.wait_ge(*seen("xa_catp", i + 1))
                A(catT[:, 1].rearrange("p h t -> p (h t)"), bank16(XF), ACT.Copy).then_inc(
                    sem("xa_ck"), 1)

            def x2_values(i, j):
                act.wait_ge(sem("xa_v"), i + 1)
                act.wait_ge(*seen("xa_pv", i * NQ))
                for s in range(2):
                    last = A(vs[:, 0, :, s, 0:XD], vf.rearrange("p (h d) -> p h d", d=XD), ACT.Copy,
                             scale=cs[:, C_SEG + s:C_SEG + s + 1])
                last.then_inc(sem("xa_vh"), 1)

            def x2_maxima(i, q):
                act.wait_ge(*seen("xa_mTp", i * NQ + q + 1))
                act.wait_ge(*seen("xa_sT", i * NQ + q))
                A(shift[0:2, :], bank16(XS)[0:2, 0:512], ACT.Copy).then_inc(sem("xa_mT"), 1)

            def x2_exp(i, q):
                n = i * NQ + q
                act.wait_ge(*seen("xa_sT", n + 1))
                act.wait_ge(*seen("xa_pl", n))
                A(xp, bank(XS), ACT.Exp, bias=ln_ps, scale=XD ** -0.5).then_inc(sem("xa_e"), 1)

            def p_hi(i, q):
                n = i * NQ + q
                act.wait_ge(*seen("xa_e", n + 1))
                act.wait_ge(*seen("xa_pv", n))
                A(xpT[:, 0].rearrange("p h q -> p (h q)"), xp, ACT.Copy).then_inc(sem("xa_ph"), 1)

            def x2_context(i, q):
                act.wait_ge(sem("xa_c"), i * NQ + q + 1)
                if q == 0:
                    act.wait_ge(*seen("xa_cTp", i))
                A(context(0, q), ctx_sum, ACT.Copy).then_inc(sem("xa_ch"), 1)

            def x3_turn_c(i, j, beside):
                act.wait_ge(*seen("xa_cTp", i + 1))
                act.wait_ge(*seen("xb_tp", i))
                A(xcT.rearrange("p l k t -> p (l k t)"), bank16(XP)[:, 0:512], ACT.Copy).then_inc(
                    sem("xa_cT"), 1)

            def x3_h0(i, j, beside):
                act.wait_ge(sem("xb_z"), i + 1)
                A(zjunk, z, ACT.Square, accum_out=b_ss).then_inc(sem("xb_ss"), 1)

            def x3_split(i, j, beside):
                act.wait_ge(sem("xb_zr"), i + 1)
                A(zs[:, 0, :], z, ACT.Copy).then_inc(sem("xb_zh"), 1)

            def turn_z(i, j, beside):
                act.wait_ge(*seen("xb_tp", i + 1))
                A(xTn[:, :, :, j * S:(j + 1) * S],
                  bank16(XS)[:, 0:512].rearrange("p (l k t) -> p l k t", l=2, k=KC), ACT.Copy).then_inc(
                    sem("xb_xT"), 1)

            def gate(g, c):
                n = g * NC + c
                act.wait_ge(sem("g_ps"), n + 1)
                act.wait_ge(*seen("me_v", n))
                A(me_t, bank(GBK), ACT.Tanh, scale=0.5 / WS).then_inc(sem("me_t"), 1)

            def cut(g, c):
                n = g * NC + c
                act.wait_ge(*seen("me_v", n + 1))
                act.wait_ge(*seen("d_ps", n))
                A(me_hl[:, 0, :], me_p, ACT.Copy).then_inc(sem("me_hi"), 1)

            def cut_unit(u):
                act.wait_ge(sem(f"stage_in{u % 2}"), 16 * (u // 2 + 1))
                A(whi[:, u * UW:(u + 1) * UW], stage[u % 2], ACT.Copy, scale=WS).then_inc(
                    sem("stage_hi"), 1)

            steps = {"1:x_hi": x1_norm, "1:turn": x1_turn, "1:square": x1_square, "1:qk_hi": x1_hi,
                     "1:cat_q": cat_q, "1:cat_k": cat_k, "2:v_hi": x2_values, "2:maxima": x2_maxima,
                     "2:exp": x2_exp, "2:p_hi": p_hi, "2:c_hi": x2_context, "3:turn_c": x3_turn_c,
                     "3:square": x3_h0, "3:z_hi": x3_split, "3:turn_z": turn_z, "e:gate": gate,
                     "e:m_hi": cut, "w:cut": cut_unit}

            def hi_q(w, it):
                act.wait_ge(sem(("q_ps", "k_ps")[w]), it + 1)
                A(qkT[:, w, 0, :], bank(QB + w), ACT.Copy, scale=1.0 / WS).then_inc(
                    sem(("q_hi", "k_hi")[w]), 1)

            def hi_v(cnt, par, half):
                act.wait_ge(sem("v_ps"), cnt)
                A(vv[:, par, 0, 2 * half:2 * half + 2, :].rearrange("p j c -> p (j c)"), bank(VB),
                  ACT.Copy, scale=1.0 / WS).then_inc(sem("v_hi"), 1)

            def hi_o(it):
                act.wait_ge(*seen("o_ps", it + 1))
                act.wait_ge(*seen("op_ps", it))
                A(oT[:, 0].rearrange("p j k -> p (j k)"), bank(OB), ACT.Copy,
                  scale=1.0 / PS).then_inc(sem("o_hi"), 1)

            def head(g, h, hm, first=False, last2=0):
                it = g * NH + h
                act.wait_ge(sem("m_neg"), it + 1)
                act.wait_ge(*seen("p_lo", it))
                for j in range(GB):
                    last = A(pr[:, j, :], bank(SB_)[:, j * S:(j + 1) * S], ACT.Exp,
                             bias=nm4[:, j:j + 1], scale=QHD ** -0.5, accum_out=es4[:, j:j + 1])
                last.then_inc(sem("p_exp"), 1)
                if last2 != 2:
                    hi_q(0, it + 1)
                    hi_q(1, it + 1)
                if not first:
                    hi_o(it - 1)
                if not last2:
                    hi_v(it + 3, ((hm + 2) % 4) // 2, hm % 2)
                act.wait_ge(sem("p_n"), it + 1)
                act.wait_ge(*seen("pT_ps", it))
                A(phl[:, 0], pr, ACT.Copy).then_inc(sem("p_hi"), 1)

            def attention(g):
                hi_q(0, g * NH)
                hi_q(1, g * NH)
                hi_v(g * NH + 1, 0, 0)
                hi_v(g * NH + 2, 0, 1)
                head(g, 0, 0, first=True)
                head(g, 1, 1)
                with act.Fori(0, 3) as t:
                    for u in range(4):
                        head(g, t * 4 + (2 + u), (2 + u) % 4)
                head(g, 14, 2, last2=1)
                head(g, 15, 3, last2=2)
                hi_o(g * NH + 15)

            def router(g):
                act.wait_ge(sem("hid"), g + 1)
                for j in range(GB):
                    last = A(xr[:, j, :], hid[:, j, :], ACT.Square, accum_out=ss4[:, j:j + 1])
                last.then_inc(sem("rms_ss"), 1)
                act.wait_ge(sem("rms_xr"), g + 1)
                A(xrs[:, 0], xr, ACT.Copy).then_inc(sem("rms_hi"), 1)
                act.wait_ge(sem("rt_sub"), g + 1)
                A(rt_e, rt_l, ACT.Exp, scale=1.0 / WS).then_inc(sem("rt_exp"), 1)

            act.wait_ge(sem("const_in"), 80)
            A(gt[:, 0:2], cs[:, C_GATE:C_GATE + 2], ACT.Tanh).then_inc(sem("gates"), 1)
            A(grw[:, 0].rearrange("p k e -> p (k e)"), cs[:, C_RT:C_RT + KC * NE], ACT.Copy,
              scale=WS).then_inc(sem("gr_hi"), 1)
            act.wait_ge(sem("gates"), 1)
            A(gt[:, 2:3], gt[:, 1:2], ACT.Copy, scale=1.0 / WS).then_inc(sem("gates"), 1)
            act.wait_ge(sem("centred"), 3)
            A(wahi[:, :], stage_a, ACT.Copy, scale=WS).then_inc(sem("wa_hi"), 1)
            cross("act", steps, 0, False)
            with act.Fori(0, NG - 1) as g:
                attention(g)
                router(g)
                cross("act", steps, g, True)
            attention(NG - 1)
            router(NG - 1)
            last_experts(act, steps)

        @block.gpsimd
        def _(pool):
            prime(pool, "pool")
            TT = nc.gpsimd.tensor_tensor

            def rsqrt(out, tmp, in_, scale, eps, w, name, count):
                nc.gpsimd.tensor_scalar(tmp, in_, scale, eps, ALU.mult, ALU.add).then_inc(
                    sem(name + "_ve"), 1)
                pool.wait_ge(sem(name + "_ve"), count)
                TT(out, tmp, mhalf[:, 0:w], ALU.pow).then_inc(sem(name + "_rs"), 1)

            def x1_stats(i, j):
                pool.wait_ge(sem("xa_mv"), i + 1)
                apart(pool)
                rsqrt(a_rs, a_ve, a_mv[:, 1:2], 1.0, 1e-5, 1, "xa", i + 1)
                if j == 0:
                    nc.gpsimd.memset(shift, 0.0)

            def y_cut(i, j):
                pool.wait_ge(sem("y_in"), i * 16 + 16)
                pool.wait_ge(*seen("xa_kvp", i))
                apart(pool)
                nc.gpsimd.tensor_copy(ysp[:, 0, 0:MAIN], y_t[:, 0:MAIN])
                nc.gpsimd.tensor_copy(ysp[:, 2, MAIN:S], y_t[:, MAIN:S]).then_inc(sem("xa_yh"), 1)
                pool.wait_ge(sem("xa_yh"), i + 1)
                TT(ysp[:, 1, 0:MAIN], y_t[:, 0:MAIN], ysp[:, 0, 0:MAIN], ALU.subtract)
                TT(ysp[:, 3, MAIN:S], y_t[:, MAIN:S], ysp[:, 2, MAIN:S],
                   ALU.subtract).then_inc(sem("xa_yl"), 1)

            def x1_turn(i, j):
                pool.wait_ge(sem("xa_xh"), i + 1)
                TT(xs[:, 1, :], xn, xs[:, 0, :], ALU.subtract).then_inc(sem("xa_xl"), 1)

            def x1_hi(i, j):
                pool.wait_ge(sem("xa_hi"), i + 1)
                TT(cat[:, 0:16, 1, :, :], qk[:, 0:16, :].unsqueeze(2).broadcast_to([P, 16, 2, XD]),
                   cat[:, 0:16, 0, :, :], ALU.subtract)
                TT(cat[:, 16:32, :, 1, :], qk[:, 16:32, :].unsqueeze(2).broadcast_to([P, 16, 2, XD]),
                   cat[:, 16:32, :, 0, :], ALU.subtract).then_inc(sem("xa_lo"), 1)

            def x2_values(i, j):
                pool.wait_ge(*seen("xa_pv", i * NQ))
                apart(pool)
                for s in range(2):
                    nc.gpsimd.tensor_copy(vs[:, 0, :, s, XD:XD + 1],
                                          cs[:, C_SEG + s:C_SEG + s + 1].unsqueeze(1)
                                          .broadcast_to([P, XH, 1]))
                nc.gpsimd.memset(vs[:, 1, :, :, XD:XD + 1], 0.0).then_inc(sem("xa_ones"), 1)

            def x2_exp(i, q):
                pool.wait_ge(sem("xa_ph"), i * NQ + q + 1)
                TT(xpT[:, 1].rearrange("p h q -> p (h q)"), xp, xpT[:, 0].rearrange("p h q -> p (h q)"),
                   ALU.subtract).then_inc(sem("xa_pl"), 1)

            def x3_stats(i, j, beside):
                pool.wait_ge(sem("xb_mv"), i + 1)
                apart(pool)
                rsqrt(rs4[:, j:j + 1], b_ve, mv4[:, j, 1:2], 1.0, 1e-5, 1, "xb", i + 1)

            def x3_rms(i, j, beside):
                pool.wait_ge(sem("xb_ss"), i + 1)
                apart(pool)
                rsqrt(b_rs2, b_ve2, b_ss, 1.0 / D, 1e-6, 1, "xb_r", i + 1)

            def x3_split(i, j, beside):
                pool.wait_ge(sem("xb_zh"), i + 1)
                TT(zs[:, 1, :], z, zs[:, 0, :], ALU.subtract).then_inc(sem("xb_zl"), 1)

            def cut(g, c):
                pool.wait_ge(sem("me_hi"), g * NC + c + 1)
                TT(me_hl[:, 1, :], me_p, me_hl[:, 0, :], ALU.subtract).then_inc(sem("me_lo"), 1)

            steps = {"1:x_rs": x1_stats, "1:y_cut": y_cut, "1:x_lo": x1_turn, "1:qk_lo": x1_hi,
                     "2:v_ones": x2_values, "2:p_lo": x2_exp, "3:x_rs": x3_stats, "3:z_rs": x3_rms,
                     "3:z_lo": x3_split, "e:m_lo": cut}

            def attention(g):
                with pool.Fori(0, NH) as h:
                    it = g * NH + h
                    pool.wait_ge(sem("p_r"), it + 1)
                    TT(pr, pr, eq4.unsqueeze(2).broadcast_to([P, GB, S]), ALU.mult).then_inc(
                        sem("p_n"), 1)
                    pool.wait_ge(sem("p_hi"), it + 1)
                    TT(phl[:, 1], pr, phl[:, 0], ALU.subtract).then_inc(sem("p_lo"), 1)

            def router(g):
                pool.wait_ge(sem("rms_ss"), g + 1)
                apart(pool)
                rsqrt(rrs4, rve4, ss4, 1.0 / D, 1e-6, 4, "rms", g + 1)
                nc.gpsimd.memset(wcat, 0.0).then_inc(sem("zeroed"), 1)
                pool.wait_ge(sem("zeroed"), g + 1)
                apart(pool)
                nc.gpsimd.memset(wcat[:, :, NE:NE + 1], 1.0).then_inc(sem("one_set"), 1)
                pool.wait_ge(sem("rms_hi"), g + 1)
                TT(xrs[:, 1], xr, xrs[:, 0], ALU.subtract).then_inc(sem("rms_lo"), 1)

            nc.gpsimd.memset(ln_ps, float(np.log(PS))).then_inc(sem("half_set"), 1)
            nc.gpsimd.memset(mhalf[:, :], -0.5).then_inc(sem("half_set"), 1)
            nc.gpsimd.memset(ysp[:, :, :], 0.0).then_inc(sem("half_set"), 1)
            pool.wait_ge(sem("half_set"), 3)
            pool.wait_ge(sem("const_in"), 80)
            cross("pool", steps, 0, False)
            with pool.Fori(0, NG - 1) as g:
                attention(g)
                router(g)
                cross("pool", steps, g, True)
            attention(NG - 1)
            router(NG - 1)
            last_experts(pool, steps)

        @block.vector
        def _(dve):
            prime(dve, "dve")
            V = nc.vector
            STT, TT = V.scalar_tensor_tensor, V.tensor_tensor
            qkf = qk.rearrange("p h d -> p (h d)")

            def x1_stats(i, j):
                if j == 0:
                    dve.wait_ge(sem("x_in"), i * 4 + 16)
                V.bn_stats(a_st, x1[:, j, :]).then_inc(sem("xa_st"), 1)

            def x_mean(i, j):
                dve.wait_ge(sem("xa_st"), i + 1)
                apart(dve)
                V.bn_aggr(a_mv, a_st).then_inc(sem("xa_mv"), 1)

            def x1_norm(i, j):
                dve.wait_ge(sem("xa_rs"), i + 1)
                dve.wait_ge(*seen("xa_catp", i))
                V.tensor_scalar(xn, x1[:, j, :], a_mv[:, 0:1], a_rs, ALU.subtract, ALU.mult).then_inc(
                    sem("xa_xn"), 1)

            def x1_query(i, j):
                dve.wait_ge(*seen("xa_kvp", i + 1))
                dve.wait_ge(*seen("xa_vl", i))
                STT(vf, bank(XF)[:, 256:512], 1.0 / WS, cs[:, 512:768], ALU.mult, ALU.add).then_inc(
                    sem("xa_v"), 1)

            def k_row(i, j):
                dve.wait_ge(*seen("xa_kvp", i + 1))
                dve.wait_ge(sem("xa_v"), i + 1)
                STT(qkf[:, 256:512], bank(XF)[:, 0:256], 1.0 / WS, cs[:, 256:512], ALU.mult,
                    ALU.add).then_inc(sem("xa_k"), 1)

            def x1_square(i, j):
                dve.wait_ge(sem("xa_qp"), i + 1)
                STT(qkf[:, 0:256], bank(XF)[:, 0:256], 1.0 / WS, cs[:, 0:256], ALU.mult,
                    ALU.add).then_inc(sem("xa_qk"), 1)

            def newton(i, j, step):
                yi, vi = a_y.bitcast(I32), a_v.bitcast(I32)
                if step == 0:
                    dve.wait_ge(sem("xa_sq"), i + 1)
                else:
                    dve.wait_ge(sem("xa_nt"), i * NEWTON + step)
                if step == 0:
                    made = V.tensor_reduce(a_ss, sq, AX.X, ALU.add)
                elif step == 1:
                    made = V.tensor_scalar(a_v, a_ss, 1.0 / XD, 1e-6, ALU.mult, ALU.add)
                elif step == 2:
                    made = V.tensor_scalar(yi, vi, 1, None, ALU.arith_shift_right)
                elif step == 3:
                    made = V.tensor_scalar(yi, yi, -1, 0x5f3759df, ALU.mult, ALU.add)
                elif step % 3 == 1:
                    made = TT(a_t, a_y, a_y, ALU.mult)
                elif step % 3 == 2:
                    made = STT(a_t, a_t, -0.5, a_v, ALU.mult, ALU.mult)
                else:
                    made = STT(a_y, a_t, 1.5, a_y, ALU.add, ALU.mult)
                made.then_inc(sem("xa_nt"), 1)

            def x1_scale(i, j):
                dve.wait_ge(sem("xa_nt"), i * NEWTON + NEWTON)
                TT(qk, qk, a_y.unsqueeze(2).broadcast_to([P, 32, XD]), ALU.mult).then_inc(sem("xa_n1"), 1)

            qk2 = qk.rearrange("p (w h) d -> p w h d", w=2)

            def qk_w(i, j):
                dve.wait_ge(sem("xa_n1"), i + 1)
                TT(qk2, qk2, ln_rows(C_LNW), ALU.mult).then_inc(sem("xa_n2"), 1)

            def qk_b(i, j):
                dve.wait_ge(sem("xa_n2"), i + 1)
                TT(qk2, qk2, ln_rows(C_LNB), ALU.add).then_inc(sem("xa_n"), 1)

            def x2_scores(i, q):
                n = i * NQ + q
                sc = bank(XS).rearrange("p (h k) -> p h k", h=QH)
                dve.wait_ge(sem("xa_s"), n + 1)
                for s, k in SEGS:
                    last = V.tensor_reduce(a_mx[:, :, s], sc[:, :, k], AX.X, ALU.max)
                last.then_inc(sem("xa_mx"), 1)

            def negate(i, q):
                n = i * NQ + q
                dve.wait_ge(sem("xa_mx"), n + 1)
                dve.wait_ge(*seen("xa_mTp", n))
                V.tensor_scalar(a_mn, a_mx, -1.0, None, ALU.mult).then_inc(sem("xa_mn"), 1)

            def x2_values(i, j):
                dve.wait_ge(sem("xa_vh"), i + 1)
                for s in range(2):
                    last = STT(vs[:, 1, :, s, 0:XD], vf.rearrange("p (h d) -> p h d", d=XD),
                               cs[:, C_SEG + s:C_SEG + s + 1], vs[:, 0, :, s, 0:XD], ALU.mult,
                               ALU.subtract)
                last.then_inc(sem("xa_vl"), 1)

            def x2_context(i, q):
                n = i * NQ + q
                dve.wait_ge(*seen("xa_pv", n + 1))
                V.reciprocal(a_r, ctx_ps[:, :, :, XD]).then_inc(sem("xa_r"), 1)

            def c_over(i, q):
                n = i * NQ + q
                dve.wait_ge(sem("xa_r"), n + 1)
                TT(ctx_ps[:, :, :, 0:XD], ctx_ps[:, :, :, 0:XD],
                   a_r.unsqueeze(3).broadcast_to([P, QH, 2, XD]), ALU.mult).then_inc(sem("xa_t"), 1)

            def c_add(i, q):
                n = i * NQ + q
                dve.wait_ge(sem("xa_t"), n + 1)
                V.tensor_reduce(ctx_sum, ctx_ps[:, :, :, 0:XD].rearrange("p h s c -> p h c s"), AX.X,
                                ALU.add).then_inc(sem("xa_c"), 1)

            def c_lo(i, q):
                n = i * NQ + q
                dve.wait_ge(sem("xa_ch"), n + 1)
                TT(context(1, q), ctx_sum, context(0, q), ALU.subtract).then_inc(
                    sem("xa_cl"), 1)

            def x3_x1(i, j, beside):
                dve.wait_ge(sem("xa_yp"), i + 1)
                dve.wait_ge(*seen("xb_tp", i))
                STT(z, bank(XP)[:, 0:D], 1.0 / WS, cs[:, C_BO:C_BO + D], ALU.mult, ALU.add).then_inc(
                    sem("xa_o"), 1)

            def new_x(i, j, beside):
                dve.wait_ge(*seen("xa_o", i + 1))
                STT(x1[:, j, :], z, gt[:, 0:1], x1[:, j, :], ALU.mult, ALU.add).then_inc(sem("xa_x1"), 1)

            def x3_stats(i, j, beside):
                dve.wait_ge(sem("xa_x1"), i + 1)
                V.bn_stats(st4[:, j, :], x1[:, j, :]).then_inc(sem("xb_st"), 1)

            def z_mean(i, j, beside):
                dve.wait_ge(sem("xb_st"), i + 1)
                apart(dve)
                V.bn_aggr(mv4[:, j, :], st4[:, j, :]).then_inc(sem("xb_mv"), 1)

            def x3_h0(i, j, beside):
                dve.wait_ge(sem("xb_rs"), i + 1)
                V.tensor_scalar(z, x1[:, j, :], mv4[:, j, 0:1], rs4[:, j:j + 1], ALU.subtract,
                                ALU.mult).then_inc(sem("xb_z"), 1)

            def x3_rms(i, j, beside):
                dve.wait_ge(sem("xb_r_rs"), i + 1)
                STT(z, z, b_rs2, cs[:, C_LN1:C_LN1 + D], ALU.mult, ALU.mult).then_inc(sem("xb_zr"), 1)

            def gate(g, c):
                dve.wait_ge(sem("me_t"), g * NC + c + 1)
                STT(me_t, me_t, 1.0, bank(GBK), ALU.add, ALU.mult).then_inc(sem("me_a"), 1)

            def up(g, c):
                n = g * NC + c
                dve.wait_ge(sem("u_ps"), n + 1)
                dve.wait_ge(*seen("me_a", n + 1))
                TT(me_t, me_t, bank(UBK), ALU.mult).then_inc(sem("me_b"), 1)

            def weight(g, c):
                n = g * NC + c
                dve.wait_ge(sem("w_ps"), n + 1)
                dve.wait_ge(*seen("me_b", n + 1))
                dve.wait_ge(*seen("me_lo", n))
                TT(me_p, me_t, bank(WBK), ALU.mult).then_inc(sem("me_v"), 1)

            hf = hid.rearrange("p j d -> p (j d)")

            def finish(g):
                dve.wait_ge(*seen("d_ps", g * NC + NC))
                dve.wait_ge(sem("z"), g + 1)
                STT(hf, bank(AB, 2), gt[:, 2:3], hf, ALU.mult, ALU.add).then_inc(sem("fin"), 1)

            def cut_unit(u):
                dve.wait_ge(sem("stage_hi"), u + 1)
                c = slice(u * UW, (u + 1) * UW)
                STT(wlo[:, c], stage[u % 2], WS, whi[:, c], ALU.mult, ALU.subtract).then_inc(
                    sem("stage_cut"), 1)

            steps = {"1:stats": x1_stats, "1:mean": x_mean, "1:x_norm": x1_norm, "1:v_row": x1_query,
                     "1:k_row": k_row, "1:q_row": x1_square, "1:newton": newton, "1:qk_rs": x1_scale,
                     "1:qk_w": qk_w, "1:qk_b": qk_b, "2:max": x2_scores, "2:negate": negate,
                     "2:v_lo": x2_values, "2:c_sum": x2_context, "2:c_over": c_over, "2:c_add": c_add,
                     "2:c_lo": c_lo, "3:out": x3_x1, "3:new_x": new_x, "3:stats": x3_stats,
                     "3:mean": z_mean, "3:h0": x3_h0, "3:z_norm": x3_rms, "e:gate": gate, "e:up": up,
                     "e:weight": weight, "e:finish": finish, "w:cut": cut_unit}

            def lo_q(w, it):
                dve.wait_ge(sem(("q_hi", "k_hi")[w]), it + 1)
                STT(qkT[:, w, 1, :], bank(QB + w), 1.0 / WS, qkT[:, w, 0, :], ALU.mult,
                    ALU.subtract).then_inc(sem(("q_lo", "k_lo")[w]), 1)

            def lo_v(cnt, par, half):
                dve.wait_ge(sem("v_hi"), cnt)
                js = slice(2 * half, 2 * half + 2)
                STT(vv[:, par, 1, js, :].rearrange("p j c -> p (j c)"), bank(VB), 1.0 / WS,
                    vv[:, par, 0, js, :].rearrange("p j c -> p (j c)"), ALU.mult,
                    ALU.subtract).then_inc(sem("v_lo"), 1)

            def copy_pT(it):
                dve.wait_ge(*seen("pT_ps", it + 1))
                dve.wait_ge(*seen("o_ps", it))
                V.tensor_copy(pT.rearrange("p l j k -> p (l j k)"), bank16(TB)).then_inc(sem("pT_sb"), 1)

            def lo_o(it):
                dve.wait_ge(sem("o_hi"), it + 1)
                STT(oT[:, 1].rearrange("p j k -> p (j k)"), bank(OB), 1.0 / PS,
                    oT[:, 0].rearrange("p j k -> p (j k)"), ALU.mult, ALU.subtract).then_inc(
                    sem("o_lo"), 1)

            def head(g, h, hm, first=False, last2=0):
                it = g * NH + h
                dve.wait_ge(sem("s_ps"), it + 1)
                V.tensor_reduce(mx4, bank(SB_).rearrange("p (j k) -> p j k", j=GB), AX.X,
                                ALU.max).then_inc(sem("m_max"), 1)
                dve.wait_ge(sem("m_max"), it + 1)
                V.tensor_scalar(nm4, mx4, -(QHD ** -0.5), None, ALU.mult).then_inc(sem("m_neg"), 1)
                if not first:
                    copy_pT(it - 1)
                if last2 != 2:
                    lo_q(0, it + 1)
                dve.wait_ge(*seen("p_exp", it + 1))
                V.reciprocal(er4, es4).then_inc(sem("p_rec"), 1)
                dve.wait_ge(sem("p_rec"), it + 1)
                V.tensor_scalar(eq4, er4, PS, None, ALU.mult).then_inc(sem("p_r"), 1)
                if last2 != 2:
                    lo_q(1, it + 1)
                if not first:
                    lo_o(it - 1)
                if not last2:
                    lo_v(it + 3, ((hm + 2) % 4) // 2, hm % 2)

            def attention(g):
                lo_q(0, g * NH)
                lo_q(1, g * NH)
                lo_v(g * NH + 1, 0, 0)
                lo_v(g * NH + 2, 0, 1)
                head(g, 0, 0, first=True)
                head(g, 1, 1)
                with dve.Fori(0, 3) as t:
                    for u in range(4):
                        head(g, t * 4 + (2 + u), (2 + u) % 4)
                head(g, 14, 2, last2=1)
                dve.wait_ge(*seen("out_done", g * 16))
                for j in range(GB):
                    last = V.tensor_scalar(hid[:, j, :], x1[:, j, :], mv4[:, j, 0:1], rs4[:, j:j + 1],
                                           ALU.subtract, ALU.mult)
                last.then_inc(sem("h0"), 1)
                head(g, 15, 3, last2=2)
                copy_pT(g * NH + 15)
                lo_o(g * NH + 15)

            def router(g):
                dve.wait_ge(sem("h0"), g + 1)
                dve.wait_ge(*seen("op_ps", g * NH + NH))
                STT(hf, bank(AB, 2), 1.0 / WS, hf, ALU.mult, ALU.add).then_inc(sem("hid"), 1)
                dve.wait_ge(sem("rms_rs"), g + 1)
                for j in range(GB):
                    last = STT(xr[:, j, :], hid[:, j, :], rrs4[:, j:j + 1], cs[:, C_LN2:C_LN2 + D],
                               ALU.mult, ALU.mult)
                last.then_inc(sem("rms_xr"), 1)
                dve.wait_ge(sem("rms_xr"), g + 1)
                STT(hf, hf, gt[:, 1:2], x1.rearrange("p j d -> p (j d)"), ALU.mult, ALU.add).then_inc(
                    sem("z"), 1)
                dve.wait_ge(sem("rms_tp"), g + 1)
                V.tensor_copy(xT.rearrange("p l k t -> p (l k t)"), bank16(VB, 2)).then_inc(sem("rms_xT"), 1)
                RC = 14
                step = [0]

                def link(ins):
                    step[0] += 1
                    ins.then_inc(sem("rt_step"), 1)
                    dve.wait_ge(sem("rt_step"), g * RC + step[0])
                    apart(dve)

                b16 = [P, GB, NE]
                dve.wait_ge(sem("rt_ps"), g + 1)
                lg = bank(OB)[:, 0:GB * NE].rearrange("p (j e) -> p j e", j=GB)
                link(V.tensor_reduce(rt_mx, lg, AX.X, ALU.max))
                TT(rt_l, lg, rt_mx.unsqueeze(2).broadcast_to(b16), ALU.subtract).then_inc(sem("rt_sub"), 1)
                dve.wait_ge(sem("rt_exp"), g + 1)
                link(V.tensor_reduce(rt_s, rt_e, AX.X, ALU.add))
                link(V.reciprocal(rt_r, rt_s))
                link(TT(rt_p, rt_e, rt_r.unsqueeze(2).broadcast_to(b16), ALU.mult))
                for j in range(GB):
                    last = V.max(rt_8[:, j, :], rt_p[:, j, :])
                link(last)
                for j in range(GB):
                    last = V.max_index(rt_ix[:, j, :], rt_8[:, j, :], rt_p[:, j, :])
                link(last)
                link(V.tensor_copy(rt_xf, rt_ix[:, :, 0:TOPK]))
                link(TT(rt_eq, cs[:, C_IOTA:C_IOTA + NE].unsqueeze(1).unsqueeze(3)
                        .broadcast_to([P, GB, NE, TOPK]),
                        rt_xf.unsqueeze(2).broadcast_to([P, GB, NE, TOPK]), ALU.is_equal))
                link(V.tensor_reduce(rt_m, rt_eq, AX.X, ALU.add))
                link(TT(rt_w, rt_p, rt_m, ALU.mult))
                link(V.tensor_reduce(rt_s2, rt_w, AX.X, ALU.add))
                link(V.reciprocal(rt_r2, rt_s2))
                link(TT(rt_f, rt_w, rt_r2.unsqueeze(2).broadcast_to(b16), ALU.mult))
                dve.wait_ge(sem("one_set"), g + 1)
                apart(dve)
                link(V.tensor_copy(wcat[:, :, 0:NE], rt_f))
                assert step[0] == RC
                TT(wcat[:, :, 32:32 + NE], rt_f, wcat[:, :, 0:NE], ALU.subtract).then_inc(sem("rt_cat"), 1)
                dve.wait_ge(sem("wT_ps"), g + 1)
                V.tensor_copy(wT[:, :], bank16(OB)[:, 0:T]).then_inc(sem("wT_sb"), 1)

            dve.wait_ge(sem("const_in"), 80)
            dve.wait_ge(sem("wa_in"), 16)
            centred = [(stage_a[:, 0:512], 0, 32), (stage_a[:, 512:768], 32, 16),
                       (stage_a[:, 1024:1280], 48, 16), (cs[:, 0:512], 64, 32)]
            for w, o, n in centred:
                last = V.tensor_reduce(w_mu[:, o:o + n], w.rearrange("p (h d) -> p h d", d=XD), AX.X, ALU.add)
            last.then_inc(sem("centred"), 1)
            dve.wait_ge(sem("centred"), 1)
            V.tensor_scalar(w_mu, w_mu, -1.0 / XD, None, ALU.mult).then_inc(sem("centred"), 1)
            dve.wait_ge(sem("centred"), 2)
            for w, o, n in centred:
                wr = w.rearrange("p (h d) -> p h d", d=XD)
                last = TT(wr, wr, w_mu[:, o:o + n].unsqueeze(2).broadcast_to([P, n, XD]), ALU.add)
            last.then_inc(sem("centred"), 1)
            dve.wait_ge(sem("gr_hi"), 1)
            STT(grw[:, 1].rearrange("p k e -> p (k e)"), cs[:, C_RT:C_RT + KC * NE], WS,
                grw[:, 0].rearrange("p k e -> p (k e)"), ALU.mult, ALU.subtract)
            dve.wait_ge(sem("centred"), 3)
            dve.wait_ge(sem("wa_hi"), 1)
            STT(walo[:, :], stage_a, WS, wahi[:, :], ALU.mult, ALU.subtract).then_inc(
                sem("stage_cut"), 1)
            dve.wait_ge(sem("gates"), 2)
            cross("dve", steps, 0, False)
            with dve.Fori(0, NG - 1) as g:
                attention(g)
                router(g)
                cross("dve", steps, g, True)
            attention(NG - 1)
            router(NG - 1)
            last_experts(dve, steps)


def kernel(x, ctx_1024, g_xattn, g_ffn, L0_xattn_Wq, L0_xattn_bq, L0_xattn_Wk, L0_xattn_bk,
           L0_xattn_Wv, L0_xattn_bv, L0_xattn_Wkv_dca, L0_xattn_bkv_dca, L0_xattn_qn_w, L0_xattn_qn_b,
           L0_xattn_kn_w, L0_xattn_kn_b, L0_xattn_kn_dca_w, L0_xattn_kn_dca_b, L0_xattn_Wo, L0_xattn_bo,
           L0_ffn_positions, L0_ffn_ln1_w, L0_ffn_ln2_w, L0_ffn_q_w, L0_ffn_kv_w, L0_ffn_o_w,
           L0_ffn_gate_w, L0_ffn_w1, L0_ffn_w2, L0_ffn_sh_gu_w, L0_ffn_sh_down_w):
    import numpy as np
    import ml_dtypes
    import concourse.bacc as bacc
    from concourse import mybir
    from concourse.bass_utils import run_bass_kernel_spmd as run

    f = lambda a: np.asarray(a, dtype=np.float32)
    wkv = np.concatenate([f(L0_xattn_Wk), f(L0_xattn_Wv)], 1).reshape(P, XH, 2, XD)
    wkv = wkv.transpose(0, 2, 1, 3).reshape(P, 512)
    bkv = np.concatenate([f(L0_xattn_bk), f(L0_xattn_bv)]).reshape(XH, 2, XD).transpose(1, 0, 2).reshape(512)
    two = lambda w: f(w).reshape(KC, P, D).transpose(1, 0, 2).reshape(P, KC * D)
    wa = np.concatenate([two(L0_xattn_Wq), wkv, f(L0_xattn_Wkv_dca), two(L0_xattn_Wo)], 1)
    inT = lambda w: f(w).reshape(-1, P, KC, P).transpose(3, 0, 2, 1)
    q = inT(f(L0_ffn_q_w).reshape(NH, QHD, D)[:, :HD].reshape(NH * HD, D))
    kv = f(L0_ffn_kv_w)
    k, v = inT(kv[:NH * HD]), inT(kv[NH * HD:2 * NH * HD])
    o = f(L0_ffn_o_w).reshape(D, NH, HD).transpose(2, 1, 0)
    heads = np.concatenate([w.reshape(P, NH, D) for w in (q, k, v, o)], 2).reshape(P, NH * HW)
    w1, w2 = f(L0_ffn_w1), f(L0_ffn_w2)
    sgu = f(L0_ffn_sh_gu_w)
    pad = np.zeros((NC * P - NE * EI - SHI, D), np.float32)
    wg = inT(np.concatenate([w1[:, :EI].reshape(-1, D), sgu[:SHI], pad]))
    wu = inT(np.concatenate([w1[:, EI:].reshape(-1, D), sgu[SHI:], pad]))
    wd = np.concatenate([w2.transpose(0, 2, 1).reshape(-1, D), f(L0_ffn_sh_down_w).T, pad])
    wd = wd.reshape(NC, P, D).transpose(1, 0, 2)
    chunks = np.concatenate([wg.reshape(P, NC, D), wu.reshape(P, NC, D), wd], 2).reshape(P, NC * CW)
    wall = np.ascontiguousarray(np.concatenate([heads, chunks], 1))
    c = np.zeros((P, CWID), np.float32)
    c[:, 0:256] = f(L0_xattn_bq)
    c[:MAIN, 256:768] = bkv
    c[MAIN:, 256:768] = f(L0_xattn_bkv_dca)
    for off, qn, kn, kd in ((C_LNW, L0_xattn_qn_w, L0_xattn_kn_w, L0_xattn_kn_dca_w),
                            (C_LNB, L0_xattn_qn_b, L0_xattn_kn_b, L0_xattn_kn_dca_b)):
        c[:, off:off + XD] = f(qn)
        c[:MAIN, off + XD:off + 2 * XD] = f(kn)
        c[MAIN:, off + XD:off + 2 * XD] = f(kd)
    c[:, C_BO:C_BO + D] = f(L0_xattn_bo)
    c[:, C_LN1:C_LN1 + D] = f(L0_ffn_ln1_w)
    c[:, C_LN2:C_LN2 + D] = f(L0_ffn_ln2_w)
    c[:, C_GATE] = f(g_xattn)[0]
    c[:, C_GATE + 1] = f(g_ffn)[0]
    c[:, C_RT:C_RT + KC * NE] = f(L0_ffn_gate_w).reshape(NE, KC, P).transpose(2, 1, 0).reshape(P, KC * NE)
    c[:, C_IOTA:C_IOTA + NE] = np.arange(NE)
    c[:MAIN, C_SEG] = 1
    c[MAIN:, C_SEG + 1] = 1
    sel = np.zeros((P, NC * P), np.float16)
    rows = np.arange(NC * P)
    sel[np.minimum(rows // EI, NE), rows] = 0.5 / WS / WS
    sel[32 + np.minimum(rows // EI, NE), rows] = 0.5 / WS / WS
    mask = np.where(np.tril(np.ones((S, S), bool)), 0.0, MASKED)
    ident = np.zeros((P, 2 * P), np.float16)
    ident[:, :P] = np.eye(P)
    ident[0, P:P + MAIN] = 1
    ident[1, P + MAIN:] = 1
    arrays = {
        "in_x": f(x), "in_yT": np.ascontiguousarray(f(ctx_1024).transpose(0, 2, 1)),
        "in_wa": np.ascontiguousarray(wa), "in_wall": wall, "in_cst": c,
        "in_ident": ident, "in_identb": np.eye(P).astype(ml_dtypes.bfloat16),
        "in_maskb": mask.astype(ml_dtypes.bfloat16), "in_sel": sel,
    }
    nc = bacc.Bacc("TRN2", target_bir_lowering=False, num_devices=1)
    args = [nc.dram_tensor(n, a.shape, mybir.dt.from_np(a.dtype), kind="ExternalInput").ap()
            for n, a in arrays.items()]
    args.append(nc.dram_tensor("out_0", (NB, S, D), mybir.dt.float32, kind="ExternalOutput").ap())
    build(nc, *args)
    r = run(nc, [arrays], core_ids=[0])
    return r.results[0]["out_0"]
```

```python
from contextlib import ExitStack

import numpy as np
import concourse.bass as bass
from concourse import mybir
from concourse.alu_op_type import AluOpType as ALU

ACT = mybir.ActivationFunctionType
AX = mybir.AxisListType
F32, F16, BF16 = mybir.dt.float32, mybir.dt.float16, mybir.dt.bfloat16
U32, I32 = mybir.dt.uint32, mybir.dt.int32

P = 128
NB, S, D = 16, 128, 256
KC = D // P
GB = 4
NG = NB // GB
T = GB * S
XH, XD = 16, 16
DCA = 16
MAIN = S - DCA
NH, QHD, HD = 16, 192, 128
NE, EI, TOPK = 16, 176, 4
SHI = 352
NC = -(-(NE * EI + SHI) // P)
HW = 3 * D + D
CW = 3 * D
WALL = NH * HW + NC * CW
UNITS = 32
UW = WALL // UNITS
WS = 64.0
PS = 256.0
WA = 2048
NQ = 4
QH = XH // NQ
PERIODS = GB + 2
CHUNKS = (5, 5, 5, 5, 4, 1)
CUTS = (4, 4, 4, 3, 3, 0)
HEADCUTS = 14
NEWTON = 13
SEGS = ((0, slice(0, MAIN)), (1, slice(MAIN, S)))
C_BIAS, C_LNW, C_LNB, C_BO, C_LN1, C_LN2, C_GATE, C_RT, C_IOTA, C_SEG, CWID = (
    0, 768, 800, 832, 1088, 1344, 1600, 1602, 1634, 1650, 1652)
PRIMED = 1
MASKED = -1.0e12

ORDER = {
    "pe": """
        e:gate.0 2:scores.0 3:turn_c e:up.0 2:maxima.0 3:project e:weight.0 2:exp.0 e:down.0
        2:scores.1 1:turn e:gate.1 2:maxima.1 1:keys e:weight.1 2:context.0 2:exp.1 e:up.1
        2:scores.2 1:query e:down.1 2:maxima.2 e:gate.2 2:context.1 2:exp.2 e:up.2 e:weight.2
        2:scores.3 e:gate.3 2:maxima.3 e:down.2 2:exp.3 2:context.2 e:up.3 e:weight.3 e:down.3
        e:gate.4 2:context.3 3:turn_z e:up.4 e:weight.4 1:cat_q e:down.4 1:cat_k
        """,
    "act": """
        e:gate.0 3:turn_c 2:v_hi 2:maxima.0 1:x_hi 2:exp.0 2:p_hi.0 1:turn 2:maxima.1 e:m_hi.0
        e:gate.1 2:exp.1 2:c_hi.0 2:p_hi.1 1:square 2:maxima.2 e:gate.2 2:exp.2 e:m_hi.1
        2:p_hi.2 2:maxima.3 2:c_hi.1 3:z_hi e:gate.3 e:m_hi.2 2:exp.3 2:p_hi.3 1:qk_hi 2:c_hi.2
        e:m_hi.3 e:gate.4 3:turn_z 1:cat_q 2:c_hi.3 e:m_hi.4 1:cat_k
        """,
    "pool": """
        1:x_rs 1:x_lo 1:y_cut 2:v_ones 3:z_rs 2:p_lo.0 3:x_rs e:m_lo.0 2:p_lo.1 e:m_lo.1
        2:p_lo.2 e:m_lo.2 2:p_lo.3 1:qk_lo e:m_lo.3 e:m_lo.4
        """,
    "dve": """
        1:stats 1:mean 2:max.0 2:negate.0 1:x_norm e:gate.0 e:up.0 3:out 3:new_x 3:stats 3:mean
        e:weight.0 2:max.1 2:negate.1 2:v_lo 1:v_row 1:k_row 2:c_sum.0 2:c_over.0 2:c_add.0
        3:z_norm e:gate.1 2:max.2 2:negate.2 e:up.1 1:q_row 2:c_lo.0 e:weight.1 1:newton.0
        1:newton.1 1:newton.2 2:c_sum.1 1:newton.3 2:c_over.1 1:newton.4 1:newton.5 2:c_add.1
        1:newton.6 e:gate.2 1:newton.7 1:newton.8 2:max.3 1:newton.9 2:negate.3 e:up.2
        1:newton.10 e:weight.2 1:newton.11 2:c_lo.1 1:newton.12 3:z_lo 1:qk_rs 1:qk_w 2:c_sum.2
        1:qk_b 2:c_over.2 e:gate.3 2:c_add.2 e:up.3 2:c_lo.2 e:weight.3 2:c_sum.3 e:gate.4
        2:c_over.3 e:up.4 e:weight.4 2:c_add.3 2:c_lo.3
        """,
}
ORDER_START = {
    "pe": """
        3:turn_c 2:scores.0 3:project 2:maxima.0 1:turn 2:exp.0 1:keys 2:scores.1 1:query
        2:maxima.1 2:context.0 2:exp.1 2:scores.2 2:maxima.2 2:exp.2 2:context.1 2:scores.3
        2:maxima.3 2:exp.3 2:context.2 1:cat_q 3:turn_z 2:context.3 1:cat_k
        """,
    "act": """
        3:turn_c 1:x_hi 2:v_hi 2:maxima.0 1:turn w:cut.0 2:exp.0 2:p_hi.0 w:cut.1 2:maxima.1
        1:square 2:exp.1 2:p_hi.1 w:cut.2 2:c_hi.0 2:maxima.2 w:cut.3 2:exp.2 2:p_hi.2 1:qk_hi
        2:maxima.3 2:c_hi.1 3:z_hi 2:exp.3 2:p_hi.3 2:c_hi.2 1:cat_q 3:turn_z 2:c_hi.3 1:cat_k
        """,
    "pool": """
        1:y_cut 2:v_ones 1:x_rs 1:x_lo 2:p_lo.0 2:p_lo.1 3:z_rs 2:p_lo.2 3:x_rs 1:qk_lo 2:p_lo.3
        """,
    "dve": """
        1:stats 1:mean 1:x_norm 2:max.0 2:negate.0 3:out 3:new_x 2:v_lo 3:stats w:cut.0 1:v_row
        1:k_row 2:max.1 2:negate.1 1:q_row w:cut.1 1:newton.0 2:c_sum.0 1:newton.1 1:newton.2
        2:c_over.0 1:newton.3 1:newton.4 1:newton.5 2:max.2 1:newton.6 2:negate.2 1:newton.7
        2:c_add.0 1:newton.8 1:newton.9 1:newton.10 2:c_lo.0 1:newton.11 1:newton.12 1:qk_rs
        1:qk_w 3:mean 1:qk_b 2:max.3 2:negate.3 2:c_sum.1 2:c_over.1 2:c_add.1 3:z_norm 2:c_lo.1
        w:cut.2 2:c_sum.2 2:c_over.2 2:c_add.2 3:z_lo 2:c_lo.2 w:cut.3 2:c_sum.3 2:c_over.3
        2:c_add.3 2:c_lo.3
        """,
}


def build(nc, x, yT, wa, wall, cst, ident, identb, maskb, sel, out):
    assert WALL % UNITS == 0 and sum(CHUNKS) == NC and sum(CUTS) == UNITS - HEADCUTS
    assert (UNITS - HEADCUTS) * UW >= NH * HW and UNITS % 2 == 0 and HEADCUTS % 2 == 0
    with ExitStack() as ctx:
        def sb(name, shape, dt):
            return ctx.enter_context(nc.sbuf_tensor(name, shape, dt))

        sems = {}

        def sem(name):
            if name not in sems:
                sems[name] = ctx.enter_context(nc.semaphore(name))
            return sems[name]

        primed = {"p_exp": "act", "pT_sb": "dve", "o_lo": "dve", "me_a": "dve", "me_b": "dve",
                  "me_v": "dve", "p_lo": "pool", "pT_ps": "pe", "op_ps": "pe", "me_lo": "pool",
                  "o_ps": "pe", "d_ps": "pe", "out_done": "sp", "xa_yl": "pool", "xa_kvp": "pe",
                  "xa_catp": "pe", "xa_ck": "act", "xa_sT": "pe", "xa_vl": "dve", "xa_pv": "pe",
                  "xa_e": "act", "xa_pl": "pool", "xa_mTp": "pe", "xa_cl": "dve", "xa_o": "dve",
                  "xa_cTp": "pe", "xb_tp": "pe", "xb_xT": "act"}

        def apart(eng):
            eng.sem_inc(sem("apart"), 1)

        def prime(eng, name):
            for s, by in primed.items():
                if by == name:
                    eng.sem_inc(sem(s), PRIMED)

        def seen(name, n):
            assert name in primed
            return sem(name), n + PRIMED

        whi = sb("whi", [P, WALL], F16)
        wlo = sb("wlo", [P, WALL], F16)
        wahi = sb("wahi", [P, WA], F16)
        walo = sb("walo", [P, WA], F16)
        cs = sb("cs", [P, CWID], F32)
        idn2 = sb("idn2", [P, 2 * P], F16)
        idb = sb("idb", [P, P], BF16)
        msk = sb("msk", [P, S], BF16)
        sl = sb("sl", [P, NC * P], F16)
        y_t = sb("y_t", [P, S], F32)
        x1 = sb("x1", [P, GB, D], F32)
        ysp = sb("ysp", [P, 4, S], F16)
        wT = sb("wT", [P, T], F16)
        sm = sb("sm", [P, 256], F32)
        gt = sb("gt", [P, 3], F32)
        mhalf = sb("mhalf", [P, GB], F32)
        grw = sb("grw", [P, 2, KC, NE], F16)
        ar = sb("ar", [P, 10016], F32)
        ps = ctx.enter_context(nc.psum_tensor("ps", [P, 8, 512], F32))

        idn, seg = idn2[:, 0:P], idn2[:, P:2 * P]

        def words(a, n):
            return ar[:, a:a + n]

        def halves(a, n):
            return ar[:, a:a + n].bitcast(F16)

        def bank16(b, n=1):
            return ps[:, b:b + n, :].rearrange("p b w -> p (b w)").bitcast(F16)

        def bank(b, n=1):
            return ps[:, b:b + n, :].rearrange("p b w -> p (b w)")

        XS, XP, XF = 0, 1, 2
        SB_, QB, KB, VB, TB, OB, AB = 0, 1, 2, 3, 4, 5, 6
        GBK, UBK, WBK = 3, 4, 5

        xTn = halves(0, 1024).rearrange("p (l k t) -> p l k t", l=2, k=KC)
        xT = halves(1024, 1024).rearrange("p (l k t) -> p l k t", l=2, k=KC)
        hid = words(2048, 1024).rearrange("p (j d) -> p j d", j=GB)
        me_t, me_p = words(3072, 512), words(3584, 512)
        me_hl = halves(4096, 512).rearrange("p (l t) -> p l t", l=2)
        stage = [words(1024, UW), words(1024 + UW, UW)]
        stage_a = words(1024, WA)
        assert 1024 + max(2 * UW, WA) <= 4608
        A0 = 4608
        qkT = halves(A0, 1024).rearrange("p (w l t) -> p w l t", w=2, l=2)
        vv = halves(A0 + 1024, 2048).rearrange("p (r l j c) -> p r l j c", r=2, l=2, j=GB)
        pr = words(A0 + 3072, 512).rearrange("p (j k) -> p j k", j=GB)
        phl = halves(A0 + 3584, 512).rearrange("p (l j k) -> p l j k", l=2, j=GB)
        pT = halves(A0 + 4096, 512).rearrange("p (l j k) -> p l j k", l=2, j=GB)
        oT = halves(A0 + 4608, 512).rearrange("p (l j k) -> p l j k", l=2, j=GB)
        wcat = halves(A0 + 2048, 256).rearrange("p (j c) -> p j c", j=GB)
        w_mu = words(A0 + 2048, 96)
        xr = words(A0, 1024).rearrange("p (j d) -> p j d", j=GB)
        xrs = halves(A0 + 1024, 1024).rearrange("p (l j d) -> p l j d", l=2, j=GB)
        xn = words(A0, 256)
        xs = halves(A0 + 256, 256).rearrange("p (l d) -> p l d", l=2)
        xsT = halves(A0 + 512, 256).rearrange("p (l k t) -> p l k t", l=2, k=KC)
        sq = words(A0, 512).rearrange("p (h d) -> p h d", d=XD)
        cat = halves(A0, 1024).rearrange("p (h a b d) -> p h a b d", a=2, b=2, d=XD)
        catf = halves(A0, 1024)
        qk = words(A0 + 1024, 512).rearrange("p (h d) -> p h d", d=XD)
        vf = words(A0 + 1536, 256)
        catT = halves(A0 + 1792, 1024).rearrange("p (w h t) -> p w h t", w=2, h=8)
        vs = halves(A0 + 2816, 544).rearrange("p (l h s c) -> p l h s c", l=2, h=XH, s=2)
        xp = words(A0 + 3360, 512)
        xpT = halves(A0 + 3872, 512).rearrange("p (l h q) -> p l h q", l=2, h=QH)
        shift = halves(A0 + 4384, 256)
        xc = halves(A0 + 4640, 256).rearrange("p (l d) -> p l d", l=2)
        xcT = halves(A0 + 4896, 256).rearrange("p (l k t) -> p l k t", l=2, k=KC)
        zs = halves(A0 + 4896, 256).rearrange("p (l d) -> p l d", l=2)
        z = words(A0 + 5152, 256)

        st4 = sm[:, 0:24].rearrange("p (j s) -> p j s", j=GB)
        mv4 = sm[:, 24:32].rearrange("p (j s) -> p j s", j=GB)
        ve4, rs4, ss4 = sm[:, 32:36], sm[:, 36:40], sm[:, 40:44]
        rve4, rrs4 = sm[:, 44:48], sm[:, 48:52]
        mx4, nm4, es4, er4, eq4 = (sm[:, 52 + 4 * n:56 + 4 * n] for n in range(5))
        a_st, a_mv, a_ve, a_rs = sm[:, 72:78], sm[:, 78:80], sm[:, 80:81], sm[:, 81:82]
        b_ve = sm[:, 90:91]
        b_ve2, b_rs2 = sm[:, 93:94], sm[:, 94:95]
        a_ss, a_v, a_y, a_t = (sm[:, 96 + 32 * n:128 + 32 * n] for n in range(4))
        a_mx, a_r = (sm[:, 224 + 8 * n:232 + 8 * n].rearrange("p (h s) -> p h s", s=2)
                     for n in range(2))
        a_mn = sm[:, 240:244].bitcast(F16).rearrange("p (h s) -> p h s", s=2)
        ln_ps = sm[:, 244:245]
        rt = words(A0 + 2304, 768)
        rt_l, rt_e, rt_p, rt_m, rt_w, rt_f = (
            rt[:, 64 * n:64 * n + 64].rearrange("p (j e) -> p j e", j=GB) for n in range(6))
        rt_8 = rt[:, 384:416].rearrange("p (j k) -> p j k", j=GB)
        rt_ix = rt[:, 416:448].bitcast(U32).rearrange("p (j k) -> p j k", j=GB)
        rt_xf = rt[:, 448:464].rearrange("p (j k) -> p j k", j=GB)
        rt_mx, rt_s, rt_r, rt_s2, rt_r2 = (rt[:, 464 + 4 * n:468 + 4 * n] for n in range(5))
        rt_eq = rt[:, 512:768].rearrange("p (j e k) -> p j e k", j=GB, e=NE)

        def context(l, q):
            return xc[:, l, :].rearrange("p (r b d) -> p r b d", b=2, d=XD)[
                :, 4 * (q // 2):4 * (q // 2) + 4, q % 2, :]

        def head_of(q, h):
            return 2 * (4 * (q // 2) + h) + q % 2

        ctx_ps = bank(XP)[:, 0:QH * 2 * (XD + 1)].rearrange("p (h s c) -> p h s c", h=QH, s=2)
        ctx_sum = bank(XP)[:, 256:256 + QH * XD].rearrange("p (h d) -> p h d", d=XD)

        def ln_rows(c):
            return cs[:, c:c + 32].rearrange("p (w d) -> p w d", w=2).unsqueeze(2).broadcast_to(
                [P, 2, XH, XD])

        def wcol(w, off, n=P):
            return w[:, bass.ds(off, n)]

        x_d = x.rearrange("b s d -> s b d")
        y_d = yT.rearrange("b k s -> k b s")
        out_d = out.rearrange("b s d -> s b d")

        EARLY = {"pe": ("e:gate.0", "e:up.0", "e:gate.1", "e:up.1"), "pool": ("1:y_cut",),
                 "dve": ("e:gate.0", "e:up.0", "1:stats", "1:mean", "1:x_norm")}
        EARLY_START = {"pe": ("1:turn",), "act": ("1:x_hi",), "pool": ("1:x_rs", "1:x_lo"),
                       "dve": ("1:stats", "1:mean", "1:x_norm")}

        def period(steps, order, p, b1, b2, b3, g, early):
            chunk, unit = sum(CHUNKS[:p]), sum(CUTS[:p])
            for word in order.split():
                if p == 0 and word in early:
                    continue
                name, _, number = word.partition(".")
                number = int(number or 0)
                step = steps[name]
                if name[0] == "1" and b1:
                    step(*b1, number) if name == "1:newton" else step(*b1)
                elif name[0] == "2" and b2:
                    step(*b2) if name in ("2:v_hi", "2:v_lo", "2:v_ones") else step(b2[0], number)
                elif name[0] == "3" and b3:
                    step(*b3, b2 is not None)
                elif name[0] == "e" and g is not None and number < CHUNKS[p]:
                    c = chunk + number - (name == "e:down")
                    if c >= 0:
                        step(g, c)
                elif name[0] == "w" and g is None and number < CUTS[p]:
                    step(unit + number)

        def cross(engine, steps, g, chunks):
            base = (g + 1) * GB if chunks else 0
            order = (ORDER if chunks else ORDER_START)[engine]
            early = (EARLY if chunks else EARLY_START).get(engine, ())
            for p in range(PERIODS):
                b = [(base + q, q) if 0 <= q < GB else None for q in (p, p - 1, p - 2)]
                period(steps, order, p, *b, g if chunks else None, early)
            if chunks:
                if "e:down" in steps:
                    steps["e:down"](g, NC - 1)
                if "e:finish" in steps:
                    steps["e:finish"](g)

        def last_experts(engine, eng, steps):
            g = NG - 1

            def chunk(c):
                for name in ("e:gate", "e:up", "e:weight", "e:down", "e:m_hi", "e:m_lo"):
                    if isinstance(c, int) and f"{name}.{c}" in EARLY.get(engine, ()):
                        continue
                    if name in steps and name != "e:down":
                        steps[name](g, c)
                    elif name in steps and not (isinstance(c, int) and c == 0):
                        steps[name](g, c - 1)

            chunk(0)
            chunk(1)
            with eng.Fori(2, NC) as c:
                chunk(c)
            if "e:down" in steps:
                steps["e:down"](g, NC - 1)
            if "e:finish" in steps:
                steps["e:finish"](g)

        block = ctx.enter_context(nc.Block())

        @block.sync
        def _(sp):
            prime(sp, "sp")
            sp.dma_start(x1[:, :, :], x_d[:, 0:GB, :]).then_inc(sem("x_in"), 16)
            sp.dma_start(idn2[:, :], ident).then_inc(sem("idn_in"), 16)
            sp.dma_start(cs[:, :], cst).then_inc(sem("cst_in"), 16)
            sp.dma_start(stage_a, wa).then_inc(sem("wa_in"), 16)
            sp.dma_start(y_t[:, :], y_d[:, 0, :]).then_inc(sem("y_in"), 16)
            for p in range(PERIODS):
                for k in range(CUTS[p]):
                    u = sum(CUTS[:p]) + k
                    sp.wait_ge(sem("stage_cut"), max(u, 1))
                    sp.dma_start(stage[u % 2], wall[:, u * UW:(u + 1) * UW]).then_inc(
                        sem(f"stage_in{u % 2}"), 16)
                    if k == 2 and p + 1 < GB:
                        sp.wait_ge(*seen("xa_yl", p + 1))
                        sp.dma_start(y_t[:, :], y_d[:, p + 1, :]).then_inc(sem("y_in"), 16)
            sp.dma_start(idb[:, :], identb).then_inc(sem("mask_in"), 16)
            sp.dma_start(msk[:, :], maskb).then_inc(sem("mask_in"), 16)
            for u in range(UNITS - HEADCUTS, UNITS):
                sp.wait_ge(sem("stage_cut"), u)
                sp.dma_start(stage[u % 2], wall[:, u * UW:(u + 1) * UW]).then_inc(
                    sem(f"stage_in{u % 2}"), 16)
            sp.dma_start(sl[:, :], sel).then_inc(sem("sel_in"), 16)
            with sp.Fori(0, NG - 1) as g:
                sp.wait_ge(sem("z"), g * 2 + 2)
                sp.dma_start(x1[:, :, :], x_d[:, bass.ds((g + 1) * GB, GB), :]).then_inc(sem("x_in"), 16)
                for q in range(GB):
                    sp.wait_ge(*seen("xa_yl", (g + 1) * GB + q))
                    sp.dma_start(y_t[:, :], y_d[:, bass.ds((g + 1) * GB + q, 1), :]
                                 .rearrange("p b d -> p (b d)")).then_inc(sem("y_in"), 16)
                sp.wait_ge(sem("fin"), g + 1)
                sp.dma_start(out_d[:, bass.ds(g * GB, GB), :], hid).then_inc(sem("out_done"), 16)
            sp.wait_ge(sem("fin"), NG)
            sp.dma_start(out_d[:, (NG - 1) * GB:NG * GB, :], hid).then_inc(sem("out_done"), 16)
            sp.wait_ge(*seen("out_done", 16 * NG))

        @block.tensor
        def _(pe):
            prime(pe, "pe")
            mm = nc.tensor.matmul

            def three(o, l_hi, l_lo, r_hi, r_lo, start, stop):
                mm(o, l_hi, r_hi, start=start, stop=False, skip_group_check=True)
                mm(o, l_hi, r_lo, start=False, stop=False, skip_group_check=True)
                return mm(o, l_lo, r_hi, start=False, stop=stop, skip_group_check=True)

            def turn_rows(b, rows):
                t = bank16(b)[:, 0:512].rearrange("p (l k t) -> p l k t", l=2, k=KC)
                for l in range(2):
                    for k in range(KC):
                        last = nc.tensor.transpose(t[:, l, k, :], rows[:, l, k * P:(k + 1) * P], idn)
                return last

            def x1_turn(i, j):
                pe.wait_ge(sem("xa_xl"), i + 1)
                pe.wait_ge(*seen("xa_ck", i))
                turn_rows(XF, xs).then_inc(sem("xa_xTp"), 1)

            def x1_keys(i, j):
                pe.wait_ge(sem("xa_xT"), i + 1)
                pe.wait_ge(*seen("xa_yl", i + 1))
                for n, w in enumerate((512, 1024)):
                    last = three(bank(XF), ysp[:, 2 * n, :], ysp[:, 2 * n + 1, :],
                                 wahi[:, w:w + 512], walo[:, w:w + 512], n == 0, n == 1)
                last.then_inc(sem("xa_kvp"), 1)

            def x1_query(i, j):
                pe.wait_ge(sem("xa_k"), i + 1)
                for k in range(KC):
                    last = three(bank(XF)[:, 0:D], xsT[:, 0, k, :], xsT[:, 1, k, :],
                                 wahi[:, k * D:(k + 1) * D], walo[:, k * D:(k + 1) * D],
                                 k == 0, k == KC - 1)
                last.then_inc(sem("xa_qp"), 1)

            def turn_cat(w):
                for n in range(8):
                    last = nc.tensor.transpose(bank16(XF)[:, n * P:(n + 1) * P],
                                               catf[:, (8 * w + n) * P:(8 * w + n + 1) * P], idn)
                return last

            def cat_q(i, j):
                pe.wait_ge(sem("xa_lo"), i + 1)
                turn_cat(0).then_inc(sem("xa_catq"), 1)

            def cat_k(i, j):
                pe.wait_ge(sem("xa_cq"), i + 1)
                turn_cat(1).then_inc(sem("xa_catp"), 1)

            def x2_scores(i, q):
                n = i * NQ + q
                if q == 0:
                    pe.wait_ge(sem("xa_cq"), i + 1)
                    pe.wait_ge(*seen("xa_ck", i + 1))
                    if not (isinstance(i, int) and i == 0):
                        pe.wait_ge(*seen("xb_xT", i - 1))
                pe.wait_ge(*seen("xa_e", n))
                r = slice(64 * (q % 2), 64 * (q % 2) + 64)
                for h in range(QH):
                    pair = 4 * (q // 2) + h
                    last = mm(bank(XS)[:, h * P:(h + 1) * P], catT[r, 0, pair, :], catT[r, 1, pair, :],
                              start=True, stop=True, skip_group_check=True)
                last.then_inc(sem("xa_s"), 1)

            def x2_maxima(i, q):
                pe.wait_ge(sem("xa_mn"), i * NQ + q + 1)
                for h in range(QH):
                    last = nc.tensor.transpose(bank16(XS)[0:2, h * P:(h + 1) * P], a_mn[:, h, :], idn)
                last.then_inc(sem("xa_mTp"), 1)

            def x2_exp(i, q):
                pe.wait_ge(sem("xa_mT"), i * NQ + q + 1)
                mm(bank(XS), seg, shift, start=True, stop=False, skip_group_check=True)
                r = slice(64 * (q % 2), 64 * (q % 2) + 64)
                for h in range(QH):
                    pair = 4 * (q // 2) + h
                    last = mm(bank(XS)[:, h * P:(h + 1) * P], catT[r, 1, pair, :], catT[r, 0, pair, :],
                              start=False, stop=h == QH - 1, skip_group_check=True)
                last.then_inc(sem("xa_sT"), 1)

            def x2_context(i, q):
                n = i * NQ + q
                pe.wait_ge(*seen("xa_pl", n + 1))
                if q == 0:
                    pe.wait_ge(*seen("xa_vl", i + 1))
                    pe.wait_ge(sem("xa_ones"), i + 1)
                    pe.wait_ge(*seen("xa_o", i))
                pe.wait_ge(*seen("xa_cl", n))
                for h in range(QH):
                    v_hi, v_lo = (vs[:, l, head_of(q, h)].rearrange("p s c -> p (s c)") for l in range(2))
                    last = three(ctx_ps[:, h].rearrange("p s c -> p (s c)"), xpT[:, 0, h, :],
                                 xpT[:, 1, h, :], v_hi, v_lo, True, True)
                last.then_inc(sem("xa_pv"), 1)

            def x3_turn_c(i, j, beside):
                pe.wait_ge(*seen("xa_cl", i * NQ + NQ))
                turn_rows(XP, xc).then_inc(sem("xa_cTp"), 1)

            def x3_project(i, j, beside):
                pe.wait_ge(sem("xa_cT"), i + 1)
                for k in range(KC):
                    w = slice(1536 + k * D, 1536 + (k + 1) * D)
                    last = three(bank(XP)[:, 0:D], xcT[:, 0, k, :], xcT[:, 1, k, :],
                                 wahi[:, w], walo[:, w], k == 0, k == KC - 1)
                last.then_inc(sem("xa_yp"), 1)

            def turn_z(i, j, beside):
                pe.wait_ge(sem("xb_zl"), i + 1)
                pe.wait_ge(*seen("xb_xT", i))
                if beside:
                    pe.wait_ge(*seen("xa_e", i * NQ + 2 * NQ))
                turn_rows(XS, zs).then_inc(sem("xb_tp"), 1)

            def gate_or_up(g, c, w, b, free, made):
                n = g * NC + c
                pe.wait_ge(*seen(free, n))
                for k in range(KC):
                    off = c * CW + (NH * HW + w * D + k * P)
                    last = three(bank(b), wcol(whi, off), wcol(wlo, off), xT[:, 0, k, :],
                                 xT[:, 1, k, :], k == 0, k == KC - 1)
                last.then_inc(sem(made), 1)

            def gate(g, c):
                gate_or_up(g, c, 0, GBK, "me_a", "g_ps")

            def up(g, c):
                gate_or_up(g, c, 1, UBK, "me_b", "u_ps")

            def weight(g, c):
                pe.wait_ge(*seen("me_v", g * NC + c))
                mm(bank(WBK), wcol(sl, c * P), wT[:, :], start=True, stop=True,
                   skip_group_check=True).then_inc(sem("w_ps"), 1)

            def down(g, c):
                n = g * NC + c
                first, end = isinstance(c, int) and c == 0, isinstance(c, int) and c == NC - 1
                pe.wait_ge(*seen("me_lo", n + 1))
                off = c * CW + (NH * HW + 2 * D)
                for j in range(GB):
                    o = bank(AB + j // 2)[:, (j % 2) * D:(j % 2 + 1) * D]
                    cc = slice(j * S, (j + 1) * S)
                    last = three(o, me_hl[:, 0, cc], me_hl[:, 1, cc], wcol(whi, off, D),
                                 wcol(wlo, off, D), first and j % 2 == 0, end and j % 2 == 1)
                last.then_inc(sem("d_ps"), 1)

            steps = {"1:turn": x1_turn, "1:keys": x1_keys, "1:query": x1_query, "1:cat_q": cat_q,
                     "1:cat_k": cat_k, "2:scores": x2_scores, "2:maxima": x2_maxima, "2:exp": x2_exp,
                     "2:context": x2_context, "3:turn_c": x3_turn_c, "3:project": x3_project,
                     "3:turn_z": turn_z, "e:gate": gate, "e:up": up, "e:weight": weight,
                     "e:down": down}

            def turn_x(n, half):
                pe.wait_ge(sem("rms_lo"), n)
                o = bank16(VB + half).rearrange("p (l k j t) -> p l k j t", l=2, k=KC, j=2)
                for l in range(2):
                    for k in range(KC):
                        for j in range(2):
                            last = nc.tensor.transpose(o[:, l, k, j, :],
                                                       xrs[:, l, 2 * half + j, k * P:(k + 1) * P], idn)
                last.then_inc(sem("rms_tp"), 1)

            def project(w, wh):
                for k in range(KC):
                    off = wh + (w * D + k * P)
                    last = three(bank(QB + w), wcol(whi, off), wcol(wlo, off),
                                 xTn[:, 0, k, :], xTn[:, 1, k, :], k == 0, k == KC - 1)
                last.then_inc(sem("q_ps" if w == 0 else "k_ps"), 1)

            def values(wh, half):
                for jj in range(2):
                    j = 2 * half + jj
                    for k in range(KC):
                        def rv(w):
                            return w[:, bass.ds(wh + (2 * D + k * P), 2 * HW)].rearrange(
                                "p (h c) -> p h c", h=2)[:, :, 0:P]
                        last = three(bank(VB)[:, jj * 256:(jj + 1) * 256].rearrange("p (h c) -> p h c", h=2),
                                     xTn[:, 0, k, j * S:(j + 1) * S], xTn[:, 1, k, j * S:(j + 1) * S],
                                     rv(whi), rv(wlo), jj == 0 and k == 0, jj == 1 and k == KC - 1)
                last.then_inc(sem("v_ps"), 1)

            def scores(it):
                pe.wait_ge(sem("q_lo"), it + 1)
                pe.wait_ge(sem("k_lo"), it + 1)
                pe.wait_ge(*seen("p_exp", it))
                mm(bank(SB_).rearrange("p (j k) -> p j k", j=GB), idb[:, :],
                   msk[:, :].unsqueeze(1).broadcast_to([P, GB, S]), start=True, stop=False,
                   skip_group_check=True)
                for j in range(GB):
                    c = slice(j * S, (j + 1) * S)
                    last = three(bank(SB_)[:, c], qkT[:, 0, 0, c], qkT[:, 0, 1, c],
                                 qkT[:, 1, 0, c], qkT[:, 1, 1, c], False, j == GB - 1)
                last.then_inc(sem("s_ps"), 1)

            def turn_p(it):
                pe.wait_ge(*seen("p_lo", it + 1))
                pe.wait_ge(*seen("pT_sb", it))
                o = bank16(TB).rearrange("p (l j k) -> p l j k", l=2, j=GB)
                for l in range(2):
                    for j in range(GB):
                        last = nc.tensor.transpose(o[:, l, j, :], phl[:, l, j, :], idn)
                last.then_inc(sem("pT_ps"), 1)

            def attend(it, par, odd):
                pe.wait_ge(*seen("pT_sb", it + 1))
                pe.wait_ge(*seen("o_lo", it))
                for j in range(GB):
                    c = slice(odd * P, odd * P + P)
                    last = three(bank(OB)[:, j * S:(j + 1) * S], vv[:, par, 0, j, c], vv[:, par, 1, j, c],
                                 pT[:, 0, j, :], pT[:, 1, j, :], j == 0, j == GB - 1)
                last.then_inc(sem("o_ps"), 1)

            zero = ysp[:, 2, 0:1]

            def out_project(it, wh, end=False):
                pe.wait_ge(*seen("o_lo", it + 1))
                for j in range(GB):
                    o = bank(AB + j // 2)[:, (j % 2) * D:(j % 2 + 1) * D]
                    last = three(o, oT[:, 0, j, :], oT[:, 1, j, :], wcol(whi, wh + 3 * D, D),
                                 wcol(wlo, wh + 3 * D, D), False, end and j % 2 == 1)
                last.then_inc(sem("op_ps"), 1)

            def head(g, h, hm, first=False, second=False, last2=0):
                it = g * NH + h
                scores(it)
                if second:
                    for b in range(2):
                        mm(bank(AB + b), idn, zero.broadcast_to([P, 512]), start=True, stop=False,
                           skip_group_check=True)
                elif not first:
                    out_project(it - 2, (h - 2) * HW)
                if last2 != 2:
                    project(0, (h + 1) * HW)
                if not first:
                    turn_p(it - 1)
                if last2 != 2:
                    project(1, (h + 1) * HW)
                if not first:
                    attend(it - 1, ((hm - 1) % 4) // 2, (hm - 1) % 2)
                if not last2:
                    pe.wait_ge(sem("v_lo"), it + 2)
                    values((h - hm % 2 + 2) * HW, hm % 2)

            def attention(g):
                pe.wait_ge(*seen("xb_xT", g * GB + GB))
                project(0, 0)
                values(0, 0)
                project(1, 0)
                pe.wait_ge(sem("v_lo"), g * NH + 1)
                values(0, 1)
                head(g, 0, 0, first=True)
                head(g, 1, 1, second=True)
                with pe.Fori(0, 3) as t:
                    for u in range(4):
                        head(g, t * 4 + (2 + u), (2 + u) % 4)
                head(g, 14, 2, last2=1)
                head(g, 15, 3, last2=2)
                out_project(g * NH + 14, 14 * HW)
                turn_p(g * NH + 15)
                attend(g * NH + 15, 1, 1)
                out_project(g * NH + 15, 15 * HW, end=True)

            def router(g):
                turn_x(g * 2 + 1, 0)
                turn_x(g * 2 + 2, 1)
                for j in range(GB):
                    if j % 2 == 0:
                        pe.wait_ge(sem("rms_xT"), g * 2 + j // 2 + 1)
                    for k in range(KC):
                        xh, xl = (xT[:, l, k, j * S:(j + 1) * S] for l in range(2))
                        three(bank(OB)[:, j * NE:(j + 1) * NE], xh, xl, grw[:, 0, k, :], grw[:, 1, k, :],
                              k == 0, False)
                        last = mm(bank(OB)[:, j * NE:(j + 1) * NE], xl, grw[:, 1, k, :], start=False,
                                  stop=k == KC - 1, skip_group_check=True)
                last.then_inc(sem("rt_ps"), 1)
                pe.wait_ge(sem("stage_cut"), UNITS + 1)
                pe.wait_ge(sem("sel_in"), 16)
                gate(g, 0)
                up(g, 0)
                gate(g, 1)
                up(g, 1)
                pe.wait_ge(sem("rt_cat"), g + 1)
                for j in range(GB):
                    last = nc.tensor.transpose(bank16(OB)[:, j * P:(j + 1) * P], wcat[:, j, :], idn)
                last.then_inc(sem("wT_ps"), 1)
                pe.wait_ge(sem("wT_sb"), g + 1)

            pe.wait_ge(sem("idn_in"), 16)
            x1_turn(0, 0)
            pe.wait_ge(sem("stage_cut"), 1)
            cross("pe", steps, 0, False)
            pe.wait_ge(sem("stage_cut"), UNITS - HEADCUTS + 1)
            pe.wait_ge(sem("mask_in"), 32)
            attention(0)
            with pe.Fori(0, NG - 1) as g:
                router(g)
                cross("pe", steps, g, True)
                attention(g + 1)
            router(NG - 1)
            last_experts("pe", pe, steps)

        @block.scalar
        def _(act):
            prime(act, "act")
            A = nc.scalar.activation

            def x1_norm(i, j):
                act.wait_ge(sem("xa_xn"), i + 1)
                A(xs[:, 0, :], xn, ACT.Copy).then_inc(sem("xa_xh"), 1)

            def x1_turn(i, j):
                act.wait_ge(sem("xa_xTp"), i + 1)
                A(xsT.rearrange("p l k t -> p (l k t)"), bank16(XF)[:, 0:512], ACT.Copy).then_inc(
                    sem("xa_xT"), 1)

            def x1_square(i, j):
                act.wait_ge(sem("xa_qk"), i + 1)
                A(sq, qk, ACT.Square).then_inc(sem("xa_sq"), 1)

            def x1_hi(i, j):
                act.wait_ge(sem("xa_n"), i + 1)
                A(cat[:, 0:16, 0, :, :], qk[:, 0:16, :].unsqueeze(2).broadcast_to([P, 16, 2, XD]), ACT.Copy)
                A(cat[:, 16:32, :, 0, :], qk[:, 16:32, :].unsqueeze(2).broadcast_to([P, 16, 2, XD]),
                  ACT.Copy).then_inc(sem("xa_hi"), 1)

            def cat_q(i, j):
                act.wait_ge(sem("xa_catq"), i + 1)
                act.wait_ge(*seen("xa_sT", i * NQ))
                A(catT[:, 0].rearrange("p h t -> p (h t)"), bank16(XF), ACT.Copy).then_inc(
                    sem("xa_cq"), 1)

            def cat_k(i, j):
                act.wait_ge(*seen("xa_catp", i + 1))
                A(catT[:, 1].rearrange("p h t -> p (h t)"), bank16(XF), ACT.Copy).then_inc(
                    sem("xa_ck"), 1)

            def x2_values(i, j):
                act.wait_ge(sem("xa_v"), i + 1)
                act.wait_ge(*seen("xa_pv", i * NQ))
                for s in range(2):
                    last = A(vs[:, 0, :, s, 0:XD], vf.rearrange("p (h d) -> p h d", d=XD), ACT.Copy,
                             scale=cs[:, C_SEG + s:C_SEG + s + 1])
                last.then_inc(sem("xa_vh"), 1)

            def x2_maxima(i, q):
                act.wait_ge(*seen("xa_mTp", i * NQ + q + 1))
                act.wait_ge(*seen("xa_sT", i * NQ + q))
                A(shift[0:2, :], bank16(XS)[0:2, 0:512], ACT.Copy).then_inc(sem("xa_mT"), 1)

            def x2_exp(i, q):
                n = i * NQ + q
                act.wait_ge(*seen("xa_sT", n + 1))
                act.wait_ge(*seen("xa_pl", n))
                A(xp, bank(XS), ACT.Exp, bias=ln_ps, scale=XD ** -0.5).then_inc(sem("xa_e"), 1)

            def p_hi(i, q):
                n = i * NQ + q
                act.wait_ge(*seen("xa_e", n + 1))
                act.wait_ge(*seen("xa_pv", n))
                A(xpT[:, 0].rearrange("p h q -> p (h q)"), xp, ACT.Copy).then_inc(sem("xa_ph"), 1)

            def x2_context(i, q):
                act.wait_ge(sem("xa_c"), i * NQ + q + 1)
                if q == 0:
                    act.wait_ge(*seen("xa_cTp", i))
                A(context(0, q), ctx_sum, ACT.Copy).then_inc(sem("xa_ch"), 1)

            def x3_turn_c(i, j, beside):
                act.wait_ge(*seen("xa_cTp", i + 1))
                act.wait_ge(*seen("xb_tp", i))
                A(xcT.rearrange("p l k t -> p (l k t)"), bank16(XP)[:, 0:512], ACT.Copy).then_inc(
                    sem("xa_cT"), 1)

            def x3_split(i, j, beside):
                act.wait_ge(sem("xb_zr"), i + 1)
                act.wait_ge(sem("xb_r_rs"), i + 1)
                A(zs[:, 0, :], z, ACT.Copy, scale=b_rs2).then_inc(sem("xb_zh"), 1)

            def turn_z(i, j, beside):
                act.wait_ge(*seen("xb_tp", i + 1))
                A(xTn[:, :, :, j * S:(j + 1) * S],
                  bank16(XS)[:, 0:512].rearrange("p (l k t) -> p l k t", l=2, k=KC), ACT.Copy).then_inc(
                    sem("xb_xT"), 1)

            def gate(g, c):
                n = g * NC + c
                act.wait_ge(sem("g_ps"), n + 1)
                act.wait_ge(*seen("me_v", n))
                A(me_t, bank(GBK), ACT.Tanh, scale=0.5 / WS).then_inc(sem("me_t"), 1)

            def cut(g, c):
                n = g * NC + c
                act.wait_ge(*seen("me_v", n + 1))
                act.wait_ge(*seen("d_ps", n))
                A(me_hl[:, 0, :], me_p, ACT.Copy).then_inc(sem("me_hi"), 1)

            def cut_unit(u):
                act.wait_ge(sem(f"stage_in{u % 2}"), 16 * (u // 2 + 1))
                A(whi[:, u * UW:(u + 1) * UW], stage[u % 2], ACT.Copy, scale=WS).then_inc(
                    sem("stage_hi"), 1)

            steps = {"1:x_hi": x1_norm, "1:turn": x1_turn, "1:square": x1_square, "1:qk_hi": x1_hi,
                     "1:cat_q": cat_q, "1:cat_k": cat_k, "2:v_hi": x2_values, "2:maxima": x2_maxima,
                     "2:exp": x2_exp, "2:p_hi": p_hi, "2:c_hi": x2_context, "3:turn_c": x3_turn_c,
                     "3:z_hi": x3_split, "3:turn_z": turn_z, "e:gate": gate,
                     "e:m_hi": cut, "w:cut": cut_unit}

            def hi_q(w, it):
                act.wait_ge(sem(("q_ps", "k_ps")[w]), it + 1)
                A(qkT[:, w, 0, :], bank(QB + w), ACT.Copy, scale=1.0 / WS).then_inc(
                    sem(("q_hi", "k_hi")[w]), 1)

            def hi_v(cnt, par, half):
                act.wait_ge(sem("v_ps"), cnt)
                A(vv[:, par, 0, 2 * half:2 * half + 2, :].rearrange("p j c -> p (j c)"), bank(VB),
                  ACT.Copy, scale=1.0 / WS).then_inc(sem("v_hi"), 1)

            def hi_o(it):
                act.wait_ge(*seen("o_ps", it + 1))
                act.wait_ge(*seen("op_ps", it))
                A(oT[:, 0].rearrange("p j k -> p (j k)"), bank(OB), ACT.Copy,
                  scale=1.0 / PS).then_inc(sem("o_hi"), 1)

            def cut_beside(h, par):
                act.wait_ge(sem(f"stage_in{par}"), h * 8 + (16 * ((UNITS - HEADCUTS) // 2 + 1) - 8 * par))
                apart(act)
                A(whi[:, bass.ds(h * UW + (UNITS - HEADCUTS) * UW, UW)], stage[par], ACT.Copy,
                  scale=WS).then_inc(sem("stage_hi"), 1)

            def head(g, h, hm, first=False, last2=0, cuts=False):
                it = g * NH + h
                act.wait_ge(sem("m_neg"), it + 1)
                act.wait_ge(*seen("p_lo", it))
                for j in range(GB):
                    last = A(pr[:, j, :], bank(SB_)[:, j * S:(j + 1) * S], ACT.Exp,
                             bias=nm4[:, j:j + 1], scale=QHD ** -0.5, accum_out=es4[:, j:j + 1])
                last.then_inc(sem("p_exp"), 1)
                if last2 != 2:
                    hi_q(0, it + 1)
                if cuts:
                    cut_beside(h, hm % 2)
                if last2 != 2:
                    hi_q(1, it + 1)
                if not first:
                    hi_o(it - 1)
                if not last2:
                    hi_v(it + 3, ((hm + 2) % 4) // 2, hm % 2)
                act.wait_ge(sem("p_n"), it + 1)
                act.wait_ge(*seen("pT_ps", it))
                A(phl[:, 0], pr, ACT.Copy).then_inc(sem("p_hi"), 1)

            def attention(g, cuts=False):
                hi_q(0, g * NH)
                hi_v(g * NH + 1, 0, 0)
                hi_q(1, g * NH)
                hi_v(g * NH + 2, 0, 1)
                head(g, 0, 0, first=True, cuts=cuts)
                head(g, 1, 1, cuts=cuts)
                with act.Fori(0, 3) as t:
                    for u in range(4):
                        head(g, t * 4 + (2 + u), (2 + u) % 4, cuts=cuts)
                head(g, 14, 2, last2=1)
                head(g, 15, 3, last2=2)
                hi_o(g * NH + 15)

            def router(g):
                for half in range(2):
                    act.wait_ge(sem("hid"), g * 2 + half + 1)
                    for j in (2 * half, 2 * half + 1):
                        last = A(xr[:, j, :], hid[:, j, :], ACT.Square, accum_out=ss4[:, j:j + 1])
                    last.then_inc(sem("rms_ss"), 1)
                for half in range(2):
                    js = slice(2 * half, 2 * half + 2)
                    act.wait_ge(sem("rms_xr"), g * 2 + half + 1)
                    A(xrs[:, 0, js], xr[:, js], ACT.Copy).then_inc(sem("rms_hi"), 1)
                act.wait_ge(sem("rt_sub"), g + 1)
                A(rt_e, rt_l, ACT.Exp, scale=1.0 / WS).then_inc(sem("rt_exp"), 1)

            x1_norm(0, 0)
            act.wait_ge(sem("cst_in"), 16)
            A(gt[:, 0:2], cs[:, C_GATE:C_GATE + 2], ACT.Tanh).then_inc(sem("gates"), 1)
            A(grw[:, 0].rearrange("p k e -> p (k e)"), cs[:, C_RT:C_RT + KC * NE], ACT.Copy,
              scale=WS).then_inc(sem("gr_hi"), 1)
            act.wait_ge(sem("gates"), 1)
            A(gt[:, 2:3], gt[:, 1:2], ACT.Copy, scale=1.0 / WS).then_inc(sem("gates"), 1)
            act.wait_ge(sem("centred"), 3)
            A(wahi[:, :], stage_a, ACT.Copy, scale=WS).then_inc(sem("wa_hi"), 1)
            cross("act", steps, 0, False)
            attention(0, True)
            with act.Fori(0, NG - 1) as g:
                router(g)
                cross("act", steps, g, True)
                attention(g + 1)
            router(NG - 1)
            last_experts("act", act, steps)

        @block.gpsimd
        def _(pool):
            prime(pool, "pool")
            TT = nc.gpsimd.tensor_tensor

            def rsqrt(out, tmp, in_, scale, eps, w, name, count):
                nc.gpsimd.tensor_scalar(tmp, in_, scale, eps, ALU.mult, ALU.add).then_inc(
                    sem(name + "_ve"), 1)
                pool.wait_ge(sem(name + "_ve"), count)
                TT(out, tmp, mhalf[:, 0:w], ALU.pow).then_inc(sem(name + "_rs"), 1)

            def x1_stats(i, j):
                pool.wait_ge(sem("xa_mv"), i + 1)
                apart(pool)
                rsqrt(a_rs, a_ve, a_mv[:, 1:2], 1.0, 1e-5, 1, "xa", i + 1)
                if j == 0:
                    nc.gpsimd.memset(shift, 0.0)

            def y_cut(i, j):
                pool.wait_ge(sem("y_in"), i * 16 + 16)
                pool.wait_ge(*seen("xa_kvp", i))
                apart(pool)
                nc.gpsimd.tensor_copy(ysp[:, 0, 0:MAIN], y_t[:, 0:MAIN])
                nc.gpsimd.tensor_copy(ysp[:, 2, MAIN:S], y_t[:, MAIN:S]).then_inc(sem("xa_yh"), 1)
                pool.wait_ge(sem("xa_yh"), i + 1)
                TT(ysp[:, 1, 0:MAIN], y_t[:, 0:MAIN], ysp[:, 0, 0:MAIN], ALU.subtract)
                TT(ysp[:, 3, MAIN:S], y_t[:, MAIN:S], ysp[:, 2, MAIN:S],
                   ALU.subtract).then_inc(sem("xa_yl"), 1)

            def x1_turn(i, j):
                pool.wait_ge(sem("xa_xh"), i + 1)
                TT(xs[:, 1, :], xn, xs[:, 0, :], ALU.subtract).then_inc(sem("xa_xl"), 1)

            def x1_hi(i, j):
                pool.wait_ge(sem("xa_hi"), i + 1)
                TT(cat[:, 0:16, 1, :, :], qk[:, 0:16, :].unsqueeze(2).broadcast_to([P, 16, 2, XD]),
                   cat[:, 0:16, 0, :, :], ALU.subtract)
                TT(cat[:, 16:32, :, 1, :], qk[:, 16:32, :].unsqueeze(2).broadcast_to([P, 16, 2, XD]),
                   cat[:, 16:32, :, 0, :], ALU.subtract).then_inc(sem("xa_lo"), 1)

            def x2_values(i, j):
                pool.wait_ge(*seen("xa_pv", i * NQ))
                apart(pool)
                for s in range(2):
                    nc.gpsimd.tensor_copy(vs[:, 0, :, s, XD:XD + 1],
                                          cs[:, C_SEG + s:C_SEG + s + 1].unsqueeze(1)
                                          .broadcast_to([P, XH, 1]))
                nc.gpsimd.memset(vs[:, 1, :, :, XD:XD + 1], 0.0).then_inc(sem("xa_ones"), 1)

            def x2_exp(i, q):
                pool.wait_ge(sem("xa_ph"), i * NQ + q + 1)
                TT(xpT[:, 1].rearrange("p h q -> p (h q)"), xp, xpT[:, 0].rearrange("p h q -> p (h q)"),
                   ALU.subtract).then_inc(sem("xa_pl"), 1)

            def x3_stats(i, j, beside):
                pool.wait_ge(sem("xb_mv"), i + 1)
                apart(pool)
                rsqrt(rs4[:, j:j + 1], b_ve, mv4[:, j, 1:2], 1.0, 1e-5, 1, "xb", i + 1)

            def x3_rms(i, j, beside):
                pool.wait_ge(sem("xb_mv"), i + 1)
                apart(pool)
                rsqrt(b_rs2, b_ve2, mv4[:, j, 1:2], 1.0 + 1e-6, 1e-6 * 1e-5, 1, "xb_r", i + 1)

            def cut(g, c):
                pool.wait_ge(sem("me_hi"), g * NC + c + 1)
                TT(me_hl[:, 1, :], me_p, me_hl[:, 0, :], ALU.subtract).then_inc(sem("me_lo"), 1)

            steps = {"1:x_rs": x1_stats, "1:y_cut": y_cut, "1:x_lo": x1_turn, "1:qk_lo": x1_hi,
                     "2:v_ones": x2_values, "2:p_lo": x2_exp, "3:x_rs": x3_stats, "3:z_rs": x3_rms,
                     "e:m_lo": cut}

            def attention(g):
                with pool.Fori(0, NH - 1) as h:
                    it = g * NH + h
                    pool.wait_ge(sem("p_r"), it + 1)
                    TT(pr, pr, eq4.unsqueeze(2).broadcast_to([P, GB, S]), ALU.mult).then_inc(
                        sem("p_n"), 1)
                    pool.wait_ge(sem("p_hi"), it + 1)
                    TT(phl[:, 1], pr, phl[:, 0], ALU.subtract).then_inc(sem("p_lo"), 1)

            def router(g, more=True):
                for half in range(2):
                    js = slice(2 * half, 2 * half + 2)
                    pool.wait_ge(sem("rms_ss"), g * 2 + half + 1)
                    apart(pool)
                    rsqrt(rrs4[:, js], rve4[:, js], ss4[:, js], 1.0 / D, 1e-6, 2, "rms", g * 2 + half + 1)
                nc.gpsimd.memset(wcat, 0.0).then_inc(sem("zeroed"), 1)
                pool.wait_ge(sem("zeroed"), g + 1)
                apart(pool)
                nc.gpsimd.memset(wcat[:, :, NE:NE + 1], 1.0).then_inc(sem("one_set"), 1)
                if more:
                    y_cut(g * GB + GB, 0)

            nc.gpsimd.memset(ln_ps, float(np.log(PS))).then_inc(sem("half_set"), 1)
            nc.gpsimd.memset(mhalf[:, :], -0.5).then_inc(sem("half_set"), 1)
            nc.gpsimd.memset(ysp[:, :, :], 0.0).then_inc(sem("half_set"), 1)
            pool.wait_ge(sem("half_set"), 3)
            x1_stats(0, 0)
            x1_turn(0, 0)
            pool.wait_ge(sem("cst_in"), 16)
            cross("pool", steps, 0, False)
            attention(0)
            with pool.Fori(0, NG - 1) as g:
                router(g)
                cross("pool", steps, g, True)
                attention(g + 1)
            router(NG - 1, more=False)
            last_experts("pool", pool, steps)

        @block.vector
        def _(dve):
            prime(dve, "dve")
            V = nc.vector
            STT, TT = V.scalar_tensor_tensor, V.tensor_tensor
            qkf = qk.rearrange("p h d -> p (h d)")

            def x1_stats(i, j):
                if j == 0:
                    dve.wait_ge(sem("x_in"), i * 4 + 16)
                V.bn_stats(a_st, x1[:, j, :]).then_inc(sem("xa_st"), 1)

            def x_mean(i, j):
                dve.wait_ge(sem("xa_st"), i + 1)
                apart(dve)
                V.bn_aggr(a_mv, a_st).then_inc(sem("xa_mv"), 1)

            def x1_norm(i, j):
                dve.wait_ge(sem("xa_rs"), i + 1)
                dve.wait_ge(*seen("xa_catp", i))
                V.tensor_scalar(xn, x1[:, j, :], a_mv[:, 0:1], a_rs, ALU.subtract, ALU.mult).then_inc(
                    sem("xa_xn"), 1)

            def x1_query(i, j):
                dve.wait_ge(*seen("xa_kvp", i + 1))
                dve.wait_ge(*seen("xa_vl", i))
                STT(vf, bank(XF)[:, 256:512], 1.0 / WS, cs[:, 512:768], ALU.mult, ALU.add).then_inc(
                    sem("xa_v"), 1)

            def k_row(i, j):
                dve.wait_ge(*seen("xa_kvp", i + 1))
                dve.wait_ge(sem("xa_v"), i + 1)
                STT(qkf[:, 256:512], bank(XF)[:, 0:256], 1.0 / WS, cs[:, 256:512], ALU.mult,
                    ALU.add).then_inc(sem("xa_k"), 1)

            def x1_square(i, j):
                dve.wait_ge(sem("xa_qp"), i + 1)
                STT(qkf[:, 0:256], bank(XF)[:, 0:256], 1.0 / WS, cs[:, 0:256], ALU.mult,
                    ALU.add).then_inc(sem("xa_qk"), 1)

            def newton(i, j, step):
                yi, vi = a_y.bitcast(I32), a_v.bitcast(I32)
                if step == 0:
                    dve.wait_ge(sem("xa_sq"), i + 1)
                else:
                    dve.wait_ge(sem("xa_nt"), i * NEWTON + step)
                if step == 0:
                    made = V.tensor_reduce(a_ss, sq, AX.X, ALU.add)
                elif step == 1:
                    made = V.tensor_scalar(a_v, a_ss, 1.0 / XD, 1e-6, ALU.mult, ALU.add)
                elif step == 2:
                    made = V.tensor_scalar(yi, vi, 1, None, ALU.arith_shift_right)
                elif step == 3:
                    made = V.tensor_scalar(yi, yi, -1, 0x5f3759df, ALU.mult, ALU.add)
                elif step % 3 == 1:
                    made = TT(a_t, a_y, a_y, ALU.mult)
                elif step % 3 == 2:
                    made = STT(a_t, a_t, -0.5, a_v, ALU.mult, ALU.mult)
                else:
                    made = STT(a_y, a_t, 1.5, a_y, ALU.add, ALU.mult)
                made.then_inc(sem("xa_nt"), 1)

            def x1_scale(i, j):
                dve.wait_ge(sem("xa_nt"), i * NEWTON + NEWTON)
                TT(qk, qk, a_y.unsqueeze(2).broadcast_to([P, 32, XD]), ALU.mult).then_inc(sem("xa_n1"), 1)

            qk2 = qk.rearrange("p (w h) d -> p w h d", w=2)

            def qk_w(i, j):
                dve.wait_ge(sem("xa_n1"), i + 1)
                TT(qk2, qk2, ln_rows(C_LNW), ALU.mult).then_inc(sem("xa_n2"), 1)

            def qk_b(i, j):
                dve.wait_ge(sem("xa_n2"), i + 1)
                TT(qk2, qk2, ln_rows(C_LNB), ALU.add).then_inc(sem("xa_n"), 1)

            def x2_scores(i, q):
                n = i * NQ + q
                sc = bank(XS).rearrange("p (h k) -> p h k", h=QH)
                dve.wait_ge(sem("xa_s"), n + 1)
                for s, k in SEGS:
                    last = V.tensor_reduce(a_mx[:, :, s], sc[:, :, k], AX.X, ALU.max)
                last.then_inc(sem("xa_mx"), 1)

            def negate(i, q):
                n = i * NQ + q
                dve.wait_ge(sem("xa_mx"), n + 1)
                dve.wait_ge(*seen("xa_mTp", n))
                V.tensor_scalar(a_mn, a_mx, -1.0, None, ALU.mult).then_inc(sem("xa_mn"), 1)

            def x2_values(i, j):
                dve.wait_ge(sem("xa_vh"), i + 1)
                for s in range(2):
                    last = STT(vs[:, 1, :, s, 0:XD], vf.rearrange("p (h d) -> p h d", d=XD),
                               cs[:, C_SEG + s:C_SEG + s + 1], vs[:, 0, :, s, 0:XD], ALU.mult,
                               ALU.subtract)
                last.then_inc(sem("xa_vl"), 1)

            def x2_context(i, q):
                n = i * NQ + q
                dve.wait_ge(*seen("xa_pv", n + 1))
                V.reciprocal(a_r, ctx_ps[:, :, :, XD]).then_inc(sem("xa_r"), 1)

            def c_over(i, q):
                n = i * NQ + q
                dve.wait_ge(sem("xa_r"), n + 1)
                TT(ctx_ps[:, :, :, 0:XD], ctx_ps[:, :, :, 0:XD],
                   a_r.unsqueeze(3).broadcast_to([P, QH, 2, XD]), ALU.mult).then_inc(sem("xa_t"), 1)

            def c_add(i, q):
                n = i * NQ + q
                dve.wait_ge(sem("xa_t"), n + 1)
                V.tensor_reduce(ctx_sum, ctx_ps[:, :, :, 0:XD].rearrange("p h s c -> p h c s"), AX.X,
                                ALU.add).then_inc(sem("xa_c"), 1)

            def c_lo(i, q):
                n = i * NQ + q
                dve.wait_ge(sem("xa_ch"), n + 1)
                TT(context(1, q), ctx_sum, context(0, q), ALU.subtract).then_inc(
                    sem("xa_cl"), 1)

            def x3_x1(i, j, beside):
                dve.wait_ge(sem("xa_yp"), i + 1)
                dve.wait_ge(*seen("xb_tp", i))
                STT(z, bank(XP)[:, 0:D], 1.0 / WS, cs[:, C_BO:C_BO + D], ALU.mult, ALU.add).then_inc(
                    sem("xa_o"), 1)

            def new_x(i, j, beside):
                dve.wait_ge(*seen("xa_o", i + 1))
                STT(x1[:, j, :], z, gt[:, 0:1], x1[:, j, :], ALU.mult, ALU.add).then_inc(sem("xa_x1"), 1)

            def x3_stats(i, j, beside):
                dve.wait_ge(sem("xa_x1"), i + 1)
                V.bn_stats(st4[:, j, :], x1[:, j, :]).then_inc(sem("xb_st"), 1)

            def z_mean(i, j, beside):
                dve.wait_ge(sem("xb_st"), i + 1)
                apart(dve)
                V.bn_aggr(mv4[:, j, :], st4[:, j, :]).then_inc(sem("xb_mv"), 1)

            def x3_rms(i, j, beside):
                dve.wait_ge(sem("xb_mv"), i + 1)
                STT(z, x1[:, j, :], mv4[:, j, 0:1], cs[:, C_LN1:C_LN1 + D], ALU.subtract,
                    ALU.mult).then_inc(sem("xb_zr"), 1)

            def z_lo(i, j, beside):
                dve.wait_ge(sem("xb_zh"), i + 1)
                STT(zs[:, 1, :], z, b_rs2, zs[:, 0, :], ALU.mult, ALU.subtract).then_inc(sem("xb_zl"), 1)

            def gate(g, c):
                dve.wait_ge(sem("me_t"), g * NC + c + 1)
                STT(me_t, me_t, 1.0, bank(GBK), ALU.add, ALU.mult).then_inc(sem("me_a"), 1)

            def up(g, c):
                n = g * NC + c
                dve.wait_ge(sem("u_ps"), n + 1)
                dve.wait_ge(*seen("me_a", n + 1))
                TT(me_t, me_t, bank(UBK), ALU.mult).then_inc(sem("me_b"), 1)

            def weight(g, c):
                n = g * NC + c
                dve.wait_ge(sem("w_ps"), n + 1)
                dve.wait_ge(*seen("me_b", n + 1))
                dve.wait_ge(*seen("me_lo", n))
                TT(me_p, me_t, bank(WBK), ALU.mult).then_inc(sem("me_v"), 1)

            hf = hid.rearrange("p j d -> p (j d)")

            def finish(g):
                dve.wait_ge(*seen("d_ps", g * NC + NC))
                dve.wait_ge(sem("z"), g * 2 + 2)
                STT(hf, bank(AB, 2), gt[:, 2:3], hf, ALU.mult, ALU.add).then_inc(sem("fin"), 1)

            def cut_unit(u):
                dve.wait_ge(sem("stage_hi"), u + 1)
                c = slice(u * UW, (u + 1) * UW)
                STT(wlo[:, c], stage[u % 2], WS, whi[:, c], ALU.mult, ALU.subtract).then_inc(
                    sem("stage_cut"), 1)

            steps = {"1:stats": x1_stats, "1:mean": x_mean, "1:x_norm": x1_norm, "1:v_row": x1_query,
                     "1:k_row": k_row, "1:q_row": x1_square, "1:newton": newton, "1:qk_rs": x1_scale,
                     "1:qk_w": qk_w, "1:qk_b": qk_b, "2:max": x2_scores, "2:negate": negate,
                     "2:v_lo": x2_values, "2:c_sum": x2_context, "2:c_over": c_over, "2:c_add": c_add,
                     "2:c_lo": c_lo, "3:out": x3_x1, "3:new_x": new_x, "3:stats": x3_stats,
                     "3:mean": z_mean, "3:z_norm": x3_rms, "3:z_lo": z_lo, "e:gate": gate, "e:up": up,
                     "e:weight": weight, "e:finish": finish, "w:cut": cut_unit}

            def lo_q(w, it):
                dve.wait_ge(sem(("q_hi", "k_hi")[w]), it + 1)
                STT(qkT[:, w, 1, :], bank(QB + w), 1.0 / WS, qkT[:, w, 0, :], ALU.mult,
                    ALU.subtract).then_inc(sem(("q_lo", "k_lo")[w]), 1)

            def lo_v(cnt, par, half):
                dve.wait_ge(sem("v_hi"), cnt)
                js = slice(2 * half, 2 * half + 2)
                STT(vv[:, par, 1, js, :].rearrange("p j c -> p (j c)"), bank(VB), 1.0 / WS,
                    vv[:, par, 0, js, :].rearrange("p j c -> p (j c)"), ALU.mult,
                    ALU.subtract).then_inc(sem("v_lo"), 1)

            def copy_pT(it):
                dve.wait_ge(*seen("pT_ps", it + 1))
                dve.wait_ge(*seen("o_ps", it))
                V.tensor_copy(pT.rearrange("p l j k -> p (l j k)"), bank16(TB)).then_inc(sem("pT_sb"), 1)

            def lo_o(it):
                dve.wait_ge(sem("o_hi"), it + 1)
                STT(oT[:, 1].rearrange("p j k -> p (j k)"), bank(OB), 1.0 / PS,
                    oT[:, 0].rearrange("p j k -> p (j k)"), ALU.mult, ALU.subtract).then_inc(
                    sem("o_lo"), 1)

            def cut_beside(h, par):
                dve.wait_ge(sem("stage_hi"), h + (UNITS - HEADCUTS + 1))
                apart(dve)
                c = bass.ds(h * UW + (UNITS - HEADCUTS) * UW, UW)
                STT(wlo[:, c], stage[par], WS, whi[:, c], ALU.mult, ALU.subtract).then_inc(
                    sem("stage_cut"), 1)

            def head(g, h, hm, first=False, last2=0, cuts=False):
                it = g * NH + h
                dve.wait_ge(sem("s_ps"), it + 1)
                V.tensor_reduce(mx4, bank(SB_).rearrange("p (j k) -> p j k", j=GB), AX.X,
                                ALU.max).then_inc(sem("m_max"), 1)
                dve.wait_ge(sem("m_max"), it + 1)
                V.tensor_scalar(nm4, mx4, -(QHD ** -0.5), None, ALU.mult).then_inc(sem("m_neg"), 1)
                if cuts:
                    cut_beside(h - 1, (hm - 1) % 2)
                if not first:
                    copy_pT(it - 1)
                if last2 != 2:
                    lo_q(0, it + 1)
                dve.wait_ge(*seen("p_exp", it + 1))
                V.reciprocal(er4, es4).then_inc(sem("p_rec"), 1)
                dve.wait_ge(sem("p_rec"), it + 1)
                V.tensor_scalar(eq4, er4, PS, None, ALU.mult).then_inc(sem("p_r"), 1)
                if last2 != 2:
                    lo_q(1, it + 1)
                if not first and last2 != 2:
                    lo_o(it - 1)
                if not last2:
                    lo_v(it + 3, ((hm + 2) % 4) // 2, hm % 2)

            def attention(g, cuts=False):
                lo_q(0, g * NH)
                lo_v(g * NH + 1, 0, 0)
                lo_q(1, g * NH)
                lo_v(g * NH + 2, 0, 1)
                head(g, 0, 0, first=True)
                head(g, 1, 1, cuts=cuts)
                with dve.Fori(0, 3) as t:
                    for u in range(4):
                        head(g, t * 4 + (2 + u), (2 + u) % 4, cuts=cuts)
                head(g, 14, 2, last2=1, cuts=cuts)
                dve.wait_ge(sem("xb_rs"), g * GB + GB)
                dve.wait_ge(*seen("out_done", g * 16))
                for j in range(GB):
                    last = V.tensor_scalar(hid[:, j, :], x1[:, j, :], mv4[:, j, 0:1], rs4[:, j:j + 1],
                                           ALU.subtract, ALU.mult)
                last.then_inc(sem("h0"), 1)
                head(g, 15, 3, last2=2)
                it = g * NH + 15
                dve.wait_ge(sem("p_r"), it + 1)
                TT(pr, pr, eq4.unsqueeze(2).broadcast_to([P, GB, S]), ALU.mult).then_inc(sem("p_n"), 1)
                lo_o(g * NH + 14)
                dve.wait_ge(sem("p_hi"), it + 1)
                TT(phl[:, 1], pr, phl[:, 0], ALU.subtract).then_inc(sem("p_lo"), 1)
                copy_pT(g * NH + 15)
                lo_o(g * NH + 15)

            def router(g, more=True):
                dve.wait_ge(sem("h0"), g + 1)
                dve.wait_ge(*seen("op_ps", g * NH + NH))
                for half in range(2):
                    c = slice(half * 512, half * 512 + 512)
                    STT(hf[:, c], bank(AB + half), 1.0 / WS, hf[:, c], ALU.mult, ALU.add).then_inc(
                        sem("hid"), 1)
                for half in range(2):
                    dve.wait_ge(sem("rms_rs"), g * 2 + half + 1)
                    for j in (2 * half, 2 * half + 1):
                        last = STT(xr[:, j, :], hid[:, j, :], rrs4[:, j:j + 1], cs[:, C_LN2:C_LN2 + D],
                                   ALU.mult, ALU.mult)
                    last.then_inc(sem("rms_xr"), 1)

                def zrow(half):
                    js = slice(2 * half, 2 * half + 2)
                    dve.wait_ge(sem("rms_xr"), g * 2 + half + 1)
                    STT(hid[:, js, :], hid[:, js, :], gt[:, 1:2], x1[:, js, :], ALU.mult,
                        ALU.add).then_inc(sem("z"), 1)

                for half in range(2):
                    js = slice(2 * half, 2 * half + 2)
                    dve.wait_ge(sem("rms_hi"), g * 2 + half + 1)
                    TT(xrs[:, 1, js], xr[:, js], xrs[:, 0, js], ALU.subtract).then_inc(sem("rms_lo"), 1)
                for half in range(2):
                    if half == 0:
                        zrow(0)
                    dve.wait_ge(sem("rms_tp"), g * 2 + half + 1)
                    V.tensor_copy(xT[:, :, :, half * 256:half * 256 + 256],
                                  bank16(VB + half).rearrange("p (l k t) -> p l k t", l=2, k=KC)).then_inc(
                        sem("rms_xT"), 1)
                zrow(1)
                RC = 14
                step = [0]

                def link(ins):
                    step[0] += 1
                    ins.then_inc(sem("rt_step"), 1)
                    dve.wait_ge(sem("rt_step"), g * RC + step[0])
                    apart(dve)

                b16 = [P, GB, NE]
                dve.wait_ge(sem("rt_ps"), g + 1)
                lg = bank(OB)[:, 0:GB * NE].rearrange("p (j e) -> p j e", j=GB)
                link(V.tensor_reduce(rt_mx, lg, AX.X, ALU.max))
                TT(rt_l, lg, rt_mx.unsqueeze(2).broadcast_to(b16), ALU.subtract).then_inc(sem("rt_sub"), 1)
                dve.wait_ge(sem("rt_exp"), g + 1)
                link(V.tensor_reduce(rt_s, rt_e, AX.X, ALU.add))
                link(V.reciprocal(rt_r, rt_s))
                link(TT(rt_p, rt_e, rt_r.unsqueeze(2).broadcast_to(b16), ALU.mult))
                for j in range(GB):
                    last = V.max(rt_8[:, j, :], rt_p[:, j, :])
                link(last)
                for j in range(GB):
                    last = V.max_index(rt_ix[:, j, :], rt_8[:, j, :], rt_p[:, j, :])
                link(last)
                link(V.tensor_copy(rt_xf, rt_ix[:, :, 0:TOPK]))
                gate(g, 0)
                link(TT(rt_eq, cs[:, C_IOTA:C_IOTA + NE].unsqueeze(1).unsqueeze(3)
                        .broadcast_to([P, GB, NE, TOPK]),
                        rt_xf.unsqueeze(2).broadcast_to([P, GB, NE, TOPK]), ALU.is_equal))
                link(V.tensor_reduce(rt_m, rt_eq, AX.X, ALU.add))
                link(TT(rt_w, rt_p, rt_m, ALU.mult))
                up(g, 0)
                if more:
                    x1_stats(g * GB + GB, 0)
                link(V.tensor_reduce(rt_s2, rt_w, AX.X, ALU.add))
                if more:
                    x_mean(g * GB + GB, 0)
                link(V.reciprocal(rt_r2, rt_s2))
                link(TT(rt_f, rt_w, rt_r2.unsqueeze(2).broadcast_to(b16), ALU.mult))
                dve.wait_ge(sem("one_set"), g + 1)
                apart(dve)
                link(V.tensor_copy(wcat[:, :, 0:NE], rt_f))
                assert step[0] == RC
                TT(wcat[:, :, 32:32 + NE], rt_f, wcat[:, :, 0:NE], ALU.subtract).then_inc(sem("rt_cat"), 1)
                if more:
                    x1_norm(g * GB + GB, 0)
                dve.wait_ge(sem("wT_ps"), g + 1)
                V.tensor_copy(wT[:, :], bank16(OB)[:, 0:T]).then_inc(sem("wT_sb"), 1)

            x1_stats(0, 0)
            x_mean(0, 0)
            x1_norm(0, 0)
            dve.wait_ge(sem("cst_in"), 16)
            dve.wait_ge(sem("wa_in"), 16)
            centred = [(stage_a[:, 0:512], 0, 32), (stage_a[:, 512:768], 32, 16),
                       (stage_a[:, 1024:1280], 48, 16), (cs[:, 0:512], 64, 32)]
            for w, o, n in centred:
                last = V.tensor_reduce(w_mu[:, o:o + n], w.rearrange("p (h d) -> p h d", d=XD), AX.X, ALU.add)
            last.then_inc(sem("centred"), 1)
            dve.wait_ge(sem("centred"), 1)
            V.tensor_scalar(w_mu, w_mu, -1.0 / XD, None, ALU.mult).then_inc(sem("centred"), 1)
            dve.wait_ge(sem("centred"), 2)
            for w, o, n in centred:
                wr = w.rearrange("p (h d) -> p h d", d=XD)
                last = TT(wr, wr, w_mu[:, o:o + n].unsqueeze(2).broadcast_to([P, n, XD]), ALU.add)
            last.then_inc(sem("centred"), 1)
            dve.wait_ge(sem("gr_hi"), 1)
            STT(grw[:, 1].rearrange("p k e -> p (k e)"), cs[:, C_RT:C_RT + KC * NE], WS,
                grw[:, 0].rearrange("p k e -> p (k e)"), ALU.mult, ALU.subtract)
            dve.wait_ge(sem("centred"), 3)
            dve.wait_ge(sem("wa_hi"), 1)
            STT(walo[:, :], stage_a, WS, wahi[:, :], ALU.mult, ALU.subtract).then_inc(
                sem("stage_cut"), 1)
            dve.wait_ge(sem("gates"), 2)
            cross("dve", steps, 0, False)
            attention(0, True)
            with dve.Fori(0, NG - 1) as g:
                router(g)
                cross("dve", steps, g, True)
                attention(g + 1)
            router(NG - 1, more=False)
            last_experts("dve", dve, steps)


def kernel(x, ctx_1024, g_xattn, g_ffn, L0_xattn_Wq, L0_xattn_bq, L0_xattn_Wk, L0_xattn_bk,
           L0_xattn_Wv, L0_xattn_bv, L0_xattn_Wkv_dca, L0_xattn_bkv_dca, L0_xattn_qn_w, L0_xattn_qn_b,
           L0_xattn_kn_w, L0_xattn_kn_b, L0_xattn_kn_dca_w, L0_xattn_kn_dca_b, L0_xattn_Wo, L0_xattn_bo,
           L0_ffn_positions, L0_ffn_ln1_w, L0_ffn_ln2_w, L0_ffn_q_w, L0_ffn_kv_w, L0_ffn_o_w,
           L0_ffn_gate_w, L0_ffn_w1, L0_ffn_w2, L0_ffn_sh_gu_w, L0_ffn_sh_down_w):
    import numpy as np
    import ml_dtypes
    import concourse.bacc as bacc
    from concourse import mybir
    from concourse.bass_utils import run_bass_kernel_spmd as run

    f = lambda a: np.asarray(a, dtype=np.float32)
    wkv = np.concatenate([f(L0_xattn_Wk), f(L0_xattn_Wv)], 1).reshape(P, XH, 2, XD)
    wkv = wkv.transpose(0, 2, 1, 3).reshape(P, 512)
    bkv = np.concatenate([f(L0_xattn_bk), f(L0_xattn_bv)]).reshape(XH, 2, XD).transpose(1, 0, 2).reshape(512)
    two = lambda w: f(w).reshape(KC, P, D).transpose(1, 0, 2).reshape(P, KC * D)
    wa = np.concatenate([two(L0_xattn_Wq), wkv, f(L0_xattn_Wkv_dca), two(L0_xattn_Wo)], 1)
    inT = lambda w: f(w).reshape(-1, P, KC, P).transpose(3, 0, 2, 1)
    q = inT(f(L0_ffn_q_w).reshape(NH, QHD, D)[:, :HD].reshape(NH * HD, D))
    kv = f(L0_ffn_kv_w)
    k, v = inT(kv[:NH * HD]), inT(kv[NH * HD:2 * NH * HD])
    o = f(L0_ffn_o_w).reshape(D, NH, HD).transpose(2, 1, 0)
    heads = np.concatenate([w.reshape(P, NH, D) for w in (q, k, v, o)], 2).reshape(P, NH * HW)
    w1, w2 = f(L0_ffn_w1), f(L0_ffn_w2)
    sgu = f(L0_ffn_sh_gu_w)
    pad = np.zeros((NC * P - NE * EI - SHI, D), np.float32)
    wg = inT(np.concatenate([w1[:, :EI].reshape(-1, D), sgu[:SHI], pad]))
    wu = inT(np.concatenate([w1[:, EI:].reshape(-1, D), sgu[SHI:], pad]))
    wd = np.concatenate([w2.transpose(0, 2, 1).reshape(-1, D), f(L0_ffn_sh_down_w).T, pad])
    wd = wd.reshape(NC, P, D).transpose(1, 0, 2)
    chunks = np.concatenate([wg.reshape(P, NC, D), wu.reshape(P, NC, D), wd], 2).reshape(P, NC * CW)
    wall = np.ascontiguousarray(np.concatenate([heads, chunks], 1))
    c = np.zeros((P, CWID), np.float32)
    c[:, 0:256] = f(L0_xattn_bq)
    c[:MAIN, 256:768] = bkv
    c[MAIN:, 256:768] = f(L0_xattn_bkv_dca)
    for off, qn, kn, kd in ((C_LNW, L0_xattn_qn_w, L0_xattn_kn_w, L0_xattn_kn_dca_w),
                            (C_LNB, L0_xattn_qn_b, L0_xattn_kn_b, L0_xattn_kn_dca_b)):
        c[:, off:off + XD] = f(qn)
        c[:MAIN, off + XD:off + 2 * XD] = f(kn)
        c[MAIN:, off + XD:off + 2 * XD] = f(kd)
    c[:, C_BO:C_BO + D] = f(L0_xattn_bo)
    c[:, C_LN1:C_LN1 + D] = f(L0_ffn_ln1_w)
    c[:, C_LN2:C_LN2 + D] = f(L0_ffn_ln2_w)
    c[:, C_GATE] = f(g_xattn)[0]
    c[:, C_GATE + 1] = f(g_ffn)[0]
    c[:, C_RT:C_RT + KC * NE] = f(L0_ffn_gate_w).reshape(NE, KC, P).transpose(2, 1, 0).reshape(P, KC * NE)
    c[:, C_IOTA:C_IOTA + NE] = np.arange(NE)
    c[:MAIN, C_SEG] = 1
    c[MAIN:, C_SEG + 1] = 1
    sel = np.zeros((P, NC * P), np.float16)
    rows = np.arange(NC * P)
    sel[np.minimum(rows // EI, NE), rows] = 0.5 / WS / WS
    sel[32 + np.minimum(rows // EI, NE), rows] = 0.5 / WS / WS
    mask = np.where(np.tril(np.ones((S, S), bool)), 0.0, MASKED)
    ident = np.zeros((P, 2 * P), np.float16)
    ident[:, :P] = np.eye(P)
    ident[0, P:P + MAIN] = 1
    ident[1, P + MAIN:] = 1
    arrays = {
        "in_x": f(x), "in_yT": np.ascontiguousarray(f(ctx_1024).transpose(0, 2, 1)),
        "in_wa": np.ascontiguousarray(wa), "in_wall": wall, "in_cst": c,
        "in_ident": ident, "in_identb": np.eye(P).astype(ml_dtypes.bfloat16),
        "in_maskb": mask.astype(ml_dtypes.bfloat16), "in_sel": sel,
    }
    nc = bacc.Bacc("TRN2", target_bir_lowering=False, num_devices=1)
    args = [nc.dram_tensor(n, a.shape, mybir.dt.from_np(a.dtype), kind="ExternalInput").ap()
            for n, a in arrays.items()]
    args.append(nc.dram_tensor("out_0", (NB, S, D), mybir.dt.float32, kind="ExternalOutput").ap())
    build(nc, *args)
    r = run(nc, [arrays], core_ids=[0])
    return r.results[0]["out_0"]
```
